# Optimizing a Trainium2 kernel written in Bass

```python
import numpy as np
import jax
import jax.numpy as jnp

def _softmax(x, axis=-1):
    return jax.nn.softmax(x, axis=axis)

def _gelu(x):
    return jax.nn.gelu(x, approximate=True)

def _silu(x):
    return jax.nn.silu(x)

def _sigmoid(x):
    return jax.nn.sigmoid(x)

def _layernorm(x, axis=-1, eps=1e-05):
    m = jnp.mean(x, axis=axis, keepdims=True)
    v = jnp.var(x, axis=axis, keepdims=True)
    return (x - m) / jnp.sqrt(v + eps)

def _scatter_add(tgt, idx, src, axis=0):
    return tgt.at[idx].add(src)

def _segment_sum(src, seg, n):
    return jax.ops.segment_sum(src, seg, n)
kernel_name = 'mk_adaln_d2_jaxref_r4_c106ce'

def setup_inputs(seed: int=0):
    np.random.seed(seed)
    _w = jnp.asarray

    def _L0_attn_setup():
        import math
        import jax, jax.numpy as jnp
        import numpy as np
        N_HEADS = 16

        def _phi(x, rf, m):
            norms_sq = jnp.sum(x * x, axis=-1, keepdims=True)
            proj = jnp.einsum('bhtd,md->bhtm', x, rf)
            scale = jnp.exp(-norms_sq * 0.5) / math.sqrt(m)
            return jnp.concatenate([jnp.cos(proj), jnp.sin(proj)], axis=-1) * scale
        key = jax.random.key(seed)
        ks = jax.random.split(key, 6)
        B, T, D = (2, 1024, 256)
        m, dh = (64, D // N_HEADS)
        x = jax.random.normal(ks[0], (B, T, D), dtype=jnp.float32)
        s = 1.0 / math.sqrt(D)
        wq = jax.random.normal(ks[1], (D, D), dtype=jnp.float32) * s
        wk = jax.random.normal(ks[2], (D, D), dtype=jnp.float32) * s
        wv = jax.random.normal(ks[3], (D, D), dtype=jnp.float32) * s
        wo = jax.random.normal(ks[4], (D, D), dtype=jnp.float32) * s
        rf = jax.random.normal(ks[5], (m, dh), dtype=jnp.float32) / math.sqrt(dh)
        return {'x': x, 'wq': wq, 'wk': wk, 'wv': wv, 'wo': wo, 'rf': rf}
    _L0_attn_in = _L0_attn_setup()

    def _L0_ffn_setup():
        import jax, jax.numpy as jnp
        import numpy as np
        B, S, H = (2, 512, 256)
        E_ROUTED = 8
        TOP_K = 2
        I = 512
        key = jax.random.key(seed)
        ks = jax.random.split(key, 9)
        s = 0.02
        return {'x': jax.random.normal(ks[0], (B, S, H), dtype=jnp.float32), 'shared_gate': jax.random.normal(ks[1], (I, H), dtype=jnp.float32) * s, 'shared_up': jax.random.normal(ks[2], (I, H), dtype=jnp.float32) * s, 'shared_down': jax.random.normal(ks[3], (H, I), dtype=jnp.float32) * s, 'gate_w': jax.random.normal(ks[4], (E_ROUTED, H, I), dtype=jnp.float32) * s, 'up_w': jax.random.normal(ks[5], (E_ROUTED, H, I), dtype=jnp.float32) * s, 'down_w': jax.random.normal(ks[6], (E_ROUTED, I, H), dtype=jnp.float32) * s, 'router_w': jax.random.normal(ks[7], (E_ROUTED, H), dtype=jnp.float32) * s, 'routing_bias': jnp.zeros((E_ROUTED,), dtype=jnp.float32)}
    _L0_ffn_in = _L0_ffn_setup()
    _L0_c = _w((lambda *s: np.random.randn(*s).astype(np.float32) * 0.05)(4, 256))
    _L0_wmod = _w((lambda *s: np.random.randn(*s).astype(np.float32) * 0.05)(256, 6 * 256) * 256 ** (-0.5))

    def _L1_attn_setup():
        import jax, jax.numpy as jnp
        import numpy as np
        B, L, D = (2, 2048, 256)
        key = jax.random.key(seed)
        ks = jax.random.split(key, 6)
        x = jax.random.normal(ks[0], (B, L, D), dtype=jnp.float32)
        mag = jnp.abs(jax.random.normal(ks[1], (D,), dtype=jnp.float32))
        ang = (2.0 * np.pi * jnp.arange(D) / D).astype(jnp.float32)
        phazor_real = mag * jnp.cos(ang)
        phazor_imag = mag * jnp.sin(ang)
        phazor_init_real = jax.random.normal(ks[2], (D,), dtype=jnp.float32)
        phazor_init_imag = jax.random.normal(ks[3], (D,), dtype=jnp.float32)
        last_conv_real = jax.random.normal(ks[4], (D,), dtype=jnp.float32)
        last_conv_imag = jax.random.normal(ks[5], (D,), dtype=jnp.float32)
        return {'x': x, 'phazor_real': phazor_real, 'phazor_imag': phazor_imag, 'phazor_init_real': phazor_init_real, 'phazor_init_imag': phazor_init_imag, 'last_conv_real': last_conv_real, 'last_conv_imag': last_conv_imag}
    _L1_attn_in = _L1_attn_setup()

    def _L1_ffn_setup():
        import jax, jax.numpy as jnp
        import numpy as np
        NUM_EXPERTS = 8
        TOP_K = 2
        CAP_RATIO = 1.25
        INIT_STD = 0.02
        key = jax.random.key(seed)
        k1, k2, k3, k4 = jax.random.split(key, 4)
        B, T, H, F = (4, 512, 256, 1024)
        x = jax.random.normal(k1, (B, T, H), jnp.float32)
        router_w = jax.random.normal(k2, (NUM_EXPERTS, H), jnp.float32) * INIT_STD
        w1 = jax.random.normal(k3, (NUM_EXPERTS, H, F), jnp.float32) * INIT_STD
        w2 = jax.random.normal(k4, (NUM_EXPERTS, F, H), jnp.float32) * INIT_STD
        return {'x': x, 'router_w': router_w, 'w1': w1, 'w2': w2}
    _L1_ffn_in = _L1_ffn_setup()
    _L1_c = _w((lambda *s: np.random.randn(*s).astype(np.float32) * 0.05)(4, 256))
    _L1_wmod = _w((lambda *s: np.random.randn(*s).astype(np.float32) * 0.05)(256, 6 * 256) * 256 ** (-0.5))
    _d = {'L0_attn_x': _L0_attn_in['x'], 'L0_attn_wq': _L0_attn_in['wq'], 'L0_attn_wk': _L0_attn_in['wk'], 'L0_attn_wv': _L0_attn_in['wv'], 'L0_attn_wo': _L0_attn_in['wo'], 'L0_attn_rf': _L0_attn_in['rf'], 'L0_ffn_shared_gate': _L0_ffn_in['shared_gate'], 'L0_ffn_shared_up': _L0_ffn_in['shared_up'], 'L0_ffn_shared_down': _L0_ffn_in['shared_down'], 'L0_ffn_gate_w': _L0_ffn_in['gate_w'], 'L0_ffn_up_w': _L0_ffn_in['up_w'], 'L0_ffn_down_w': _L0_ffn_in['down_w'], 'L0_ffn_router_w': _L0_ffn_in['router_w'], 'L0_ffn_routing_bias': _L0_ffn_in['routing_bias'], 'L0_c': _L0_c, 'L0_wmod': _L0_wmod, 'L1_attn_phazor_real': _L1_attn_in['phazor_real'], 'L1_attn_phazor_imag': _L1_attn_in['phazor_imag'], 'L1_attn_phazor_init_real': _L1_attn_in['phazor_init_real'], 'L1_attn_phazor_init_imag': _L1_attn_in['phazor_init_imag'], 'L1_attn_last_conv_real': _L1_attn_in['last_conv_real'], 'L1_attn_last_conv_imag': _L1_attn_in['last_conv_imag'], 'L1_ffn_router_w': _L1_ffn_in['router_w'], 'L1_ffn_w1': _L1_ffn_in['w1'], 'L1_ffn_w2': _L1_ffn_in['w2'], 'L1_c': _L1_c, 'L1_wmod': _L1_wmod}
    _x0 = _d['L0_attn_x']
    _d['L0_attn_x'] = jax.random.normal(jax.random.fold_in(jax.random.key(seed), 1), (4, 1024, 256), dtype=_x0.dtype)
    del _x0
    return _d

def reference(L0_attn_x, L0_attn_wq, L0_attn_wk, L0_attn_wv, L0_attn_wo, L0_attn_rf, L0_ffn_shared_gate, L0_ffn_shared_up, L0_ffn_shared_down, L0_ffn_gate_w, L0_ffn_up_w, L0_ffn_down_w, L0_ffn_router_w, L0_ffn_routing_bias, L0_c, L0_wmod, L1_attn_phazor_real, L1_attn_phazor_imag, L1_attn_phazor_init_real, L1_attn_phazor_init_imag, L1_attn_last_conv_real, L1_attn_last_conv_imag, L1_ffn_router_w, L1_ffn_w1, L1_ffn_w2, L1_c, L1_wmod):

    def _L0_attn_ref(x, wq, wk, wv, wo, rf):
        import math
        import jax, jax.numpy as jnp
        import numpy as np
        N_HEADS = 16

        def _phi(x, rf, m):
            norms_sq = jnp.sum(x * x, axis=-1, keepdims=True)
            proj = jnp.einsum('bhtd,md->bhtm', x, rf)
            scale = jnp.exp(-norms_sq * 0.5) / math.sqrt(m)
            return jnp.concatenate([jnp.cos(proj), jnp.sin(proj)], axis=-1) * scale
        B, T, D = x.shape
        H = N_HEADS
        Dh = D // H
        m = rf.shape[0]

        def heads(w):
            return (x @ w.T).reshape(B, T, H, Dh).transpose(0, 2, 1, 3)
        Q, K, V = (heads(wq), heads(wk), heads(wv))
        Qf = _phi(Q, rf, m)
        Kf = _phi(K, rf, m)
        KV = jnp.einsum('bhnd,bhnv->bhdv', Kf, V)
        QKV = jnp.einsum('bhnd,bhdv->bhnv', Qf, KV)
        K_sum = jnp.sum(Kf, axis=2)
        Z = jnp.maximum(jnp.einsum('bhnd,bhd->bhn', Qf, K_sum)[..., None], 1e-06)
        out = (QKV / Z).transpose(0, 2, 1, 3).reshape(B, T, D)
        return out @ wo.T

    def _L0_ffn_ref(x, shared_gate, shared_up, shared_down, gate_w, up_w, down_w, router_w, routing_bias):
        import jax, jax.numpy as jnp
        import numpy as np
        B, S, H = (2, 512, 256)
        E_ROUTED = 8
        TOP_K = 2
        I = 512
        b, s, h = x.shape
        shared = jnp.einsum('bsi,hi->bsh', jax.nn.silu(jnp.einsum('bsh,ih->bsi', x, shared_gate)) * jnp.einsum('bsh,ih->bsi', x, shared_up), shared_down)
        logits = jnp.einsum('bsh,eh->bse', x, router_w) + routing_bias
        probs = jax.nn.sigmoid(logits)
        scores, indices = jax.lax.top_k(probs, TOP_K)
        scores = scores / jnp.sum(scores, axis=-1, keepdims=True)
        t = b * s
        xf = x.reshape(t, h)
        idx = indices.reshape(t, TOP_K)
        sc = scores.reshape(t, TOP_K)
        w = jnp.zeros((t, E_ROUTED), dtype=x.dtype)
        w = w.at[jnp.arange(t)[:, None], idx].add(sc)
        g = jax.nn.silu(jnp.einsum('th,ehi->tei', xf, gate_w))
        u = jnp.einsum('th,ehi->tei', xf, up_w)
        combined = jnp.einsum('tei,eih,te->th', g * u, down_w, w)
        return shared + combined.reshape(b, s, h)

    def _L1_attn_ref(x, phazor_real, phazor_imag, phazor_init_real, phazor_init_imag, last_conv_real, last_conv_imag):
        import jax, jax.numpy as jnp
        import numpy as np
        B, L, D = (2, 2048, 256)
        b, length, dim = x.shape
        dtype = x.dtype
        ph = jnp.exp(-(phazor_real * phazor_real + phazor_imag * phazor_imag)) * jnp.exp(1j * jnp.arctan2(phazor_imag, phazor_real))
        prog = jnp.power(ph[None, :], jnp.arange(length)[:, None])
        pinit = phazor_init_real + 1j * phazor_init_imag
        filt = prog * pinit[None, :]
        filt_fft = jnp.fft.fft(filt, n=2 * length, axis=0)
        x_fft = jnp.fft.fft(x.astype(jnp.complex64), n=2 * length, axis=1)
        conv = jnp.fft.ifft(filt_fft[None, :, :] * x_fft, axis=1)[:, :length, :]
        last = (last_conv_real + 1j * last_conv_imag)[None, None, :]
        conv_with_past = conv + last * prog[None, :, :] * ph[None, None, :]
        return conv_with_past.real.astype(dtype)

    def _L1_ffn_ref(x, router_w, w1, w2):
        import jax, jax.numpy as jnp
        import numpy as np
        NUM_EXPERTS = 8
        TOP_K = 2
        CAP_RATIO = 1.25
        INIT_STD = 0.02
        B, T, H = x.shape
        E, K = (NUM_EXPERTS, TOP_K)
        xf = x.reshape(-1, H)
        N = xf.shape[0]
        P = N * K
        capacity = int(CAP_RATio * N * K / E) + 1 if False else int(CAP_RATIO * N * K / E) + 1
        logits = xf @ router_w.T
        probs = jax.nn.softmax(logits, axis=-1)
        k_probs, k_idx = jax.lax.top_k(probs, K)
        k_probs = k_probs / jnp.sum(k_probs, axis=-1, keepdims=True)
        flat_e = k_idx.reshape(-1)
        onehot = jax.nn.one_hot(flat_e, E, dtype=jnp.int32)
        rank = jnp.take_along_axis(jnp.cumsum(onehot, axis=0) - 1, flat_e[:, None], axis=1)[:, 0]
        keep = rank < capacity
        slot = jnp.minimum(rank, capacity - 1)
        token_id = jnp.arange(P) // K
        dispatched = jnp.where(keep[:, None], xf[token_id], 0.0)
        buf = jnp.zeros((E, capacity, H), x.dtype).at[flat_e, slot].add(dispatched)
        h = jax.nn.silu(jnp.einsum('ech,ehf->ecf', buf, w1))
        out_buf = jnp.einsum('ecf,efh->ech', h, w2)
        pair_out = out_buf[flat_e, slot] * keep[:, None].astype(x.dtype)
        combined = jnp.sum(pair_out.reshape(N, K, H) * k_probs[..., None], axis=1)
        return combined.reshape(B, T, H) + x
    x = L0_attn_x
    mod = (_silu(L0_c) @ L0_wmod).reshape(L0_c.shape[0], 6, 1, -1)
    sa, ca, ga, sb, cb, gb = (mod[:, 0], mod[:, 1], mod[:, 2], mod[:, 3], mod[:, 4], mod[:, 5])
    ga = (2 * (ga >= 0) - 1) * jnp.maximum(jnp.abs(ga), 0.25)
    gb = (2 * (gb >= 0) - 1) * jnp.maximum(jnp.abs(gb), 0.25)
    h = _layernorm(x, axis=-1) * (1 + ca) + sa
    x = x + ga * _L0_attn_ref(h, L0_attn_wq, L0_attn_wk, L0_attn_wv, L0_attn_wo, L0_attn_rf)
    h = _layernorm(x, axis=-1) * (1 + cb) + sb
    x = x + gb * _L0_ffn_ref(h, L0_ffn_shared_gate, L0_ffn_shared_up, L0_ffn_shared_down, L0_ffn_gate_w, L0_ffn_up_w, L0_ffn_down_w, L0_ffn_router_w, L0_ffn_routing_bias)
    mod = (_silu(L1_c) @ L1_wmod).reshape(L1_c.shape[0], 6, 1, -1)
    sa, ca, ga, sb, cb, gb = (mod[:, 0], mod[:, 1], mod[:, 2], mod[:, 3], mod[:, 4], mod[:, 5])
    ga = (2 * (ga >= 0) - 1) * jnp.maximum(jnp.abs(ga), 0.25)
    gb = (2 * (gb >= 0) - 1) * jnp.maximum(jnp.abs(gb), 0.25)
    h = _layernorm(x, axis=-1) * (1 + ca) + sa
    x = x + ga * _L1_attn_ref(h, L1_attn_phazor_real, L1_attn_phazor_imag, L1_attn_phazor_init_real, L1_attn_phazor_init_imag, L1_attn_last_conv_real, L1_attn_last_conv_imag)
    h = _layernorm(x, axis=-1) * (1 + cb) + sb
    x = x + gb * _L1_ffn_ref(h, L1_ffn_router_w, L1_ffn_w1, L1_ffn_w2)
    return x

_drawn_inputs = setup_inputs


def setup_inputs(seed=0):
    import zlib

    import numpy as np

    out = dict(_drawn_inputs(seed))
    spreads = {'L0_ffn_routing_bias': (0.0, 0.8)}
    factors = {'L0_attn_wq': 8.0,
     'L0_attn_wk': 2.733,
     'L0_attn_wv': 2.737,
     'L0_attn_wo': 2.788,
     'L0_attn_rf': 8.0,
     'L0_ffn_shared_gate': 8.0,
     'L0_ffn_shared_up': 8.0,
     'L0_ffn_shared_down': 8.0,
     'L0_ffn_gate_w': 8.0,
     'L0_ffn_up_w': 8.0,
     'L0_ffn_down_w': 8.0,
     'L0_ffn_router_w': 8.0,
     'L0_c': 2.766,
     'L1_attn_last_conv_imag': 10.643,
     'L1_ffn_router_w': 5.384,
     'L1_ffn_w1': 4.672,
     'L1_ffn_w2': 4.644,
     'L1_attn_last_conv_real': 6.481}
    for name, (base, spread) in spreads.items():
        noise = np.random.default_rng([zlib.crc32(name.encode()), seed]).standard_normal(out[name].shape)
        drawn = base * np.exp(spread * noise) if base else spread * noise
        out[name] = jnp.asarray(drawn.astype(out[name].dtype))
    for name, factor in factors.items():
        out[name] = (out[name] * factor).astype(out[name].dtype)
    return out
```

```python
import math
from contextlib import ExitStack

import numpy as np

import concourse.bass as bass
from concourse import mybir

F32 = mybir.dt.float32
I32 = mybir.dt.int32
U32 = mybir.dt.uint32
ACT = mybir.ActivationFunctionType
ALU = mybir.AluOpType
AXX = mybir.AxisListType.X

P = 128
BATCH, SEQ, D = 4, 1024, 256
TOK = BATCH * SEQ
NT = TOK // P
TPB = SEQ // P
KD = D // P
G = 512
TPG = G // P
NG = TOK // G
HEADS, DH, FEAT = 16, 16, 64
HPK = P // DH
PAIRS = HEADS // 2
VA = DH + 2
EPS = 1e-5
ROUND = 1.5 * 2.0 ** 23
E = 8
FF0, FF1 = 512, 1024
BLK0 = 512
NB0 = (2 * TOK + E * (BLK0 - 1)) // BLK0
CAP = int(1.25 * TOK * 2 / E) + 1
BLK1, RT1 = 432, 108
NB1 = -(-CAP // BLK1)
SLOTS1 = NB1 * BLK1
DROP = 1 << 20
SHIFT_A, SCALE_A, GATE_A, SHIFT_B, SCALE_B, GATE_B = range(6)


def counter():
    n = 0

    def more(k=1):
        nonlocal n
        n += k
        return n
    return more


def one(ap):
    return ap.rearrange("p o n -> p (o n)")


def row(ap, i):
    return one(ap[:, bass.ds(i, 1), :])


def build_program(nc, A, out, stop=99):
    ctx = ExitStack()
    with ctx:
        def sb(name, shape, dt=F32, stack=ctx):
            return stack.enter_context(nc.sbuf_tensor(name, shape, dt))

        def sem(name):
            return ctx.enter_context(nc.semaphore(name))

        S = {}
        x = sb("x", [P, NT, D])
        ident = sb("ident", [P, P])
        before = sb("before", [P, P])
        ones = sb("ones", [P, P])
        half_pi = sb("half_pi", [P, 1])
        zero = sb("zero", [P, 1024])
        modb = sb("modb", [P, BATCH, 6, D])
        stats = sb("stats", [P, NT, 6])
        mean = sb("mean", [P, NT])
        rstd = sb("rstd", [P, NT])
        ntmp = sb("ntmp", [P, 3, NT])
        seed = sb("seed", [P, NT], I32)
        mod_rows = [nc.dram_tensor(f"mod_rows{l}", (BATCH, 6 * D), F32) for l in range(2)]
        slots0 = nc.dram_tensor("slots0", (NB0 * BLK0, D), F32)
        slots1 = nc.dram_tensor("slots1", (E * SLOTS1, D), F32)
        y0 = nc.dram_tensor("y0", (NB0 * BLK0, D), F32)
        y1 = nc.dram_tensor("y1", (E * SLOTS1, D), F32)
        zeroed = sem("zeroed")
        mod_loaded = sem("mod_loaded")
        env = dict(locals())
        setup(nc, A, env)
        layer_stats(nc, env, 0)
        if stop >= 1:
            attention(nc, A, env)
        if stop >= 2:
            layer_stats(nc, env, 1)
            experts_of(nc, A, env, 0)
        if stop >= 3:
            layer_stats(nc, env, 2)
            recurrence(nc, A, env)
        if stop >= 4:
            layer_stats(nc, env, 3)
            experts_of(nc, A, env, 1)
        store_x(nc, env, out)


def experts_of(nc, A, env, layer):
    with ExitStack() as st:
        sb = lambda n, s, dt=F32: st.enter_context(nc.sbuf_tensor(f"{n}{layer}", s, dt))
        own = dict(env)
        own["weight"] = sb("weight", [P, 2, NT])
        own["put"] = sb("put", [P, 2, NT], U32)
        own["get"] = sb("get", [P, 2, NT], U32)
        own["experts"] = sb("experts", [1, NB0 + 1], I32)
        with ExitStack() as st2:
            own["hall"] = st2.enter_context(nc.sbuf_tensor(f"hall{layer}", [P, NT, D], F32))
            own["logits"] = st2.enter_context(nc.sbuf_tensor(f"logits{layer}", [P, NT, E], F32))
            dense_and_router(nc, A, own, layer)
            routing(nc, A, own, layer)
        expert_blocks(nc, A, own, layer)
        combine(nc, A, own, layer)


def setup(nc, A, env):
    with ExitStack() as st:
        sb = lambda n, s, dt=F32: st.enter_context(nc.sbuf_tensor(n, s, dt))
        sem = lambda n: st.enter_context(nc.semaphore(n))
        x, ident, before, ones, half_pi = (env[k] for k in ("x", "ident", "before", "ones", "half_pi"))
        ct = sb("ct", [P, 2, KD, BATCH])
        wmod = sb("wmod", [P, 2, KD, 6 * D])
        mods = sb("mods", [BATCH, 2, 6, D])
        sgn = sb("sgn", [BATCH, 2, D])
        zero = env["zero"]
        ps = st.enter_context(nc.psum_tensor("mod_ps", [BATCH, 2, 3, 512], F32))
        loaded, silu_done, mod_ps_ready, copied = sem("loaded"), sem("silu_done"), sem("mod_ps_ready"), sem("copied")
        mod_step, mods_ready, rows_stored, const_step, zero_ready, x_loaded = (
            sem("mod_step"), sem("mods_ready"), sem("rows_stored"), sem("const_step"), sem("zero_ready"), sem("x_loaded"))
        block = st.enter_context(nc.Block())

        @block.sync
        def _(sp):
            for l in range(2):
                sp.dma_start(ct[:, l], A[f"ct{l}"].rearrange("(k p) b -> p k b", p=P)).then_inc(loaded, 16)
                sp.dma_start(wmod[:, l], A[f"L{l}_wmod"].rearrange("(k p) n -> p k n", p=P)).then_inc(loaded, 16)
            xin = A["L0_attn_x"].rearrange("b (t p) d -> p (b t) d", p=P)
            for q in range(4):
                sp.dma_start(x[:, 8 * q:8 * q + 8, :], xin[:, 8 * q:8 * q + 8, :]).then_inc(x_loaded, 16)
            sp.wait_ge(mods_ready, 1)
            for l in range(2):
                sp.dma_start(env["mod_rows"][l].ap(), mods[:, l].rearrange("b s d -> b (s d)")).then_inc(rows_stored, 16)
            sp.wait_ge(rows_stored, 32)
            sp.dma_start(env["modb"][:].rearrange("p b s d -> p (b s d)"),
                         env["mod_rows"][0].ap().rearrange("(o b) n -> o (b n)", o=1).to_broadcast([P, BATCH * 6 * D])
                         ).then_inc(env["mod_loaded"], 16)
            sp.wait_ge(x_loaded, 64)
            sp.wait_ge(env["mod_loaded"], 16)

        @block.gpsimd
        def _(pool):
            pool.memset(ident[:, :], 0.0).then_inc(const_step, 1)
            pool.memset(ones[:, :], 1.0).then_inc(const_step, 1)
            pool.wait_ge(const_step, 2)
            pool.affine_select(out=ident[:, :], in_=ident[:, :], compare_op=ALU.not_equal, fill=1.0,
                               base=0, pattern=[[-1, P]], channel_multiplier=1).then_inc(const_step, 1)
            pool.affine_select(out=before[:, :], in_=ones[:, :], compare_op=ALU.is_gt, fill=0.0,
                               base=0, pattern=[[1, P]], channel_multiplier=-1).then_inc(const_step, 1)
            pool.memset(half_pi[:, :], math.pi / 2).then_inc(const_step, 1)
            pool.wait_ge(const_step, 5)

        @block.scalar
        def _(act):
            act.wait_ge(zero_ready, 1)
            env["zero_dmas"] = 0
            for name, rows in (("slots0", NB0 * BLK0), ("slots1", E * SLOTS1)):
                per = rows * D // P
                flat = env[name].ap().rearrange("(p n) d -> p (n d)", p=P)
                for at in range(0, per, 1024):
                    n = min(1024, per - at)
                    act.dma_start(flat[:, at:at + n], zero[:, 0:n]).then_inc(env["zeroed"], 16)
                    env["zero_dmas"] += 1
            act.wait_ge(loaded, 64)
            act.activation(ct[:], ct[:], ACT.Silu).then_inc(silu_done, 1)

        @block.tensor
        def _(pe):
            pe.wait_ge(silu_done, 1)
            for l in range(2):
                for n in range(3):
                    if l == 1:
                        pe.wait_ge(copied, n + 1)
                    for k in range(KD):
                        mm = pe.matmul(ps[:, 0, n], ct[:, l, k, :], wmod[:, l, k, 512 * n:512 * n + 512],
                                       start=k == 0, stop=k == KD - 1)
                    mm.then_inc(mod_ps_ready, 1)

        @block.vector
        def _(dve):
            dve.memset(zero[:, :], 0.0).then_inc(zero_ready, 1)
            for l in range(2):
                for n in range(3):
                    dve.wait_ge(mod_ps_ready, 3 * l + n + 1)
                    dve.tensor_copy(mods[:, l, 2 * n:2 * n + 2, :],
                                    ps[:, 0, n].rearrange("b (s d) -> b s d", s=2)).then_inc(copied, 1)
            dve.wait_ge(copied, 6)
            n = counter()
            for l in range(2):
                for scale in (SCALE_A, SCALE_B):
                    dve.tensor_scalar(mods[:, l, scale], mods[:, l, scale], 1.0, None, ALU.add).then_inc(mod_step, 1)
                    n()
                for gate in (GATE_A, GATE_B):
                    g = mods[:, l, gate]
                    dve.tensor_scalar(sgn[:, 0], g, 0.0, 2.0, ALU.is_ge, ALU.mult).then_inc(mod_step, 1)
                    dve.wait_ge(mod_step, n())
                    dve.scalar_tensor_tensor(out=sgn[:, 1], in0=sgn[:, 0], scalar=-1.0, in1=g,
                                             op0=ALU.add, op1=ALU.mult).then_inc(mod_step, 1)
                    dve.wait_ge(mod_step, n())
                    dve.tensor_scalar(sgn[:, 1], sgn[:, 1], 0.25, None, ALU.max).then_inc(mod_step, 1)
                    dve.wait_ge(mod_step, n())
                    dve.scalar_tensor_tensor(out=g, in0=sgn[:, 0], scalar=-1.0, in1=sgn[:, 1],
                                             op0=ALU.add, op1=ALU.mult).then_inc(mod_step, 1)
                    dve.wait_ge(mod_step, n())
            dve.tensor_copy(sgn[:, 0, 0:1], mods[:, 0, 0, 0:1]).then_inc(mods_ready, 1)


def layer_stats(nc, env, at):
    with ExitStack() as st:
        sem = lambda n: st.enter_context(nc.semaphore(f"{n}_{at}"))
        x, stats, mean, rstd, ntmp, seed = (env[k] for k in ("x", "stats", "mean", "rstd", "ntmp", "seed"))
        stats_done, rstd_step = sem("stats_done"), sem("rstd_step")
        block = st.enter_context(nc.Block())

        @block.vector
        def _(dve):
            with dve.Fori(0, NT) as t:
                dve.bn_stats(row(stats, t), row(x, t)).then_inc(stats_done, 1)
            dve.wait_ge(stats_done, NT)
            var, half, y, y2 = ntmp[:, 0], ntmp[:, 1], rstd[:, :], ntmp[:, 2]
            mean_e, m2_e, mean_o, m2_o = (stats[:, :, i] for i in (1, 2, 4, 5))
            n = counter()
            dve.tensor_tensor(half, mean_e, mean_o, ALU.subtract).then_inc(rstd_step, 1)
            dve.tensor_tensor(var, m2_e, m2_o, ALU.add).then_inc(rstd_step, 1)
            dve.tensor_tensor(y2, mean_e, mean_o, ALU.add).then_inc(rstd_step, 1)
            dve.wait_ge(rstd_step, n(3))
            dve.tensor_tensor(half, half, half, ALU.mult).then_inc(rstd_step, 1)
            dve.tensor_scalar(mean[:, :], y2, 0.5, None, ALU.mult).then_inc(rstd_step, 1)
            dve.tensor_scalar(var, var, 1.0 / D, EPS, ALU.mult, ALU.add).then_inc(rstd_step, 1)
            dve.wait_ge(rstd_step, n(3))
            dve.scalar_tensor_tensor(out=var, in0=half, scalar=0.25, in1=var, op0=ALU.mult, op1=ALU.add
                                     ).then_inc(rstd_step, 1)
            dve.wait_ge(rstd_step, n())
            inverse_sqrt(dve, var, half, y, y2, seed[:, :], rstd_step, n)


def inverse_sqrt(dve, v, half, y, y2, seed, step, n):
    dve.tensor_scalar(seed, v.bitcast(I32), 1, None, ALU.logical_shift_right).then_inc(step, 1)
    dve.tensor_scalar(half, v, -0.5, None, ALU.mult).then_inc(step, 1)
    dve.wait_ge(step, n(2))
    dve.tensor_scalar(y.bitcast(I32), seed, -1.0, float(0x5F3759DF), ALU.mult, ALU.add).then_inc(step, 1)
    dve.wait_ge(step, n())
    for _ in range(4):
        dve.tensor_tensor(y2, y, y, ALU.mult).then_inc(step, 1)
        dve.wait_ge(step, n())
        dve.tensor_tensor(y2, y2, half, ALU.mult).then_inc(step, 1)
        dve.wait_ge(step, n())
        dve.scalar_tensor_tensor(out=y, in0=y2, scalar=1.5, in1=y, op0=ALU.add, op1=ALU.mult).then_inc(step, 1)
        dve.wait_ge(step, n())


def modulate(dve, env, T, dst, xs, batch, shift, scale, step, value):
    x, mean, rstd, modb = env["x"], env["mean"], env["rstd"], env["modb"]

    def mod(i):
        return modb[:, bass.ds(batch, 1), i, :].rearrange("p o n -> p (o n)")
    dve.scalar_tensor_tensor(out=xs, in0=row(x, T), scalar=mean[:, bass.ds(T, 1)], in1=mod(scale),
                             op0=ALU.subtract, op1=ALU.mult).then_inc(step, 1)
    dve.wait_ge(step, value)
    return dve.scalar_tensor_tensor(out=dst, in0=xs, scalar=rstd[:, bass.ds(T, 1)], in1=mod(shift),
                                    op0=ALU.mult, op1=ALU.add)


def attention(nc, A, env):
    with ExitStack() as st:
        sb = lambda n, s, dt=F32: st.enter_context(nc.sbuf_tensor("at_" + n, s, dt))
        sem = lambda n: st.enter_context(nc.semaphore("at_" + n))
        bank = lambda n: st.enter_context(nc.psum_tensor("at_" + n, [P, 512], F32))
        x, ident, modb, half_pi = (env[k] for k in ("x", "ident", "modb", "half_pi"))
        w = {k: sb(k, [P, KD, D]) for k in ("wqT", "wkT", "wvT", "woT")}
        rf = sb("rf", [P, HPK * FEAT])
        headsel = sb("headsel", [P, HPK])
        xs = sb("xs", [P, 2, D])
        h = sb("h", [P, 2, D])
        hT = sb("hT", [P, KD, SEQ])
        qkT = sb("qkT", [P, 2, KD, SEQ])
        sq = sb("sq", [P, 2, KD, SEQ])
        ex = sb("ex", [P, TPB, 2, HEADS])
        sc = sb("sc", [P, TPB, 2, HEADS])
        va = sb("va", [P, TPB, HEADS, VA])
        turn = sb("turn", [P, 2, 512])
        frac = sb("frac", [P, 2, 512])
        fabs = sb("fabs", [P, 2, 512])
        kf = sb("kf", [P, 2, 2, HEADS * FEAT])
        kv = sb("kv", [P, PAIRS, 2, 2 * VA])
        qf = sb("qf", [P, PAIRS, 2, G])
        o = sb("o", [P, 2, D])
        oT = sb("oT", [P, 2, KD, P])
        z = sb("z", [P, 4, HEADS])
        att = sb("att", [P, 2, D])
        mm = [bank(f"mm{i}") for i in range(2)]
        dd = [bank(f"dd{i}") for i in range(2)]
        up = [bank(f"u{i}") for i in range(2)]
        kvp = [bank(f"kv{i}") for i in range(2)]
        w_loaded, rf_zero, rf_ready, const_step = sem("w_loaded"), sem("rf_zero"), sem("rf_ready"), sem("const_step")
        h_ready, h_used, xs_ready = sem("h_ready"), sem("h_used"), sem("xs_ready")
        mm_ready, mm_done, dd_ready, dd_done = sem("mm_ready"), sem("mm_done"), sem("dd_ready"), sem("dd_done")
        u_ready, u_used, turn_ready, frac_ready, fabs_ready, feat_ready, kf_used = (
            sem("u_ready"), sem("u_used"), sem("turn_ready"), sem("frac_ready"), sem("fabs_ready"),
            sem("feat_ready"), sem("kf_used"))
        norms_ready, ex_ready, sc_ready, va_ready, kvp_ready, kv_ready, z_step, x_done = (
            sem("norms_ready"), sem("ex_ready"), sem("sc_ready"), sem("va_ready"), sem("kvp_ready"),
            sem("kv_ready"), sem("z_step"), sem("x_done"))
        block = st.enter_context(nc.Block())
        NGB = SEQ // G
        MM_HT, MM_QK = KD * NGB, 2 * KD * NGB
        MM_BATCH = MM_HT + MM_QK + TPB
        DD_V = TPB // 2
        DD_BATCH = DD_V + 2 * TPB
        U_K = 2 * TPB
        U_BATCH = U_K + PAIRS * NGB
        Z_TILE = 4

        @block.sync
        def _(sp):
            for k in w:
                sp.dma_start(w[k][:], A[k].rearrange("(k p) n -> p k n", p=P)).then_inc(w_loaded, 16)
            sp.wait_ge(rf_zero, 1)
            for i in range(HPK):
                sp.dma_start(rf[i * DH:(i + 1) * DH, i * FEAT:(i + 1) * FEAT], A["rfT"]).then_inc(w_loaded, 16)

        @block.gpsimd
        def _(pool):
            pool.memset(rf[:, :], 0.0).then_inc(rf_zero, 1)
            pool.memset(headsel[:, :], 1.0).then_inc(const_step, 1)
            pool.memset(kv[:], 0.0).then_inc(const_step, 1)
            pool.memset(va[:], 0.0).then_inc(const_step, 1)
            pool.wait_ge(const_step, 3)
            pool.affine_select(out=headsel[:, :], in_=headsel[:, :], compare_op=ALU.is_ge, fill=0.0, base=0,
                               pattern=[[-DH, HPK]], channel_multiplier=1).then_inc(const_step, 1)
            pool.wait_ge(const_step, 4)
            pool.affine_select(out=headsel[:, :], in_=headsel[:, :], compare_op=ALU.is_ge, fill=0.0, base=DH - 1,
                               pattern=[[DH, HPK]], channel_multiplier=-1).then_inc(const_step, 1)
            pool.sem_inc(x_done, 2)
            with pool.Fori(0, BATCH) as b:
                for t in range(TPB):
                    pool.wait_ge(dd_done, b * DD_BATCH + DD_V + 2 * t + 2 + 2)
                    T = b * TPB + t
                    pool.tensor_tensor(row(x, T), row(x, T), att[:, t % 2], ALU.add).then_inc(x_done, 1)

        @block.tensor
        def _(pe):
            pe.sem_inc(h_used, 2)
            pe.sem_inc(kf_used, 2)
            pe.wait_ge(rf_ready, 1)
            pe.wait_ge(w_loaded, 16 * (4 + HPK))
            pe.wait_ge(const_step, 5)
            with pe.Fori(0, BATCH) as b:
                mf, df = counter(), counter()

                def mm_bank():
                    i = mf()
                    pe.wait_ge(mm_done, b * MM_BATCH + i)
                    return mm[(i - 1) % 2]

                def dd_bank():
                    i = df()
                    pe.wait_ge(dd_done, b * DD_BATCH + i)
                    return dd[(i - 1) % 2]

                for g in range(NGB):
                    banks = [mm_bank(), mm_bank()]
                    for t in range(TPG):
                        pe.wait_ge(h_ready, b * TPB + g * TPG + t + 1)
                        for j in range(KD):
                            i = pe.transpose(banks[j][:, t * P:(t + 1) * P], h[:, t % 2, j * P:(j + 1) * P], ident[:, :])
                        i.then_inc(h_used, 1)
                pe.wait_ge(mm_done, b * MM_BATCH + MM_HT + 2)
                for m, name in enumerate(("wqT", "wkT")):
                    for j in range(KD):
                        for g in range(NGB):
                            bk = mm_bank()
                            for k in range(KD):
                                i = pe.matmul(bk[:, :], w[name][:, k, j * P:(j + 1) * P], hT[:, k, g * G:(g + 1) * G],
                                              start=k == 0, stop=k == KD - 1)
                            i.then_inc(mm_ready, 1)
                pe.wait_ge(mm_done, b * MM_BATCH + MM_HT + MM_QK + 2)
                for t in range(TPB):
                    for m in range(2):
                        for j in range(KD):
                            c = ((t * 2 + m) * KD + j) * HPK
                            i = pe.matmul(kvp[0][:, c:c + HPK], sq[:, m, j, t * P:(t + 1) * P], headsel[:, :],
                                          start=True, stop=True)
                i.then_inc(norms_ready, 1)
                for t2 in range(DD_V):
                    bk = dd_bank()
                    for t in (2 * t2, 2 * t2 + 1):
                        for k in range(KD):
                            i = pe.matmul(bk[:, (t % 2) * D:(t % 2 + 1) * D], hT[:, k, t * P:(t + 1) * P],
                                          w["wvT"][:, k, :], start=k == 0, stop=k == KD - 1)
                    i.then_inc(dd_ready, 1)

                def k_project(t):
                    for j in range(KD):
                        pe.wait_ge(u_used, b * U_BATCH + 2 * t + j + 1)
                        pe.matmul(up[j][:, :], qkT[:, 1, j, t * P:(t + 1) * P], rf[:, :],
                                  start=True, stop=True).then_inc(u_ready, 1)
                k_project(0)
                for t in range(TPB):
                    if t + 1 < TPB:
                        k_project(t + 1)
                    if t == 0:
                        pe.wait_ge(dd_done, b * DD_BATCH + DD_V + 2)
                        pe.wait_ge(ex_ready, b + 1)
                    pe.wait_ge(feat_ready, b * U_BATCH + 2 * t + 2 + 2)
                    for cs in range(2):
                        for p in range(PAIRS):
                            i = pe.matmul(kvp[cs][:, 2 * VA * p:2 * VA * (p + 1)], kf[:, t % 2, cs, p * P:(p + 1) * P],
                                          va[:, t, 2 * p:2 * p + 2, :].rearrange("p h v -> p (h v)"),
                                          start=t == 0 and p == 0, stop=t == TPB - 1, skip_group_check=True)
                    i.then_inc(kf_used, 1)
                for g in range(NGB):
                    for p in range(PAIRS):
                        pe.wait_ge(u_used, b * U_BATCH + U_K + g * PAIRS + p + 1)
                        j, c = p // (PAIRS // KD), p % (PAIRS // KD)
                        pe.matmul(up[p % 2][:, :], rf[:, c * P:(c + 1) * P], qkT[:, 0, j, g * G:(g + 1) * G],
                                  start=True, stop=True).then_inc(u_ready, 1)
                    pe.wait_ge(kv_ready, (b + 1) * 4)
                    pe.wait_ge(feat_ready, b * U_BATCH + U_K + (g + 1) * PAIRS + 2)
                    for t in range(TPG):
                        bk = dd_bank()
                        for p in range(PAIRS):
                            for cs in range(2):
                                i = pe.matmul(bk[:, 2 * VA * p:2 * VA * (p + 1)],
                                              qf[:, p, cs, t * P:(t + 1) * P], kv[:, p, cs, :],
                                              start=cs == 0, stop=cs == 1)
                        i.then_inc(dd_ready, 1)
                        n = df(0)
                        bk = mm_bank()
                        pe.wait_ge(dd_done, b * DD_BATCH + n + 2)
                        for j in range(KD):
                            i = pe.transpose(bk[:, j * P:(j + 1) * P], o[:, t % 2, j * P:(j + 1) * P], ident[:, :])
                        i.then_inc(mm_ready, 1)
                        n = mf(0)
                        bk = dd_bank()
                        pe.wait_ge(mm_done, b * MM_BATCH + n + 2)
                        for k in range(KD):
                            i = pe.matmul(bk[:, 0:D], oT[:, t % 2, k, :], w["woT"][:, k, :],
                                          start=k == 0, stop=k == KD - 1)
                        i.then_inc(dd_ready, 1)

        @block.scalar
        def _(act):
            act.wait_ge(w_loaded, 16 * (4 + HPK))
            act.activation(rf[:, :], rf[:, :], ACT.Copy, scale=1.0 / (2 * math.pi)).then_inc(rf_ready, 1)
            act.sem_inc(mm_done, 2)
            act.sem_inc(feat_ready, 2)
            with act.Fori(0, BATCH) as b:
                for g in range(NGB):
                    act.wait_ge(h_used, b * TPB + (g + 1) * TPG + 2)
                    for j in range(KD):
                        act.activation(hT[:, j, g * G:(g + 1) * G], mm[j][:, :], ACT.Copy).then_inc(mm_done, 1)
                for m in range(2):
                    for j in range(KD):
                        for g in range(NGB):
                            n = 4 * m + 2 * j + g
                            act.wait_ge(mm_ready, b * (MM_QK + TPB) + n + 1)
                            act.activation(qkT[:, m, j, g * G:(g + 1) * G], mm[n % 2][:, :], ACT.Copy)
                            act.activation(sq[:, m, j, g * G:(g + 1) * G], mm[n % 2][:, :], ACT.Square).then_inc(mm_done, 1)
                act.wait_ge(norms_ready, b + 1)
                act.activation(ex[:].rearrange("p t m h -> p (t m h)"), kvp[0][:, 0:TPB * 2 * HEADS], ACT.Exp,
                               scale=-0.5).then_inc(ex_ready, 1)

                def features(u, cos, sin):
                    n = b * U_BATCH + u
                    i = u % 2
                    act.wait_ge(frac_ready, n + 1)
                    act.activation(fabs[:, i], frac[:, i], ACT.Abs).then_inc(fabs_ready, 1)
                    act.activation(sin, frac[:, i], ACT.Sin, scale=2 * math.pi)
                    act.wait_ge(fabs_ready, n + 1)
                    act.activation(cos, fabs[:, i], ACT.Sin, scale=-2 * math.pi,
                                   bias=half_pi[:, 0:1]).then_inc(feat_ready, 1)
                for t in range(TPB):
                    act.wait_ge(kf_used, b * TPB + t + 1)
                    for j in range(KD):
                        features(2 * t + j, *(kf[:, t % 2, cs, j * 512:(j + 1) * 512] for cs in range(2)))
                for g in range(NGB):
                    for p in range(PAIRS):
                        features(U_K + g * PAIRS + p, *(qf[:, p, cs, :] for cs in range(2)))
                    for t in range(TPG):
                        n = MM_QK + g * TPG + t
                        act.wait_ge(mm_ready, b * (MM_QK + TPB) + n + 1)
                        act.activation(oT[:, t % 2].rearrange("p k n -> p (k n)"), mm[n % 2][:, 0:D],
                                       ACT.Copy).then_inc(mm_done, 1)

        @block.vector
        def _(dve):
            dve.sem_inc(dd_done, 2)
            dve.sem_inc(u_used, 2)
            dve.wait_ge(const_step, 5)
            with dve.Fori(0, BATCH) as b:
                for t in range(TPB):
                    T = b * TPB + t
                    dve.wait_ge(h_used, T + 1)
                    modulate(dve, env, T, h[:, t % 2], xs[:, t % 2], b, SHIFT_A, SCALE_A, xs_ready, T + 1
                             ).then_inc(h_ready, 1)
                dve.wait_ge(ex_ready, b + 1)
                dve.tensor_scalar(sc[:], ex[:], 1.0 / math.sqrt(FEAT), None, ALU.mult).then_inc(sc_ready, 1)
                dve.wait_ge(sc_ready, b + 1)
                dve.tensor_copy(va[:, :, :, DH], sc[:, :, 1, :]).then_inc(va_ready, 1)
                for t2 in range(DD_V):
                    dve.wait_ge(dd_ready, b * DD_BATCH + t2 + 1)
                    for t in (2 * t2, 2 * t2 + 1):
                        i = dve.tensor_tensor(va[:, t, :, 0:DH],
                                              dd[t2 % 2][:, (t % 2) * D:(t % 2 + 1) * D].rearrange("p (h v) -> p h v", v=DH),
                                              sc[:, t, 1, :].unsqueeze(2).to_broadcast([P, HEADS, DH]), ALU.mult)
                    i.then_inc(dd_done, 1)

                def reduce_turns(us):
                    last = None
                    for u in [*us, None]:
                        if u is not None:
                            n = b * U_BATCH + u
                            dve.wait_ge(u_ready, n + 1)
                            dve.tensor_scalar(turn[:, u % 2], up[u % 2][:, :], ROUND, ROUND, ALU.add, ALU.subtract
                                              ).then_inc(turn_ready, 1)
                        if last is not None:
                            n = b * U_BATCH + last
                            dve.wait_ge(turn_ready, n + 1)
                            dve.wait_ge(feat_ready, n + 1)
                            dve.tensor_tensor(frac[:, last % 2], up[last % 2][:, :], turn[:, last % 2], ALU.subtract
                                              ).then_inc(frac_ready, 1)
                            dve.wait_ge(frac_ready, n + 1)
                            dve.sem_inc(u_used, 1)
                        last = u
                reduce_turns(range(U_K))
                dve.wait_ge(kf_used, (b + 1) * TPB + 2)
                for cs in range(2):
                    for hh in range(2):
                        q = slice(hh * FEAT, (hh + 1) * FEAT)
                        dve.tensor_copy(kv[q, :, cs, hh * VA:(hh + 1) * VA],
                                        kvp[cs][q, 0:PAIRS * 2 * VA].rearrange("p (a v) -> p a v", v=2 * VA)
                                        [:, :, hh * VA:(hh + 1) * VA]).then_inc(kv_ready, 1)
                for g in range(NGB):
                    reduce_turns(range(U_K + g * PAIRS, U_K + (g + 1) * PAIRS))
                    for t in range(TPG):
                        tb = g * TPG + t
                        T = b * TPB + tb
                        f = DD_V + 2 * tb
                        dve.wait_ge(dd_ready, b * DD_BATCH + f + 1)
                        raw = dd[f % 2][:, 0:HEADS * VA].rearrange("p (h v) -> p h v", v=VA)
                        dve.tensor_tensor(z[:, 0], raw[:, :, DH], sc[:, tb, 0, :], ALU.mult).then_inc(z_step, 1)
                        dve.wait_ge(z_step, T * Z_TILE + 1)
                        dve.tensor_scalar(z[:, 1], z[:, 0], 1e-6, None, ALU.max).then_inc(z_step, 1)
                        dve.wait_ge(z_step, T * Z_TILE + 2)
                        dve.reciprocal(z[:, 2], z[:, 1]).then_inc(z_step, 1)
                        dve.wait_ge(z_step, T * Z_TILE + 3)
                        dve.tensor_tensor(z[:, 3], z[:, 2], sc[:, tb, 0, :], ALU.mult).then_inc(z_step, 1)
                        dve.wait_ge(z_step, T * Z_TILE + 4)
                        dve.tensor_tensor(o[:, t % 2].rearrange("p (h v) -> p h v", v=DH), raw[:, :, 0:DH],
                                          z[:, 3].unsqueeze(2).to_broadcast([P, HEADS, DH]), ALU.mult
                                          ).then_inc(dd_done, 1)
                        dve.wait_ge(dd_ready, b * DD_BATCH + f + 2)
                        dve.wait_ge(x_done, T + 1)
                        dve.tensor_tensor(att[:, t % 2], dd[(f + 1) % 2][:, 0:D],
                                          modb[:, bass.ds(b, 1), GATE_A, :].rearrange("p o n -> p (o n)"), ALU.mult
                                          ).then_inc(dd_done, 1)


def recurrence(nc, A, env):
    with ExitStack() as st:
        sb = lambda n, s, dt=F32: st.enter_context(nc.sbuf_tensor("rc_" + n, s, dt))
        sem = lambda n: st.enter_context(nc.semaphore("rc_" + n))
        bank = lambda n: st.enter_context(nc.psum_tensor("rc_" + n, [P, 512], F32))
        x, ident, modb = (env[k] for k in ("x", "ident", "modb"))
        par = sb("par", [P, 6, KD])
        rho = sb("rho", [P, KD])
        first = sb("first", [P, 2, KD])
        rot = sb("rot", [P, 2, KD, SEQ])
        coef = sb("coef", [P, 2, KD, SEQ])
        tmp = sb("tmp", [P, 10, KD])
        tmp_i = sb("tmp_i", [P, KD], I32)
        scratch = sb("scratch", [P, 2, SEQ])
        par_loaded, tab = sem("par_loaded"), sem("tab")

        with nc.Block() as block:
            @block.sync
            def _(sp):
                sp.dma_start(par[:], A["phasor"]).then_inc(par_loaded, 16)
                sp.dma_start(modb[:].rearrange("p b s d -> p (b s d)"),
                             env["mod_rows"][1].ap().rearrange("(o b) n -> o (b n)", o=1).to_broadcast([P, BATCH * 6 * D])
                             ).then_inc(env["mod_loaded"], 16)
                sp.wait_ge(env["mod_loaded"], 32)

            @block.vector
            def _(dve):
                n = counter()
                a, b, init_re, init_im, last_re, last_im = (par[:, i] for i in range(6))
                t = [tmp[:, i] for i in range(10)]
                dve.wait_ge(par_loaded, 16)

                def ts(out, in0, s1, s2, op0, op1=None):
                    dve.tensor_scalar(out, in0, s1, s2, op0, *([op1] if op1 is not None else [])).then_inc(tab, 1)
                    dve.wait_ge(tab, n())

                def tt(out, in0, in1, op):
                    dve.tensor_tensor(out, in0, in1, op).then_inc(tab, 1)
                    dve.wait_ge(tab, n())

                def stt(out, in0, s, in1, op0, op1):
                    dve.scalar_tensor_tensor(out=out, in0=in0, scalar=s, in1=in1, op0=op0, op1=op1).then_inc(tab, 1)
                    dve.wait_ge(tab, n())

                tt(t[0], a, a, ALU.mult)
                tt(t[1], b, b, ALU.mult)
                tt(t[0], t[0], t[1], ALU.add)
                ts(t[1], t[0], 87.3, None, ALU.is_le)
                ts(t[0], t[0], 87.3, None, ALU.min)
                ts(t[2], t[0], math.log2(math.e), ROUND, ALU.mult, ALU.add)
                ts(t[2], t[2], ROUND, None, ALU.subtract)
                ln2_hi = 0.693359375
                stt(t[0], t[2], -ln2_hi, t[0], ALU.mult, ALU.add)
                stt(t[0], t[2], -(math.log(2) - ln2_hi), t[0], ALU.mult, ALU.add)
                ts(t[0], t[0], -1.0, None, ALU.mult)
                ts(t[3], t[0], 1.0 / 8, 1.0, ALU.mult, ALU.add)
                for k in range(7, 0, -1):
                    stt(t[3], t[3], 1.0 / k, t[0], ALU.mult, ALU.mult)
                    ts(t[3], t[3], 1.0, None, ALU.add)
                ts(tmp_i[:, :], t[2], -float(1 << 23), 127.0 * (1 << 23), ALU.mult, ALU.add)
                tt(t[3], t[3], tmp_i[:, :].bitcast(F32), ALU.mult)
                tt(rho[:, :], t[3], t[1], ALU.mult)
                ts(t[0], a, -1.0, None, ALU.mult)
                ts(t[1], b, -1.0, None, ALU.mult)
                tt(t[0], t[0], a, ALU.max)
                tt(t[1], t[1], b, ALU.max)
                tt(t[0], t[0], t[1], ALU.max)
                ts(t[1], t[0], 1.2e-38, None, ALU.is_lt)
                tt(t[0], t[0], t[1], ALU.add)
                dve.reciprocal(t[0], t[0]).then_inc(tab, 1)
                dve.wait_ge(tab, n())
                tt(t[2], a, t[0], ALU.mult)
                tt(t[2], t[2], t[1], ALU.add)
                tt(t[3], b, t[0], ALU.mult)
                tt(t[4], t[2], t[2], ALU.mult)
                tt(t[5], t[3], t[3], ALU.mult)
                tt(t[4], t[4], t[5], ALU.add)
                inverse_sqrt(dve, t[4], t[5], t[6], t[7], tmp_i[:, :], tab, n)
                c, s = t[2], t[3]
                tt(c, c, t[6], ALU.mult)
                tt(s, s, t[6], ALU.mult)
                tt(t[0], c, last_re, ALU.mult)
                tt(t[1], s, last_im, ALU.mult)
                tt(first[:, 0], t[0], t[1], ALU.subtract)
                tt(t[0], s, last_re, ALU.mult)
                tt(t[1], c, last_im, ALU.mult)
                tt(first[:, 1], t[0], t[1], ALU.add)
                dve.memset(rot[:, 0, :, 0:1], 1.0).then_inc(tab, 1)
                dve.memset(rot[:, 1, :, 0:1], 0.0).then_inc(tab, 1)
                dve.wait_ge(tab, n(2))
                m = 1
                while m < SEQ:
                    for k in range(KD):
                        ck, sk = c[:, k:k + 1], s[:, k:k + 1]
                        for i, (own, other, sign) in enumerate(((0, 1, ALU.subtract), (1, 0, ALU.add))):
                            dve.tensor_scalar(scratch[:, i, 0:m], rot[:, other, k, 0:m], sk, None, ALU.mult).then_inc(tab, 1)
                        dve.wait_ge(tab, n(2))
                        for i, (own, other, sign) in enumerate(((0, 1, ALU.subtract), (1, 0, ALU.add))):
                            dve.scalar_tensor_tensor(out=rot[:, own, k, m:2 * m], in0=rot[:, own, k, 0:m], scalar=ck,
                                                     in1=scratch[:, i, 0:m], op0=ALU.mult, op1=sign).then_inc(tab, 1)
                        dve.wait_ge(tab, n(2))
                    tt(t[0], c, c, ALU.mult)
                    tt(t[1], s, s, ALU.mult)
                    stt(s, s, 2.0, c, ALU.mult, ALU.mult)
                    tt(c, t[0], t[1], ALU.subtract)
                    m *= 2
                for k in range(KD):
                    re, im = init_re[:, k:k + 1], init_im[:, k:k + 1]
                    for i, (q, r2) in enumerate(((im, 1), (re, 1))):
                        dve.tensor_scalar(scratch[:, i], rot[:, 1, k, :], q, None, ALU.mult).then_inc(tab, 1)
                    dve.wait_ge(tab, n(2))
                    for i, (q, sign) in enumerate(((re, ALU.add), (im, ALU.subtract))):
                        dve.scalar_tensor_tensor(out=coef[:, i, k, :], in0=rot[:, 0, k, :], scalar=q,
                                                 in1=scratch[:, i], op0=ALU.mult, op1=sign).then_inc(tab, 1)
                    dve.wait_ge(tab, n(2))

        xs = sb("xs", [P, 2, D])
        h = sb("h", [P, TPG, D])
        hT = sb("hT", [P, KD, SEQ])
        r = sb("r", [P, 2, 2, SEQ])
        yT = sb("yT", [P, KD, SEQ])
        gated = sb("gated", [P, 2, 2, D])
        tp = [bank(f"tp{i}") for i in range(4)]
        dd = [bank(f"dd{i}") for i in range(2)]
        h_ready, h_used, xs_ready, hT_done, re_ready, im_ready, scanned, turned_re, turned_im, y_ready, dd_ready, dd_done, x_done = (
            sem(k) for k in ("h_ready", "h_used", "xs_ready", "hT_done", "re_ready", "im_ready", "scanned", "turned_re",
                             "turned_im", "y_ready", "dd_ready", "dd_done", "x_done"))
        NGB = SEQ // G
        UB = TPB // 2
        block = st.enter_context(nc.Block())

        @block.gpsimd
        def _(pool):
            pool.sem_inc(x_done, 2)
            with pool.Fori(0, BATCH) as b:
                for k in range(KD):
                    pool.wait_ge(hT_done, b * KD * NGB + KD * NGB)
                    pool.tensor_tensor(r[:, k, 1, :], coef[:, 1, k, :], hT[:, k, :], ALU.mult).then_inc(im_ready, 1)
                for k in range(KD):
                    pool.wait_ge(scanned, (b * KD + k) * 2 + 2)
                    pool.tensor_tensor(r[:, k, 1, :], rot[:, 1, k, :], r[:, k, 1, :], ALU.mult).then_inc(turned_im, 1)
                for u in range(UB):
                    pool.wait_ge(dd_done, b * UB + u + 1 + 2)
                    xx = x[:, bass.ds(b * TPB + 2 * u, 2), :]
                    pool.tensor_tensor(xx, xx, gated[:, u % 2], ALU.add).then_inc(x_done, 1)

        @block.tensor
        def _(pe):
            pe.sem_inc(h_used, TPG)
            with pe.Fori(0, BATCH) as b:
                for g in range(NGB):
                    for t in range(TPG):
                        pe.wait_ge(h_ready, b * TPB + g * TPG + t + 1)
                        for k in range(KD):
                            i = pe.transpose(tp[2 * g + k][:, t * P:(t + 1) * P], h[:, t, k * P:(k + 1) * P], ident[:, :])
                        i.then_inc(h_used, 1)
                pe.wait_ge(y_ready, (b + 1) * KD)
                for u in range(UB):
                    pe.wait_ge(dd_done, b * UB + u + 1)
                    for t in range(2):
                        for k in range(KD):
                            c = (2 * u + t) * P
                            i = pe.transpose(dd[u % 2][:, t * D + k * P:t * D + (k + 1) * P], yT[:, k, c:c + P], ident[:, :])
                    i.then_inc(dd_ready, 1)

        @block.scalar
        def _(act):
            with act.Fori(0, BATCH) as b:
                for g in range(NGB):
                    act.wait_ge(h_used, b * TPB + (g + 1) * TPG + TPG)
                    for k in range(KD):
                        act.activation(hT[:, k, g * G:(g + 1) * G], tp[2 * g + k][:, :], ACT.Copy).then_inc(hT_done, 1)

        @block.vector
        def _(dve):
            dve.sem_inc(dd_done, 2)
            with dve.Fori(0, BATCH) as b:
                for t in range(TPB):
                    T = b * TPB + t
                    dve.wait_ge(h_used, T + 1)
                    modulate(dve, env, T, h[:, t % TPG], xs[:, t % 2], b, SHIFT_A, SCALE_A, xs_ready, T + 1
                             ).then_inc(h_ready, 1)
                dve.wait_ge(hT_done, (b + 1) * KD * NGB)
                for k in range(KD):
                    dve.tensor_tensor(r[:, k, 0, :], coef[:, 0, k, :], hT[:, k, :], ALU.mult).then_inc(re_ready, 1)
                for k in range(KD):
                    decay = rho[:, k:k + 1].to_broadcast([P, SEQ])
                    for i, ready in enumerate((re_ready, im_ready)):
                        dve.wait_ge(ready, b * KD + k + 1)
                        dve.tensor_tensor_scan(r[:, k, i, :], decay, r[:, k, i, :], first[:, i, k:k + 1], ALU.mult, ALU.add
                                               ).then_inc(scanned, 1)
                    dve.wait_ge(scanned, (b * KD + k) * 2 + 2)
                    dve.tensor_tensor(r[:, k, 0, :], rot[:, 0, k, :], r[:, k, 0, :], ALU.mult).then_inc(turned_re, 1)
                for k in range(KD):
                    dve.wait_ge(turned_re, b * KD + k + 1)
                    dve.wait_ge(turned_im, b * KD + k + 1)
                    dve.tensor_tensor(yT[:, k, :], r[:, k, 0, :], r[:, k, 1, :], ALU.subtract).then_inc(y_ready, 1)
                for u in range(UB):
                    dve.wait_ge(dd_ready, b * UB + u + 1)
                    dve.wait_ge(x_done, b * UB + u + 1)
                    dve.tensor_tensor(gated[:, u % 2], dd[u % 2][:, :].rearrange("p (t d) -> p t d", d=D),
                                      modb[:, bass.ds(b, 1), GATE_A, :].to_broadcast([P, 2, D]), ALU.mult
                                      ).then_inc(dd_done, 1)


def dense_and_router(nc, A, env, layer):
    with ExitStack() as st:
        sb = lambda n, s, dt=F32: st.enter_context(nc.sbuf_tensor(f"dn{layer}_" + n, s, dt))
        sem = lambda n: st.enter_context(nc.semaphore(f"dn{layer}_" + n))
        bank = lambda n: st.enter_context(nc.psum_tensor(f"dn{layer}_" + n, [P, 512], F32))
        x, ident, modb, hall, logits = (env[k] for k in ("x", "ident", "modb", "hall", "logits"))
        shared = layer == 0
        FK = FF0 // P
        rw = sb("rw", [P, KD, E])
        if shared:
            wg, wu, wd = sb("wg", [P, KD, FF0]), sb("wu", [P, KD, FF0]), sb("wd", [P, FK, D])
        xs = sb("xs", [P, 2, D])
        h = sb("h", [P, TPG, D])
        hT = sb("hT", [P, KD, G])
        silu = sb("silu", [P, 2, G])
        aT = sb("aT", [P, FK, G])
        gated = sb("gated", [P, 2, 2, D])
        if not shared:
            gh = sb("gh", [P, 2, D])
            gh_ready = sem("gh_ready")
        tp = [bank(f"tp{i}") for i in range(KD)]
        gp = [bank(f"gp{i}") for i in range(2)]
        upp = [bank(f"up{i}") for i in range(2)]
        dd = [bank(f"dd{i}") for i in range(2)]
        w_loaded, h_ready, h_used, h_kept, xs_ready, hT_done = (
            sem("w_loaded"), sem("h_ready"), sem("h_used"), sem("h_kept"), sem("xs_ready"), sem("hT_done"))
        gu_ready, silu_ready, a_done, dd_ready, dd_done, x_done = (
            sem("gu_ready"), sem("silu_ready"), sem("a_done"), sem("dd_ready"), sem("dd_done"), sem("x_done"))
        block = st.enter_context(nc.Block())
        NGB = SEQ // G
        DDG = 1 + 2 * shared

        def sweep(engine, body):
            with engine.Fori(0, BATCH - 1) as b:
                body(b, False)
            body(BATCH - 1, True)

        @block.sync
        def _(sp):
            sp.dma_start(rw[:], A[f"rw{layer}T"].rearrange("(k p) n -> p k n", p=P)).then_inc(w_loaded, 16)
            if shared:
                for t, k in ((wg, "sgT"), (wu, "suT"), (wd, "sdT")):
                    sp.dma_start(t[:], A[k].rearrange("(k p) n -> p k n", p=P)).then_inc(w_loaded, 16)

        @block.gpsimd
        def _(pool):
            pool.sem_inc(h_kept, TPG)
            pool.sem_inc(x_done, 2)

            def keep(gi):
                for t in range(TPG):
                    T = gi * TPG + t
                    pool.wait_ge(h_ready, T + 1)
                    pool.tensor_copy(row(hall, T), h[:, t]).then_inc(h_kept, 1)
                    if not shared:
                        pool.wait_ge(gh_ready, T + 1)
                        pool.tensor_tensor(row(x, T), row(x, T), gh[:, t % 2], ALU.add).then_inc(x_done, 1)

            def add_shared(gi):
                for u in range(2):
                    pool.wait_ge(dd_done, gi * DDG + 1 + u + 1 + 2)
                    xx = x[:, bass.ds(gi * TPG + 2 * u, 2), :]
                    pool.tensor_tensor(xx, xx, gated[:, u], ALU.add).then_inc(x_done, 1)
            keep(0)

            def body(b, last):
                for g in range(NGB):
                    gi = b * NGB + g
                    if not (last and g == NGB - 1):
                        keep(gi + 1)
                    if shared:
                        add_shared(gi)
            sweep(pool, body)

        @block.tensor
        def _(pe):
            pe.sem_inc(h_used, TPG)
            pe.wait_ge(w_loaded, 16 * (1 + 3 * shared))

            def transposes(gi):
                pe.wait_ge(hT_done, gi * KD + KD)
                for t in range(TPG):
                    pe.wait_ge(h_ready, gi * TPG + t + 1)
                    for j in range(KD):
                        i = pe.transpose(tp[j][:, t * P:(t + 1) * P], h[:, t, j * P:(j + 1) * P], ident[:, :])
                    i.then_inc(h_used, 1)
            transposes(0)

            def body(b, last):
                df = counter()

                def dd_bank():
                    i = df()
                    pe.wait_ge(dd_done, b * NGB * DDG + i)
                    return dd[(i - 1) % 2]
                for g in range(NGB):
                    gi = b * NGB + g
                    pe.wait_ge(hT_done, gi * KD + 2 * KD)
                    bk = dd_bank()
                    for t in range(TPG):
                        for k in range(KD):
                            i = pe.matmul(bk[:, t * E:(t + 1) * E], hT[:, k, t * P:(t + 1) * P], rw[:, k, :],
                                          start=k == 0, stop=k == KD - 1)
                    i.then_inc(dd_ready, 1)
                    if shared:
                        for f in range(FK):
                            pe.wait_ge(a_done, gi * FK + f + 1)
                            for wt, bkk in ((wg, gp), (wu, upp)):
                                for k in range(KD):
                                    i = pe.matmul(bkk[f % 2][:, :], wt[:, k, f * P:(f + 1) * P], hT[:, k, :],
                                                  start=k == 0, stop=k == KD - 1)
                            i.then_inc(gu_ready, 1)
                    if not (last and g == NGB - 1):
                        transposes(gi + 1)
                    if shared:
                        pe.wait_ge(a_done, (gi + 1) * FK + 2)
                        for u in range(2):
                            bk = dd_bank()
                            for t in range(2):
                                for k in range(FK):
                                    c = (2 * u + t) * P
                                    i = pe.matmul(bk[:, t * D:(t + 1) * D], aT[:, k, c:c + P], wd[:, k, :],
                                                  start=k == 0, stop=k == FK - 1)
                            i.then_inc(dd_ready, 1)
            sweep(pe, body)

        @block.scalar
        def _(act):
            act.sem_inc(hT_done, KD)

            def copy_hT(gi):
                act.wait_ge(h_used, (gi + 1) * TPG + TPG)
                for j in range(KD):
                    act.activation(hT[:, j, :], tp[j][:, :], ACT.Copy).then_inc(hT_done, 1)
            copy_hT(0)

            def body(b, last):
                for g in range(NGB):
                    gi = b * NGB + g
                    if shared:
                        for f in range(FK):
                            act.wait_ge(gu_ready, gi * FK + f + 1)
                            act.activation(silu[:, f % 2], gp[f % 2][:, :], ACT.Silu).then_inc(silu_ready, 1)
                    if not (last and g == NGB - 1):
                        copy_hT(gi + 1)
            sweep(act, body)

        @block.vector
        def _(dve):
            dve.sem_inc(a_done, 2)
            dve.sem_inc(dd_done, 2)
            if not shared:
                dve.sem_inc(a_done, 1)

            def make_h(gi, batch):
                for t in range(TPG):
                    T = gi * TPG + t
                    dve.wait_ge(h_used, T + 1)
                    dve.wait_ge(h_kept, T + 1)
                    modulate(dve, env, T, h[:, t], xs[:, t % 2], batch, SHIFT_B, SCALE_B, xs_ready, T + 1
                             ).then_inc(h_ready, 1)
                    if not shared:
                        dve.wait_ge(h_ready, T + 1)
                        dve.wait_ge(x_done, T + 1)
                        dve.tensor_tensor(gh[:, t % 2], h[:, t],
                                          modb[:, bass.ds(batch, 1), GATE_B, :].rearrange("p o n -> p (o n)"),
                                          ALU.mult).then_inc(gh_ready, 1)
            make_h(0, 0)

            def body(b, last):
                df = counter()
                for g in range(NGB):
                    gi = b * NGB + g
                    if not (last and g == NGB - 1):
                        make_h(gi + 1, b + (g + 1) // NGB)
                    n = df()
                    dve.wait_ge(dd_ready, b * NGB * DDG + n)
                    dve.tensor_copy(logits[:, bass.ds(gi * TPG, TPG), :],
                                    dd[(n - 1) % 2][:, 0:TPG * E].rearrange("p (t e) -> p t e", e=E)).then_inc(dd_done, 1)
                    if not shared:
                        continue
                    for f in range(FK):
                        dve.wait_ge(silu_ready, gi * FK + f + 1)
                        dve.tensor_tensor(aT[:, f, :], upp[f % 2][:, :], silu[:, f % 2], ALU.mult).then_inc(a_done, 1)
                    for u in range(2):
                        n = df()
                        dve.wait_ge(dd_ready, b * NGB * DDG + n)
                        dve.wait_ge(x_done, gi * 2 + u + 1)
                        dve.tensor_tensor(gated[:, u], dd[(n - 1) % 2][:, :].rearrange("p (t d) -> p t d", d=D),
                                          modb[:, bass.ds(b, 1), GATE_B, :].to_broadcast([P, 2, D]), ALU.mult
                                          ).then_inc(dd_done, 1)
            sweep(dve, body)


def routing(nc, A, env, layer):
    with ExitStack() as st:
        sb = lambda n, s, dt=F32: st.enter_context(nc.sbuf_tensor(f"rt{layer}_" + n, s, dt))
        sem = lambda n: st.enter_context(nc.semaphore(f"rt{layer}_" + n))
        before, ones, hall, logits = (env[k] for k in ("before", "ones", "hall", "logits"))
        weight, put, get, experts = (env[k] for k in ("weight", "put", "get", "experts"))
        bias = sb("bias", [P, E])
        prob, work, m1, m2, both, rank = (sb(k, [P, NT, E]) for k in ("prob", "work", "m1", "m2", "both", "rank"))
        best = sb("best", [P, 2, NT])
        pick = sb("pick", [P, NT])
        order = sb("order", [P, E])
        run = sb("run", [P, NT, E])
        need = sb("need", [P, E])
        upto = sb("upto", [P, E])
        base = sb("base", [P, E])
        slot = sb("slot", [P, NT])
        slot2 = sb("slot2", [P, NT])
        block_id = sb("block_id", [P, NB0 + 1])
        fits = sb("fits", [P, NB0 + 1, E])
        ps = [st.enter_context(nc.psum_tensor(f"rt{layer}_ps{i}", [P, 512], F32)) for i in range(2)]
        step, bias_loaded, exp_in, exp_done, both_ready, ranks_ready, const_ready, routed, sent = (
            sem("step"), sem("bias_loaded"), sem("exp_in"), sem("exp_done"), sem("both_ready"), sem("ranks_ready"),
            sem("const_ready"), sem("routed"), sem("sent"))
        block = st.enter_context(nc.Block())

        def over_e(ap):
            return ap.unsqueeze(2).to_broadcast([P, NT, E])

        def over_t(ap):
            return ap.unsqueeze(1).to_broadcast([P, NT, E])

        @block.sync
        def _(sp):
            if layer == 0:
                sp.dma_start(bias[:, :], A["L0_ffn_routing_bias"].rearrange("(o e) -> o e", o=1).to_broadcast([P, E])
                             ).then_inc(bias_loaded, 16)

        @block.gpsimd
        def _(pool):
            pool.iota(order[:, :], pattern=[[-1, E]], base=E, channel_multiplier=0,
                      allow_small_or_imprecise_dtypes=True).then_inc(const_ready, 1)
            pool.iota(block_id[:, :], pattern=[[1, NB0 + 1]], base=0, channel_multiplier=0,
                      allow_small_or_imprecise_dtypes=True).then_inc(const_ready, 1)
            pool.wait_ge(env["zeroed"], 16 * env["zero_dmas"])
            pool.wait_ge(routed, 1)
            slots = env[f"slots{layer}"].ap()
            for t in range(NT):
                for c in range(2):
                    pool.indirect_dma_start(slots, bass.IndirectOffsetOnAxis(ap=put[:, c, t:t + 1], axis=0),
                                            hall[:, t, :], None, bounds_check=slots.shape[0] - 1,
                                            oob_is_err=False).then_inc(sent, 16)
            pool.wait_ge(sent, 16 * 2 * NT)

        @block.scalar
        def _(act):
            act.wait_ge(exp_in, 1)
            act.activation(prob[:], work[:], ACT.Exp, scale=-1.0 if layer == 0 else 1.0).then_inc(exp_done, 1)

        @block.tensor
        def _(pe):
            pe.wait_ge(both_ready, 1)
            m = both[:].rearrange("p t e -> p (t e)")
            pe.matmul(ps[0][:, 0:NT * E], before[:, :], m, start=True, stop=True).then_inc(ranks_ready, 1)
            pe.matmul(ps[1][:, 0:NT * E], ones[:, :], m, start=True, stop=True).then_inc(ranks_ready, 1)

        @block.vector
        def _(dve):
            n = counter()
            if layer == 0:
                dve.wait_ge(bias_loaded, 16)
                dve.tensor_tensor(work[:], logits[:], over_t(bias[:, :]), ALU.add).then_inc(exp_in, 1)
                dve.wait_ge(exp_done, 1)
                dve.tensor_scalar(work[:], prob[:], 1.0, None, ALU.add).then_inc(step, 1)
                dve.wait_ge(step, n())
                dve.reciprocal(prob[:], work[:]).then_inc(step, 1)
                dve.wait_ge(step, n())
            else:
                dve.tensor_reduce(pick[:, :], logits[:], AXX, ALU.max).then_inc(step, 1)
                dve.wait_ge(step, n())
                dve.tensor_tensor(work[:], logits[:], over_e(pick[:, :]), ALU.subtract).then_inc(exp_in, 1)
                dve.wait_ge(exp_done, 1)
                dve.tensor_reduce(pick[:, :], prob[:], AXX, ALU.add).then_inc(step, 1)
                dve.wait_ge(step, n())
                dve.reciprocal(slot[:, :], pick[:, :]).then_inc(step, 1)
                dve.wait_ge(step, n())
                dve.tensor_tensor(prob[:], prob[:], over_e(slot[:, :]), ALU.mult).then_inc(step, 1)
                dve.wait_ge(step, n())
            dve.wait_ge(const_ready, 2)
            for c, m in enumerate((m1, m2)):
                dve.tensor_reduce(best[:, c], prob[:], AXX, ALU.max).then_inc(step, 1)
                dve.wait_ge(step, n())
                dve.tensor_tensor(work[:], prob[:], over_e(best[:, c]), ALU.is_equal).then_inc(step, 1)
                dve.wait_ge(step, n())
                dve.tensor_tensor(work[:], work[:], over_t(order[:, :]), ALU.mult).then_inc(step, 1)
                dve.wait_ge(step, n())
                dve.tensor_reduce(pick[:, :], work[:], AXX, ALU.max).then_inc(step, 1)
                dve.wait_ge(step, n())
                dve.tensor_tensor(m[:], work[:], over_e(pick[:, :]), ALU.is_equal).then_inc(step, 1)
                dve.wait_ge(step, n())
                if c == 0:
                    dve.scalar_tensor_tensor(out=prob[:].rearrange("p t e -> p (t e)"),
                                             in0=m[:].rearrange("p t e -> p (t e)"), scalar=-4.0,
                                             in1=prob[:].rearrange("p t e -> p (t e)"),
                                             op0=ALU.mult, op1=ALU.add).then_inc(step, 1)
                    dve.wait_ge(step, n())
            dve.tensor_tensor(both[:], m1[:], m2[:], ALU.add).then_inc(both_ready, 1)
            dve.tensor_tensor(pick[:, :], best[:, 0], best[:, 1], ALU.add).then_inc(step, 1)
            dve.wait_ge(step, n())
            dve.reciprocal(slot[:, :], pick[:, :]).then_inc(step, 1)
            dve.wait_ge(step, n())
            for c in range(2):
                dve.tensor_tensor(weight[:, c], best[:, c], slot[:, :], ALU.mult).then_inc(step, 1)
            dve.wait_ge(step, n(2))
            dve.wait_ge(ranks_ready, 2)
            total = ps[1][:, 0:NT * E].rearrange("p (t e) -> p t e", e=E)
            for e in range(E):
                dve.tensor_tensor_scan(run[:, :, e], ones[:, 0:NT], total[:, :, e], 0.0, ALU.mult, ALU.add
                                       ).then_inc(step, 1)
            dve.wait_ge(step, n(E))
            dve.tensor_tensor(rank[:], run[:], total, ALU.subtract).then_inc(step, 1)
            dve.wait_ge(step, n())
            dve.tensor_tensor(rank[:], rank[:], ps[0][:, 0:NT * E].rearrange("p (t e) -> p t e", e=E), ALU.add
                              ).then_inc(step, 1)
            dve.wait_ge(step, n())
            if layer == 0:
                dve.tensor_scalar(need[:, :], run[:, NT - 1, :], 1.0 / BLK0,
                                  (BLK0 - 1) / BLK0 - 0.5 + 0.5 / BLK0, ALU.mult, ALU.add).then_inc(step, 1)
                dve.wait_ge(step, n())
                dve.tensor_scalar(need[:, :], need[:, :], ROUND, ROUND, ALU.add, ALU.subtract).then_inc(step, 1)
                dve.wait_ge(step, n())
                dve.tensor_tensor_scan(upto[:, :], ones[:, 0:E], need[:, :], 0.0, ALU.mult, ALU.add).then_inc(step, 1)
                dve.wait_ge(step, n())
                dve.tensor_tensor(base[:, :], upto[:, :], need[:, :], ALU.subtract).then_inc(step, 1)
                nb = NB0 + 1
                dve.tensor_tensor(fits[:], upto[:, :].unsqueeze(1).to_broadcast([P, nb, E]),
                                  block_id[:, :].unsqueeze(2).to_broadcast([P, nb, E]), ALU.is_le).then_inc(step, 1)
                dve.wait_ge(step, n(2))
                dve.tensor_scalar(base[:, :], base[:, :], float(BLK0), None, ALU.mult).then_inc(step, 1)
                dve.tensor_reduce(block_id[:, :], fits[:], AXX, ALU.add).then_inc(step, 1)
                dve.wait_ge(step, n(2))
                dve.tensor_scalar(experts[0:1, :], block_id[0:1, :], float(E - 1), None, ALU.min).then_inc(step, 1)
                n()
            else:
                dve.tensor_scalar(base[:, :], order[:, :], -float(SLOTS1), float(E * SLOTS1), ALU.mult, ALU.add
                                  ).then_inc(step, 1)
                dve.wait_ge(step, n())
            dve.tensor_tensor(work[:], rank[:], over_t(base[:, :]), ALU.add).then_inc(step, 1)
            dve.wait_ge(step, n())
            for c, m in enumerate((m1, m2)):
                dve.tensor_tensor(prob[:], m[:], work[:], ALU.mult).then_inc(step, 1)
                dve.wait_ge(step, n())
                dve.tensor_reduce(slot[:, :], prob[:], AXX, ALU.add).then_inc(step, 1)
                dve.wait_ge(step, n())
                if layer == 1:
                    dve.tensor_tensor(prob[:], m[:], rank[:], ALU.mult).then_inc(step, 1)
                    dve.wait_ge(step, n())
                    dve.tensor_reduce(pick[:, :], prob[:], AXX, ALU.add).then_inc(step, 1)
                    dve.wait_ge(step, n())
                    dve.tensor_scalar(pick[:, :], pick[:, :], float(CAP), None, ALU.is_lt).then_inc(step, 1)
                    dve.wait_ge(step, n())
                    dve.tensor_tensor(weight[:, c], weight[:, c], pick[:, :], ALU.mult).then_inc(step, 1)
                    dve.tensor_tensor(slot[:, :], slot[:, :], pick[:, :], ALU.mult).then_inc(step, 1)
                    dve.wait_ge(step, n(2))
                    dve.tensor_scalar(slot2[:, :], pick[:, :], -float(DROP), float(DROP), ALU.mult, ALU.add
                                      ).then_inc(step, 1)
                    dve.tensor_copy(get[:, c], slot[:, :]).then_inc(step, 1)
                    dve.wait_ge(step, n(2))
                    dve.tensor_tensor(put[:, c], slot[:, :], slot2[:, :], ALU.add).then_inc(step, 1)
                    dve.wait_ge(step, n())
                else:
                    dve.tensor_copy(get[:, c], slot[:, :]).then_inc(step, 1)
                    dve.tensor_copy(put[:, c], slot[:, :]).then_inc(step, 1)
                    dve.wait_ge(step, n(2))
            dve.sem_inc(routed, 1)


def expert_blocks(nc, A, env, layer):
    with ExitStack() as st:
        sb = lambda n, s, dt=F32: st.enter_context(nc.sbuf_tensor(f"ex{layer}_" + n, s, dt))
        sem = lambda n: st.enter_context(nc.semaphore(f"ex{layer}_" + n))
        bank = lambda n: st.enter_context(nc.psum_tensor(f"ex{layer}_" + n, [P, 512], F32))
        ident, experts = env["ident"], env["experts"]
        gated = layer == 0
        FF = FF0 if gated else FF1
        FK = FF // P
        R = P if gated else RT1
        BLK = TPG * R
        NBLK = NB0 if gated else E * NB1
        SAME = 1 if gated else NB1
        BODY = 2 * SAME
        LOOPS = (NBLK - 1) // BODY
        win = [sb(f"win{i}", [P, 1 + gated, KD, FF]) for i in range(2)]
        wout = [sb(f"wout{i}", [P, FK, D]) for i in range(2)]
        rows = sb("rows", [P, 2, TPG, D])
        hT = sb("hT", [P, KD, BLK])
        silu = sb("silu", [P, 2, BLK])
        aT = sb("aT", [P, FK, BLK])
        ysb = sb("ysb", [P, 2, TPG, D])
        tp = [bank(f"tp{i}") for i in range(KD)]
        gp = [bank(f"gp{i}") for i in range(2)]
        upp = [bank(f"up{i}") for i in range(2)]
        dd = [bank(f"dd{i}") for i in range(2)]
        w_loaded = [sem(f"w_loaded{i}") for i in range(2)]
        w_used = [sem(f"w_used{i}") for i in range(2)]
        rows_loaded = [sem(f"rows_loaded{i}") for i in range(2)]
        y_stored = [sem(f"y_stored{i}") for i in range(2)]
        rows_used, hT_done, gu_ready, silu_ready, a_done, dd_ready, dd_done = (
            sem("rows_used"), sem("hT_done"), sem("gu_ready"), sem("silu_ready"), sem("a_done"),
            sem("dd_ready"), sem("dd_done"))
        block = st.enter_context(nc.Block())
        src = env[f"slots{layer}"].ap()
        dst = env[f"y{layer}"].ap()
        n_w = 3 if gated else 2

        def sweep(engine, body):
            with engine.Fori(0, LOOPS) as i:
                for s in range(BODY):
                    body(i * BODY + s, i, s)
            for s in range(NBLK - LOOPS * BODY):
                body(LOOPS * BODY + s, LOOPS, s)

        def last(i, s):
            return isinstance(i, int) and i * BODY + s == NBLK - 1

        @block.sync
        def _(sp):
            def load_weights(i, s):
                par = s // SAME % 2
                sp.wait_ge(w_used[par], i + 1)
                if gated:
                    e = sp.value_load(experts[0:1, bass.ds(i * BODY + s, 1)], min_val=0, max_val=E - 1)
                    names = (("L0_ffn_gate_w", win[par][:, 0]), ("L0_ffn_up_w", win[par][:, 1]), ("L0_ffn_down_w", wout[par][:]))
                else:
                    e = i * 2 + par
                    names = (("L1_ffn_w1", win[par][:, 0]), ("L1_ffn_w2", wout[par][:]))
                for name, tile in names:
                    sp.dma_start(tile, A[name][bass.ds(e, 1)].rearrange("o (k p) n -> p (o k) n", p=P)
                                 ).then_inc(w_loaded[par], 16)

            def load_rows(n, s):
                sp.wait_ge(rows_used, n + 1)
                sp.dma_start(rows[0:R, s % 2], src[bass.ds(n * BLK, BLK), :].rearrange("(t p) d -> p t d", p=R)
                             ).then_inc(rows_loaded[s % 2], 16)
            load_weights(0, 0)
            load_rows(0, 0)

            def body(n, i, s):
                if not last(i, s):
                    ni, ns = (i, s + 1) if s + 1 < BODY else (i + 1, 0)
                    load_rows(n + 1, s + 1)
                    if ns % SAME == 0:
                        load_weights(ni, ns)
                sp.wait_ge(dd_done, 2 * n + 2 + 2)
                sp.dma_start(dst[bass.ds(n * BLK, BLK), :].rearrange("(t p) d -> p t d", p=R), ysb[0:R, s % 2]
                             ).then_inc(y_stored[s % 2], 16)
            sweep(sp, body)
            sp.wait_ge(y_stored[0], 16 * (-(-NBLK // 2)) + 16)
            sp.wait_ge(y_stored[1], 16 * (NBLK // 2) + 16)

        @block.tensor
        def _(pe):
            for i in range(2):
                pe.sem_inc(w_used[i], 1)
            pe.sem_inc(rows_used, 2)

            def transposes(n, i, s):
                pe.wait_ge(hT_done, n * KD + KD)
                pe.wait_ge(rows_loaded[s % 2], 16 * (i * (BODY // 2) + s // 2 + 1))
                for t in range(TPG):
                    for j in range(KD):
                        m = pe.transpose(tp[j][:, t * R:(t + 1) * R], rows[0:R, s % 2, t, j * P:(j + 1) * P],
                                         ident[0:R, 0:R])
                m.then_inc(rows_used, 1)
            transposes(0, 0, 0)

            def body(n, i, s):
                par = s // SAME % 2
                if s % SAME == 0:
                    pe.wait_ge(w_loaded[par], 16 * n_w * (i + 1))
                pe.wait_ge(hT_done, n * KD + 2 * KD)
                for f in range(FK):
                    pe.wait_ge(a_done, n * FK + f + 1)
                    for m in range(1 + gated):
                        for k in range(KD):
                            q = pe.matmul((gp, upp)[m][f % 2][:, 0:BLK], win[par][:, m, k, f * P:(f + 1) * P], hT[:, k, :],
                                          start=k == 0, stop=k == KD - 1)
                    q.then_inc(gu_ready, 1)
                if not last(i, s):
                    transposes(n + 1, *((i, s + 1) if s + 1 < BODY else (i + 1, 0)))
                pe.wait_ge(a_done, (n + 1) * FK + 2)
                for u in range(2):
                    pe.wait_ge(dd_done, 2 * n + u + 1)
                    for t in range(2):
                        for k in range(FK):
                            c = (2 * u + t) * R
                            q = pe.matmul(dd[u][0:R, t * D:(t + 1) * D], aT[:, k, c:c + R], wout[par][:, k, :],
                                          start=k == 0, stop=k == FK - 1)
                    if u == 0:
                        q.then_inc(dd_ready, 1)
                q.then_inc(dd_ready, 1)
                if s % SAME == SAME - 1:
                    pe.wait_ge(dd_ready, 2 * n + 2)
                    pe.sem_inc(w_used[par], 1)
            sweep(pe, body)

        @block.scalar
        def _(act):
            act.sem_inc(hT_done, KD)
            if not gated:
                act.sem_inc(a_done, 2)

            def copy_hT(n):
                act.wait_ge(rows_used, n + 1 + 2)
                for j in range(KD):
                    act.activation(hT[:, j, :], tp[j][:, 0:BLK], ACT.Copy).then_inc(hT_done, 1)
            copy_hT(0)

            def body(n, i, s):
                for f in range(FK):
                    act.wait_ge(gu_ready, n * FK + f + 1)
                    if gated:
                        act.activation(silu[:, f % 2], gp[f % 2][:, 0:BLK], ACT.Silu).then_inc(silu_ready, 1)
                    else:
                        act.activation(aT[:, f, :], gp[f % 2][:, 0:BLK], ACT.Silu).then_inc(a_done, 1)
                if not last(i, s):
                    copy_hT(n + 1)
            sweep(act, body)

        @block.vector
        def _(dve):
            if gated:
                dve.sem_inc(a_done, 2)
            dve.sem_inc(dd_done, 2)
            for i in range(2):
                dve.sem_inc(y_stored[i], 16)

            def body(n, i, s):
                if gated:
                    for f in range(FK):
                        dve.wait_ge(silu_ready, n * FK + f + 1)
                        dve.tensor_tensor(aT[:, f, :], upp[f % 2][:, 0:BLK], silu[:, f % 2], ALU.mult).then_inc(a_done, 1)
                dve.wait_ge(y_stored[s % 2], 16 * (i * (BODY // 2) + s // 2) + 16)
                for u in range(2):
                    dve.wait_ge(dd_ready, 2 * n + u + 1)
                    dve.tensor_copy(ysb[0:R, s % 2, 2 * u:2 * u + 2, :],
                                    dd[u][0:R, :].rearrange("p (t d) -> p t d", d=D)).then_inc(dd_done, 1)
            sweep(dve, body)


def combine(nc, A, env, layer, out=None):
    with ExitStack() as st:
        sb = lambda n, s, dt=F32: st.enter_context(nc.sbuf_tensor(f"cb{layer}_" + n, s, dt))
        sem = lambda n: st.enter_context(nc.semaphore(f"cb{layer}_" + n))
        x, modb, weight, get = (env[k] for k in ("x", "modb", "weight", "get"))
        NBUF = 4
        y = sb("y", [P, NBUF, 2, D])
        s1 = sb("s1", [P, NBUF, D])
        fetched = [sem(f"fetched{i}") for i in range(NBUF)]
        y_used, scaled, summed, x_done = sem("y_used"), sem("scaled"), sem("summed"), sem("x_done")
        block = st.enter_context(nc.Block())

        @block.gpsimd
        def _(pool):
            for t in range(NT):
                if t >= NBUF:
                    pool.wait_ge(y_used, t - NBUF + 1)
                for c in range(2):
                    pool.indirect_dma_start(y[:, t % NBUF, c, :], None, env[f"y{layer}"].ap(),
                                            bass.IndirectOffsetOnAxis(ap=get[:, c, t:t + 1], axis=0)
                                            ).then_inc(fetched[t % NBUF], 16)

        @block.vector
        def _(dve):
            for t in range(NT):
                i = t % NBUF
                dve.wait_ge(fetched[i], 32 * (t // NBUF + 1))
                dve.tensor_scalar(s1[:, i], y[:, i, 0], weight[:, 0, t:t + 1], None, ALU.mult).then_inc(scaled, 1)
                dve.wait_ge(scaled, t + 1)
                dve.scalar_tensor_tensor(out=s1[:, i], in0=y[:, i, 1], scalar=weight[:, 1, t:t + 1], in1=s1[:, i],
                                         op0=ALU.mult, op1=ALU.add).then_inc(y_used, 1)
                dve.wait_ge(y_used, t + 1)
                dve.tensor_tensor(s1[:, i], s1[:, i], modb[:, t // TPB, GATE_B, :], ALU.mult).then_inc(summed, 1)
                dve.wait_ge(summed, t + 1)
                dve.tensor_tensor(x[:, t], x[:, t], s1[:, i], ALU.add).then_inc(x_done, 1)


def store_x(nc, env, out):
    with ExitStack() as st:
        stored = st.enter_context(nc.semaphore("stored"))
        block = st.enter_context(nc.Block())

        @block.sync
        def _(sp):
            sp.dma_start(out.rearrange("b (t p) d -> p (b t) d", p=P), env["x"][:]).then_inc(stored, 16)
            sp.wait_ge(stored, 16)
            sp.wait_ge(env["zeroed"], 16 * env["zero_dmas"])


_PLAIN = ["L0_attn_x", "L0_wmod", "L1_wmod", "L0_ffn_gate_w", "L0_ffn_up_w", "L0_ffn_down_w", "L0_ffn_routing_bias",
          "L1_ffn_w1", "L1_ffn_w2"]
_TRANSPOSED = {"ct0": "L0_c", "ct1": "L1_c", "wqT": "L0_attn_wq", "wkT": "L0_attn_wk", "wvT": "L0_attn_wv",
               "woT": "L0_attn_wo", "rfT": "L0_attn_rf", "sgT": "L0_ffn_shared_gate", "suT": "L0_ffn_shared_up",
               "sdT": "L0_ffn_shared_down", "rw0T": "L0_ffn_router_w", "rw1T": "L1_ffn_router_w"}
_COLUMNS = ["L1_attn_phazor_real", "L1_attn_phazor_imag", "L1_attn_phazor_init_real", "L1_attn_phazor_init_imag",
            "L1_attn_last_conv_real", "L1_attn_last_conv_imag"]


def layout(inputs):
    a = {k: np.ascontiguousarray(inputs[k]) for k in _PLAIN}
    a |= {k: np.ascontiguousarray(np.asarray(inputs[v]).T) for k, v in _TRANSPOSED.items()}
    a["phasor"] = np.ascontiguousarray(
        np.stack([np.asarray(inputs[k]) for k in _COLUMNS]).reshape(6, KD, P).transpose(2, 0, 1))
    return a


def kernel(**inputs):
    import concourse.bacc as _bacc
    from concourse.bass_utils import run_bass_kernel_spmd as _run

    nc = _bacc.Bacc("TRN2", target_bir_lowering=False, num_devices=1)
    arrays = layout(inputs)
    A = {k: nc.dram_tensor(k, v.shape, mybir.dt.from_np(v.dtype), kind="ExternalInput").ap() for k, v in arrays.items()}
    out = nc.dram_tensor("out", (BATCH, SEQ, D), F32, kind="ExternalOutput").ap()
    build_program(nc, A, out)
    return _run(nc, [arrays], core_ids=[0]).results[0]["out"]
```

```python
import math
from contextlib import ExitStack

import numpy as np

import concourse.bass as bass
from concourse import mybir

F32 = mybir.dt.float32
F32R = mybir.dt.float32r
I32 = mybir.dt.int32
U32 = mybir.dt.uint32
ACT = mybir.ActivationFunctionType
ALU = mybir.AluOpType
AXX = mybir.AxisListType.X

P = 128
BATCH, SEQ, D = 4, 1024, 256
TOK = BATCH * SEQ
NT = TOK // P
TPB = SEQ // P
KD = D // P
G = 512
TPG = G // P
NG = TOK // G
HEADS, DH, FEAT = 16, 16, 64
HPK = P // DH
PAIRS = HEADS // 2
VA = DH + 2
EPS = 1e-5
QN_MAX = 165.0
ROUND = 1.5 * 2.0 ** 23
E = 8
FF0, FF1 = 512, 1024
BLK0 = 512
NB0 = (2 * TOK + E * (BLK0 - 1)) // BLK0
CAP = int(1.25 * TOK * 2 / E) + 1
BLK1, RT1 = 432, 108
NB1 = -(-CAP // BLK1)
SLOTS1 = NB1 * BLK1
STATS_STEPS = 19
ZERO = 512
DROP = 1 << 20
SHIFT_A, SCALE_A, GATE_A, SHIFT_B, SCALE_B, GATE_B = range(6)


def counter(n=0):

    def more(k=1):
        nonlocal n
        n += k
        return n
    return more


def one(ap):
    return ap.rearrange("p o n -> p (o n)")


def row(ap, i):
    return one(ap[:, bass.ds(i, 1), :])


def build_program(nc, A, out, stop=99):
    ctx = ExitStack()
    with ctx:
        def sb(name, shape, dt=F32, stack=ctx):
            return stack.enter_context(nc.sbuf_tensor(name, shape, dt))

        def sem(name):
            return ctx.enter_context(nc.semaphore(name))

        S = {}
        x = sb("x", [P, NT, D])
        ident = sb("ident", [P, P])
        before = sb("before", [P, P])
        ones = sb("ones", [P, P])
        half_pi = sb("half_pi", [P, 1])
        zero = sb("zero", [P, ZERO])
        modb = sb("modb", [P, BATCH, 6, D])
        stats = sb("stats", [P, NT, 6])
        mean = sb("mean", [P, NT])
        rstd = sb("rstd", [P, NT])
        ntmp = sb("ntmp", [P, 3, NT])
        seed = sb("seed", [P, NT], I32)
        mod_rows = [nc.dram_tensor(f"mod_rows{l}", (BATCH, 6 * D), F32) for l in range(2)]
        slots0 = nc.dram_tensor("slots0", (NB0 * BLK0, D), F32)
        slots1 = nc.dram_tensor("slots1", (E * SLOTS1, D), F32)
        y0 = nc.dram_tensor("y0", (NB0 * BLK0, D), F32)
        y1 = nc.dram_tensor("y1", (E * SLOTS1, D), F32)
        zeroed = sem("zeroed")
        stats_done, rstd_step = sem("stats_done"), sem("rstd_step")
        mod_loaded = sem("mod_loaded")
        env = dict(locals())
        setup(nc, A, env)
        layer_stats(nc, env, 0)
        if stop >= 1:
            attention(nc, A, env)
        if stop >= 2:
            layer_stats(nc, env, 1)
            experts_of(nc, A, env, 0)
        if stop >= 3:
            layer_stats(nc, env, 2)
            recurrence(nc, A, env)
        if stop >= 4:
            layer_stats(nc, env, 3)
            experts_of(nc, A, env, 1)
        store_x(nc, env, out)


def experts_of(nc, A, env, layer):
    with ExitStack() as st:
        sb = lambda n, s, dt=F32: st.enter_context(nc.sbuf_tensor(f"{n}{layer}", s, dt))
        own = dict(env)
        own["weight"] = sb("weight", [P, 2, NT])
        own["put"] = sb("put", [P, 2, NT], U32)
        own["get"] = sb("get", [P, 2, NT], U32)
        own["experts"] = sb("experts", [1, NB0 + 1], I32)
        with ExitStack() as st2:
            own["hall"] = st2.enter_context(nc.sbuf_tensor(f"hall{layer}", [P, NT, D], F32))
            own["logits"] = st2.enter_context(nc.sbuf_tensor(f"logits{layer}", [P, NT, E], F32))
            dense_and_router(nc, A, own, layer)
            routing(nc, A, own, layer)
        expert_blocks(nc, A, own, layer)
        combine(nc, A, own, layer)


def setup(nc, A, env):
    with ExitStack() as st:
        sb = lambda n, s, dt=F32: st.enter_context(nc.sbuf_tensor(n, s, dt))
        sem = lambda n: st.enter_context(nc.semaphore(n))
        x, ident, before, ones, half_pi = (env[k] for k in ("x", "ident", "before", "ones", "half_pi"))
        ct = sb("ct", [P, 2, KD, BATCH])
        wmod = sb("wmod", [P, 2, KD, 6 * D])
        mods = sb("mods", [BATCH, 2, 6, D])
        sgn = sb("sgn", [BATCH, 2, D])
        zero = env["zero"]
        env["zero_dmas"] = 0
        ps = st.enter_context(nc.psum_tensor("mod_ps", [BATCH, 2, 3, 512], F32))
        loaded, silu_done, mod_ps_ready, copied = sem("loaded"), sem("silu_done"), sem("mod_ps_ready"), sem("copied")
        mod_step, mods_ready, rows_stored, const_step, zero_ready, x_loaded = (
            sem("mod_step"), sem("mods_ready"), sem("rows_stored"), sem("const_step"), sem("zero_ready"), sem("x_loaded"))
        block = st.enter_context(nc.Block())

        @block.sync
        def _(sp):
            for l in range(2):
                sp.dma_start(ct[:, l], A[f"ct{l}"].rearrange("(k p) b -> p k b", p=P)).then_inc(loaded, 16)
                sp.dma_start(wmod[:, l], A[f"L{l}_wmod"].rearrange("(k p) n -> p k n", p=P)).then_inc(loaded, 16)
            xin = A["L0_attn_x"].rearrange("b (t p) d -> p (b t) d", p=P)
            for q in range(4):
                sp.dma_start(x[:, 8 * q:8 * q + 8, :], xin[:, 8 * q:8 * q + 8, :]).then_inc(x_loaded, 16)
            sp.wait_ge(mods_ready, 1)
            for l in range(2):
                sp.dma_start(env["mod_rows"][l].ap(), mods[:, l].rearrange("b s d -> b (s d)")).then_inc(rows_stored, 16)
            sp.wait_ge(rows_stored, 32)
            sp.dma_start(env["modb"][:].rearrange("p b s d -> p (b s d)"),
                         env["mod_rows"][0].ap().rearrange("(o b) n -> o (b n)", o=1).to_broadcast([P, BATCH * 6 * D])
                         ).then_inc(env["mod_loaded"], 16)
            sp.wait_ge(x_loaded, 64)
            sp.wait_ge(env["mod_loaded"], 16)

        @block.gpsimd
        def _(pool):
            pool.memset(ident[:, :], 0.0).then_inc(const_step, 1)
            pool.memset(ones[:, :], 1.0).then_inc(const_step, 1)
            pool.wait_ge(const_step, 2)
            pool.affine_select(out=ident[:, :], in_=ident[:, :], compare_op=ALU.not_equal, fill=1.0,
                               base=0, pattern=[[-1, P]], channel_multiplier=1).then_inc(const_step, 1)
            pool.affine_select(out=before[:, :], in_=ones[:, :], compare_op=ALU.is_gt, fill=0.0,
                               base=0, pattern=[[1, P]], channel_multiplier=-1).then_inc(const_step, 1)
            pool.memset(half_pi[:, :], math.pi / 2).then_inc(const_step, 1)
            pool.wait_ge(const_step, 5)

        @block.scalar
        def _(act):
            act.wait_ge(loaded, 64)
            act.activation(ct[:], ct[:], ACT.Silu).then_inc(silu_done, 1)

        @block.tensor
        def _(pe):
            pe.wait_ge(silu_done, 1)
            for l in range(2):
                for n in range(3):
                    if l == 1:
                        pe.wait_ge(copied, n + 1)
                    for k in range(KD):
                        mm = pe.matmul(ps[:, 0, n], ct[:, l, k, :], wmod[:, l, k, 512 * n:512 * n + 512],
                                       start=k == 0, stop=k == KD - 1)
                    mm.then_inc(mod_ps_ready, 1)

        @block.vector
        def _(dve):
            dve.memset(zero[:, :], 0.0).then_inc(zero_ready, 1)
            for l in range(2):
                for n in range(3):
                    dve.wait_ge(mod_ps_ready, 3 * l + n + 1)
                    dve.tensor_copy(mods[:, l, 2 * n:2 * n + 2, :],
                                    ps[:, 0, n].rearrange("b (s d) -> b s d", s=2)).then_inc(copied, 1)
            dve.wait_ge(copied, 6)
            n = counter()
            for l in range(2):
                for scale in (SCALE_A, SCALE_B):
                    dve.tensor_scalar(mods[:, l, scale], mods[:, l, scale], 1.0, None, ALU.add).then_inc(mod_step, 1)
                    n()
                for gate in (GATE_A, GATE_B):
                    g = mods[:, l, gate]
                    dve.tensor_scalar(sgn[:, 0], g, 0.0, 2.0, ALU.is_ge, ALU.mult).then_inc(mod_step, 1)
                    dve.wait_ge(mod_step, n())
                    dve.scalar_tensor_tensor(out=sgn[:, 1], in0=sgn[:, 0], scalar=-1.0, in1=g,
                                             op0=ALU.add, op1=ALU.mult).then_inc(mod_step, 1)
                    dve.wait_ge(mod_step, n())
                    dve.tensor_scalar(sgn[:, 1], sgn[:, 1], 0.25, None, ALU.max).then_inc(mod_step, 1)
                    dve.wait_ge(mod_step, n())
                    dve.scalar_tensor_tensor(out=g, in0=sgn[:, 0], scalar=-1.0, in1=sgn[:, 1],
                                             op0=ALU.add, op1=ALU.mult).then_inc(mod_step, 1)
                    dve.wait_ge(mod_step, n())
            dve.tensor_copy(sgn[:, 0, 0:1], mods[:, 0, 0, 0:1]).then_inc(mods_ready, 1)


def layer_stats(nc, env, at):
    with ExitStack() as st:
        x, stats, mean, rstd, ntmp, seed = (env[k] for k in ("x", "stats", "mean", "rstd", "ntmp", "seed"))
        stats_done, rstd_step = env["stats_done"], env["rstd_step"]
        block = st.enter_context(nc.Block())

        @block.vector
        def _(dve):
            with dve.Fori(0, BATCH) as b:
                for t in range(TPB):
                    dve.bn_stats(row(stats, b * TPB + t), row(x, b * TPB + t)).then_inc(stats_done, 1)
            dve.wait_ge(stats_done, (at + 1) * NT)
            var, half, y, y2 = ntmp[:, 0], ntmp[:, 1], rstd[:, :], ntmp[:, 2]
            mean_e, m2_e, mean_o, m2_o = (stats[:, :, i] for i in (1, 2, 4, 5))
            n = counter(at * STATS_STEPS)
            dve.tensor_tensor(half, mean_e, mean_o, ALU.subtract).then_inc(rstd_step, 1)
            dve.tensor_tensor(var, m2_e, m2_o, ALU.add).then_inc(rstd_step, 1)
            dve.tensor_tensor(y2, mean_e, mean_o, ALU.add).then_inc(rstd_step, 1)
            dve.wait_ge(rstd_step, n(3))
            dve.tensor_tensor(half, half, half, ALU.mult).then_inc(rstd_step, 1)
            dve.tensor_scalar(mean[:, :], y2, 0.5, None, ALU.mult).then_inc(rstd_step, 1)
            dve.tensor_scalar(var, var, 1.0 / D, EPS, ALU.mult, ALU.add).then_inc(rstd_step, 1)
            dve.wait_ge(rstd_step, n(3))
            dve.scalar_tensor_tensor(out=var, in0=half, scalar=0.25, in1=var, op0=ALU.mult, op1=ALU.add
                                     ).then_inc(rstd_step, 1)
            dve.wait_ge(rstd_step, n())
            inverse_sqrt(dve, var, half, y, y2, seed[:, :], rstd_step, n)
            assert n(0) == (at + 1) * STATS_STEPS


def inverse_sqrt(dve, v, half, y, y2, seed, step, n):
    dve.tensor_scalar(seed, v.bitcast(I32), 1, None, ALU.logical_shift_right).then_inc(step, 1)
    dve.tensor_scalar(half, v, -0.5, None, ALU.mult).then_inc(step, 1)
    dve.wait_ge(step, n(2))
    dve.tensor_scalar(y.bitcast(I32), seed, -1.0, float(0x5F3759DF), ALU.mult, ALU.add).then_inc(step, 1)
    dve.wait_ge(step, n())
    for _ in range(3):
        dve.tensor_tensor(y2, y, y, ALU.mult).then_inc(step, 1)
        dve.wait_ge(step, n())
        dve.tensor_tensor(y2, y2, half, ALU.mult).then_inc(step, 1)
        dve.wait_ge(step, n())
        dve.scalar_tensor_tensor(out=y, in0=y2, scalar=1.5, in1=y, op0=ALU.add, op1=ALU.mult).then_inc(step, 1)
        dve.wait_ge(step, n())


def modulate(dve, env, T, dst, xs, batch, shift, scale, step, value):
    x, mean, rstd, modb = env["x"], env["mean"], env["rstd"], env["modb"]

    def mod(i):
        return modb[:, bass.ds(batch, 1), i, :].rearrange("p o n -> p (o n)")
    dve.scalar_tensor_tensor(out=xs, in0=row(x, T), scalar=mean[:, bass.ds(T, 1)], in1=mod(scale),
                             op0=ALU.subtract, op1=ALU.mult).then_inc(step, 1)
    dve.wait_ge(step, value)
    return dve.scalar_tensor_tensor(out=dst, in0=xs, scalar=rstd[:, bass.ds(T, 1)], in1=mod(shift),
                                    op0=ALU.mult, op1=ALU.add)


def attention(nc, A, env):
    with ExitStack() as st:
        sb = lambda n, s, dt=F32: st.enter_context(nc.sbuf_tensor("at_" + n, s, dt))
        sem = lambda n: st.enter_context(nc.semaphore("at_" + n))
        bank = lambda n: st.enter_context(nc.psum_tensor("at_" + n, [P, 512], F32))
        x, ident, modb, half_pi = (env[k] for k in ("x", "ident", "modb", "half_pi"))
        NGB = SEQ // G
        HP = PAIRS // KD
        w = {k: sb(k, [P, KD, D]) for k in ("wqT", "wkT", "wvT", "woT")}
        rf = sb("rf", [P, HPK * FEAT])
        headsel = sb("headsel", [P, HPK])
        headblk = sb("headblk", [P, HPK, DH])
        log_k = sb("log_k", [P, 1])
        log_q = sb("log_q", [P, 1])
        xs = sb("xs", [P, 2, D])
        h = sb("h", [P, TPG, D])
        hT = sb("hT", [P, KD, SEQ])
        qkT = sb("qkT", [P, 2, KD, SEQ])
        sq = sb("sq", [P, KD, SEQ])
        ks = sb("ks", [P, TPB, 2, HEADS])
        floor = sb("floor", [P, KD, SEQ])
        va = sb("va", [P, TPB, HEADS, DH])
        turn = sb("turn", [P, 2, 512])
        frac = sb("frac", [P, 2, 512])
        fabs = sb("fabs", [P, 2, 512])
        kf = sb("kf", [P, 2, 2, HEADS * FEAT])
        sums = sb("sums", [P, 2, 512])
        raw = sums
        kvT = sb("kvT", [P, KD, 2, HP, 2, DH])
        kzT = sb("kzT", [P, KD, 2, HP, 2, DH])
        qf = sb("qf", [P, 2, HP, 2, G])
        den = sb("den", [P, 2, G])
        oT = sb("oT", [P, KD, G])
        att = sb("att", [P, 2, 2, D])
        mm = [bank(f"mm{i}") for i in range(2)]
        dd = [bank(f"dd{i}") for i in range(2)]
        up = [bank(f"u{i}") for i in range(2)]
        acc = [bank(f"acc{i}") for i in range(2)]
        w_loaded, rf_zero, rf_ready, const_step, const_ready = (
            sem("w_loaded"), sem("rf_zero"), sem("rf_ready"), sem("const_step"), sem("const_ready"))
        h_ready, h_used, xs_ready = sem("h_ready"), sem("h_used"), sem("xs_ready")
        mm_ready, mm_done, dd_ready, dd_done = sem("mm_ready"), sem("mm_done"), sem("dd_ready"), sem("dd_done")
        u_ready, turn_ready, frac_ready, fabs_ready, feat_ready, kf_used, qf_used = (
            sem("u_ready"), sem("turn_ready"), sem("frac_ready"), sem("fabs_ready"),
            sem("feat_ready"), sem("kf_used"), sem("qf_used"))
        norms_ready, ks_ready, sums_ready, z_ready, den_done, inv_ready, raw_ready, oT_ready, x_done = (
            sem(k) for k in ("norms_ready", "ks_ready", "sums_ready", "z_ready", "den_done", "inv_ready", "raw_ready",
                             "oT_ready", "x_done"))
        qn_ready, floor_ready = sem("qn_ready"), sem("floor_ready")
        block = st.enter_context(nc.Block())
        MM_HT, MM_QK, MM_S = KD * NGB, 2 * KD * NGB, 2
        MM_BATCH = MM_HT + MM_QK + MM_S
        MM_RB = MM_BATCH - MM_HT
        DD_V, DD_N, DD_O = TPB // 2, KD * NGB, TPB // 2
        DD_BATCH = DD_V + DD_N + DD_O
        U_K = 2 * TPB
        UNITS = KD * NGB
        U_BATCH = U_K + HP * UNITS

        @block.sync
        def _(sp):
            for k in w:
                sp.dma_start(w[k][:], A[k].rearrange("(k p) n -> p k n", p=P)).then_inc(w_loaded, 16)
            sp.wait_ge(rf_zero, 1)
            for i in range(HPK):
                sp.dma_start(rf[i * DH:(i + 1) * DH, i * FEAT:(i + 1) * FEAT], A["rfT"]).then_inc(w_loaded, 16)
            for name, rows in (("slots0", NB0 * BLK0), ("slots1", E * SLOTS1)):
                per = rows * D // P
                flat = env[name].ap().rearrange("(p n) d -> p (n d)", p=P)
                for at in range(0, per, ZERO):
                    n = min(ZERO, per - at)
                    sp.dma_start(flat[:, at:at + n], env["zero"][:, 0:n]).then_inc(env["zeroed"], 16)
                    env["zero_dmas"] += 1

        @block.gpsimd
        def _(pool):
            pool.memset(rf[:, :], 0.0).then_inc(rf_zero, 1)
            pool.memset(headsel[:, :], 1.0).then_inc(const_step, 1)
            pool.memset(headblk[:], 1.0).then_inc(const_step, 1)
            pool.wait_ge(const_step, 2)
            for n, (m, extra) in enumerate(((headsel, []), (headblk, [[0, DH]]))):
                pool.affine_select(out=m[:], in_=m[:], compare_op=ALU.is_ge, fill=0.0, base=0,
                                   pattern=[[-DH, HPK]] + extra, channel_multiplier=1).then_inc(const_step, 1)
                pool.wait_ge(const_step, 3 + n)
                pool.affine_select(out=m[:], in_=m[:], compare_op=ALU.is_ge, fill=0.0, base=DH - 1,
                                   pattern=[[DH, HPK]] + extra, channel_multiplier=-1).then_inc(const_ready, 1)
            for m, v in ((kvT[:], 0.0), (kzT[:], 0.0), (ks[:], 0.0), (log_k[:, :], -0.5 * math.log(FEAT)),
                         (log_q[:, :], math.log(1e-6) + 0.5 * math.log(FEAT))):
                pool.memset(m, v).then_inc(const_ready, 1)
            pool.sem_inc(x_done, 2)
            with pool.Fori(0, BATCH) as b:
                for u in range(DD_O):
                    pool.wait_ge(dd_done, b * DD_BATCH + DD_V + DD_N + u + 1 + 2)
                    xx = x[:, bass.ds(b * TPB + 2 * u, 2), :]
                    pool.tensor_tensor(xx, xx, att[:, u % 2], ALU.add).then_inc(x_done, 1)

        @block.tensor
        def _(pe):
            pe.sem_inc(h_used, TPG)
            pe.sem_inc(kf_used, 2)
            pe.sem_inc(qf_used, 2)
            pe.wait_ge(rf_ready, 1)
            pe.wait_ge(w_loaded, 16 * (4 + HPK))
            pe.wait_ge(const_ready, 7)
            with pe.Fori(0, BATCH) as b:
                mf, df = counter(), counter()

                def mm_bank():
                    i = mf()
                    pe.wait_ge(mm_done, b * MM_BATCH + i)
                    return mm[(i - 1) % 2]

                def dd_bank():
                    i = df()
                    pe.wait_ge(dd_done, b * DD_BATCH + i)
                    return dd[(i - 1) % 2]

                def project(u):
                    pe.wait_ge(frac_ready, b * U_BATCH + u + 1)
                    if u < U_K:
                        t, j = u // 2, u % 2
                        pe.matmul(up[u % 2][:, :], qkT[:, 1, j, t * P:(t + 1) * P], rf[:, :],
                                  start=True, stop=True).then_inc(u_ready, 1)
                    else:
                        unit, c = (u - U_K) // HP, (u - U_K) % HP
                        g, j = unit // KD, unit % KD
                        pe.matmul(up[u % 2][:, :], rf[:, c * P:(c + 1) * P], qkT[:, 0, j, g * G:(g + 1) * G],
                                  start=True, stop=True).then_inc(u_ready, 1)

                for g in range(NGB):
                    banks = [mm_bank(), mm_bank()]
                    for t in range(TPG):
                        pe.wait_ge(h_ready, b * TPB + g * TPG + t + 1)
                        for j in range(KD):
                            i = pe.transpose(banks[j][:, t * P:(t + 1) * P], h[:, t, j * P:(j + 1) * P], ident[:, :])
                        i.then_inc(h_used, 1)

                def heads(name):
                    for g in range(NGB):
                        for j in range(KD):
                            bk = mm_bank()
                            if name == "wkT":
                                pe.wait_ge(mm_done, b * MM_BATCH + (g + 1) * KD + 2)
                            for k in range(KD):
                                i = pe.matmul(bk[:, :], w[name][:, k, j * P:(j + 1) * P], hT[:, k, g * G:(g + 1) * G],
                                              start=k == 0, stop=k == KD - 1)
                            i.then_inc(mm_ready, 1)

                def values(t2):
                    bk = dd_bank()
                    for t in (2 * t2, 2 * t2 + 1):
                        for k in range(KD):
                            i = pe.matmul(bk[:, (t % 2) * D:(t % 2 + 1) * D], hT[:, k, t * P:(t + 1) * P],
                                          w["wvT"][:, k, :], start=k == 0, stop=k == KD - 1)
                    i.then_inc(dd_ready, 1)
                heads("wkT")
                values(0)
                values(1)
                pe.wait_ge(mm_done, b * MM_BATCH + MM_HT + MM_QK // 2 + 2)
                pe.wait_ge(raw_ready, b * UNITS + 1)
                for t in range(TPB):
                    for j in range(KD):
                        c = (t * KD + j) * HPK
                        i = pe.matmul(acc[0][:, c:c + HPK], sq[:, j, t * P:(t + 1) * P], headsel[:, :],
                                      start=True, stop=True)
                i.then_inc(norms_ready, 1)
                heads("wqT")
                for t2 in range(2, DD_V):
                    values(t2)
                for g in range(NGB):
                    for j in range(KD):
                        pe.wait_ge(mm_done, b * MM_BATCH + MM_HT + MM_QK // 2 + KD * g + j + 1 + 2)
                        bk = dd_bank()
                        pe.matmul(bk[:, :], headblk[:].rearrange("p h v -> p (h v)"), sq[:, j, g * G:(g + 1) * G],
                                  start=True, stop=True).then_inc(dd_ready, 1)

                project(0)
                project(1)
                for t in range(TPB):
                    if t + 1 < TPB:
                        project(2 * t + 2)
                        project(2 * t + 3)
                    else:
                        for c in range(HP):
                            project(U_K + c)
                    if t == 0:
                        pe.wait_ge(dd_done, b * DD_BATCH + DD_V + 2)
                        pe.wait_ge(ks_ready, b + 1)
                    pe.wait_ge(feat_ready, b * U_BATCH + 2 * t + 2 + 2)
                    for j in range(KD):
                        for c in range(HP):
                            p = j * HP + c
                            pe.matmul(acc[0][32 * c:32 * c + 32, j * 256:(j + 1) * 256],
                                      va[:, t, 2 * p:2 * p + 2, :].rearrange("p h v -> p (h v)"),
                                      kf[:, t % 2, :, p * P:(p + 1) * P],
                                      start=t == 0 and j == 0, stop=t == TPB - 1, skip_group_check=True)
                    for c in range(4):
                        i = pe.matmul(acc[1][32 * c:32 * c + 32, :], ks[:, t].rearrange("p m h -> p (m h)"),
                                      kf[:, t % 2, c // 2, (c % 2) * 512:(c % 2 + 1) * 512],
                                      start=t == 0, stop=t == TPB - 1, skip_group_check=True)
                    i.then_inc(kf_used, 1)
                pe.wait_ge(sums_ready, (b + 1) * 2)
                bk = mm_bank()
                for j in range(KD):
                    for cs in range(2):
                        i = pe.transpose(bk[:, (2 * j + cs) * P:(2 * j + cs + 1) * P],
                                         sums[:, 0, (2 * j + cs) * P:(2 * j + cs + 1) * P], ident[:, :])
                i.then_inc(mm_ready, 1)
                bk = mm_bank()
                for c in range(HP):
                    i = pe.transpose(bk[:, c * P:(c + 1) * P], sums[:, 1, c * P:(c + 1) * P], ident[:, :])
                i.then_inc(mm_ready, 1)

                def write_out(g):
                    pe.wait_ge(oT_ready, b * UNITS + (g + 1) * KD)
                    for t2 in range(TPG // 2):
                        bk = dd_bank()
                        for t in (2 * t2, 2 * t2 + 1):
                            for k in range(KD):
                                i = pe.matmul(bk[:, (t % 2) * D:(t % 2 + 1) * D], oT[:, k, t * P:(t + 1) * P],
                                              w["woT"][:, k, :], start=k == 0, stop=k == KD - 1)
                        i.then_inc(dd_ready, 1)

                for n in range(UNITS):
                    if n + 1 < UNITS:
                        for c in range(HP):
                            project(U_K + (n + 1) * HP + c)
                    if n == 0:
                        pe.wait_ge(mm_done, b * MM_BATCH + MM_BATCH + 2)
                    pe.wait_ge(feat_ready, b * U_BATCH + U_K + (n + 1) * HP + 2)
                    j = n % KD
                    for a, m, left, done in ((1, kzT, den_done, z_ready), (0, kvT, raw_ready, qf_used)):
                        pe.wait_ge(left, b * UNITS + n + 1)
                        for cs in range(2):
                            for c in range(HP):
                                i = pe.matmul(acc[a][32 * c:32 * c + 32, :], m[:, j, cs, c].rearrange("p h v -> p (h v)"),
                                              qf[:, n % 2, c, cs, :], start=cs == 0, stop=cs == 1)
                        i.then_inc(done, 1)
                    if n >= KD and n % KD == 0:
                        write_out(n // KD - 1)
                write_out(NGB - 1)

        @block.scalar
        def _(act):
            act.wait_ge(w_loaded, 16 * (4 + HPK))
            act.activation(rf[:, :], rf[:, :], ACT.Copy, scale=1.0 / (2 * math.pi)).then_inc(rf_ready, 1)
            act.sem_inc(mm_done, 2)
            act.sem_inc(feat_ready, 2)
            act.sem_inc(raw_ready, 1)
            act.wait_ge(const_ready, 7)
            with act.Fori(0, BATCH) as b:
                rf_ = counter()

                def mm_filled():
                    n = rf_()
                    act.wait_ge(mm_ready, b * MM_RB + n)
                    return mm[(n - 1) % 2]

                for g in range(NGB):
                    act.wait_ge(h_used, b * TPB + (g + 1) * TPG + TPG)
                    for j in range(KD):
                        act.activation(hT[:, j, g * G:(g + 1) * G], mm[j][:, :], ACT.Copy).then_inc(mm_done, 1)
                for m in (1, 0):
                    for g in range(NGB):
                        for j in range(KD):
                            bk = mm_filled()
                            act.activation(qkT[:, m, j, g * G:(g + 1) * G], bk[:, :], ACT.Copy)
                            act.activation(sq[:, j, g * G:(g + 1) * G], bk[:, :], ACT.Square).then_inc(mm_done, 1)
                    if m == 1:
                        act.wait_ge(norms_ready, b + 1)
                        act.activation(ks[:, :, 0, :], acc[0][:, 0:TPB * HEADS].rearrange("p (t h) -> p t h", h=HEADS),
                                       ACT.Exp, scale=-0.5, bias=log_k[:, 0:1]).then_inc(ks_ready, 1)
                act.wait_ge(qn_ready, (b + 1) * DD_N)
                act.activation(floor[:], floor[:], ACT.Exp, scale=0.5, bias=log_q[:, 0:1]).then_inc(floor_ready, 1)

                def features(u, cos, sin):
                    n = b * U_BATCH + u
                    i = u % 2
                    act.wait_ge(frac_ready, n + 1 + 2)
                    act.activation(fabs[:, i], frac[:, i], ACT.Abs).then_inc(fabs_ready, 1)
                    act.activation(sin, frac[:, i], ACT.Sin, scale=2 * math.pi)
                    act.wait_ge(fabs_ready, n + 1)
                    act.activation(cos, fabs[:, i], ACT.Sin, scale=-2 * math.pi,
                                   bias=half_pi[:, 0:1]).then_inc(feat_ready, 1)
                for t in range(TPB):
                    act.wait_ge(kf_used, b * TPB + t + 1)
                    for j in range(KD):
                        features(2 * t + j, *(kf[:, t % 2, cs, j * 512:(j + 1) * 512] for cs in range(2)))

                def copy_raw(n):
                    act.wait_ge(qf_used, b * UNITS + n + 1 + 2)
                    act.wait_ge(oT_ready, b * UNITS + n - 1) if n >= 2 else None
                    act.activation(raw[:, n % 2], acc[0][:, :], ACT.Copy).then_inc(raw_ready, 1)
                for n in range(UNITS):
                    act.wait_ge(qf_used, b * UNITS + n + 1)
                    for c in range(HP):
                        features(U_K + n * HP + c, *(qf[:, n % 2, c, cs, :] for cs in range(2)))
                    if n > 0:
                        copy_raw(n - 1)
                        continue
                    act.wait_ge(kf_used, (b + 1) * TPB + 2)
                    for a in range(2):
                        act.activation(sums[:, a], acc[a][:, :], ACT.Copy).then_inc(sums_ready, 1)
                    bk = mm_filled()
                    for hh in range(2):
                        q = slice(hh * FEAT, (hh + 1) * FEAT)
                        i = act.activation(kvT[q, :, :, :, hh, :].rearrange("p j s c v -> p (j s c) v"),
                                           bk[q, :].rearrange("p (n h v) -> p n h v", h=2, v=DH)[:, :, hh, :], ACT.Copy)
                    i.then_inc(mm_done, 1)
                    bk = mm_filled()
                    for j in range(KD):
                        for cs in range(2):
                            for hh in range(2):
                                q = slice(hh * FEAT, (hh + 1) * FEAT)
                                at = (2 * cs + j) * 32 + j * HPK + hh
                                i = act.activation(kzT[q, j, cs, :, hh, :],
                                                   bk[q, at:at + (P + 2) * (HP - 1) + 1:P + 2].unsqueeze(2)
                                                   .to_broadcast([FEAT, HP, DH]), ACT.Copy)
                    i.then_inc(mm_done, 1)
                copy_raw(UNITS - 1)

        @block.vector
        def _(dve):
            dve.sem_inc(dd_done, 2)
            dve.sem_inc(frac_ready, 2)
            dve.sem_inc(den_done, 1)

            def make_h(b, tiles):
                for t in tiles:
                    T = b * TPB + t
                    dve.wait_ge(h_used, T + 1)
                    modulate(dve, env, T, h[:, t % TPG], xs[:, t % 2], b, SHIFT_A, SCALE_A, xs_ready, T + 1
                             ).then_inc(h_ready, 1)
            make_h(0, range(TPG))

            def batch(b, last):
                make_h(b, range(TPG, TPB))
                dve.wait_ge(ks_ready, b + 1)
                for t2 in range(DD_V):
                    dve.wait_ge(dd_ready, b * DD_BATCH + t2 + 1)
                    dve.tensor_tensor(va[:, 2 * t2:2 * t2 + 2],
                                      dd[t2 % 2][:, :].rearrange("p (t h v) -> p t h v", t=2, v=DH),
                                      ks[:, 2 * t2:2 * t2 + 2, 0, :].unsqueeze(3).to_broadcast([P, 2, HEADS, DH]),
                                      ALU.mult).then_inc(dd_done, 1)
                for g in range(NGB):
                    for j in range(KD):
                        u = DD_V + KD * g + j
                        dve.wait_ge(dd_ready, b * DD_BATCH + u + 1)
                        i = dve.tensor_scalar(floor[:, j, g * G:(g + 1) * G], dd[u % 2][:, :], QN_MAX, None, ALU.min)
                        i.then_inc(dd_done, 1)
                        dve.wait_ge(dd_done, b * DD_BATCH + u + 1 + 2)
                        dve.sem_inc(qn_ready, 1)

                def reduce_turns(us):
                    for u in us:
                        n = b * U_BATCH + u
                        dve.wait_ge(u_ready, n + 1)
                        dve.tensor_scalar(turn[:, u % 2], up[u % 2][:, :], ROUND, ROUND, ALU.add, ALU.subtract
                                          ).then_inc(turn_ready, 1)
                        dve.wait_ge(turn_ready, n + 1)
                        dve.wait_ge(feat_ready, n + 1)
                        dve.tensor_tensor(frac[:, u % 2], up[u % 2][:, :], turn[:, u % 2], ALU.subtract
                                          ).then_inc(frac_ready, 1)

                def unit_turns(n):
                    reduce_turns(range(U_K + n * HP, U_K + (n + 1) * HP))

                def denominator(n):
                    g, j = n // KD, n % KD
                    dve.wait_ge(z_ready, b * UNITS + n + 1)
                    dve.wait_ge(floor_ready, b + 1)
                    dve.tensor_tensor(den[:, n % 2], acc[1][:, :], floor[:, j, g * G:(g + 1) * G], ALU.max
                                      ).then_inc(den_done, 1)

                def divide(n):
                    N = b * UNITS + n
                    dve.wait_ge(den_done, N + 1 + 1)
                    dve.reciprocal(den[:, n % 2], den[:, n % 2]).then_inc(inv_ready, 1)
                    dve.wait_ge(inv_ready, N + 1)
                    dve.wait_ge(raw_ready, N + 1 + 1)
                    dve.tensor_tensor(oT[:, n % KD, :], raw[:, n % 2], den[:, n % 2], ALU.mult).then_inc(oT_ready, 1)

                def gate_out(g):
                    for t2 in range(TPG // 2):
                        u = g * TPG // 2 + t2
                        dve.wait_ge(dd_ready, b * DD_BATCH + DD_V + DD_N + u + 1)
                        dve.wait_ge(x_done, b * DD_O + u + 1)
                        dve.tensor_tensor(att[:, u % 2], dd[u % 2][:, :].rearrange("p (t d) -> p t d", d=D),
                                          modb[:, bass.ds(b, 1), GATE_A, :].to_broadcast([P, 2, D]), ALU.mult
                                          ).then_inc(dd_done, 1)
                reduce_turns(range(U_K))
                unit_turns(0)
                for n in range(UNITS):
                    if n + 1 < UNITS:
                        unit_turns(n + 1)
                    if n > 0:
                        divide(n - 1)
                    denominator(n)
                    if n >= KD and n % KD == 0:
                        gate_out(n // KD - 1)
                if not last:
                    make_h(b + 1, range(TPG))
                divide(UNITS - 1)
                gate_out(NGB - 1)

            with dve.Fori(0, BATCH - 1) as b:
                batch(b, False)
            batch(BATCH - 1, True)


def recurrence(nc, A, env):
    with ExitStack() as st:
        sb = lambda n, s, dt=F32: st.enter_context(nc.sbuf_tensor("rc_" + n, s, dt))
        sem = lambda n: st.enter_context(nc.semaphore("rc_" + n))
        bank = lambda n: st.enter_context(nc.psum_tensor("rc_" + n, [P, 512], F32))
        x, ident, modb = (env[k] for k in ("x", "ident", "modb"))
        par = sb("par", [P, 6, KD])
        rho = sb("rho", [P, KD])
        first = sb("first", [P, 2, KD])
        rot = sb("rot", [P, 2, KD, SEQ])
        coef = sb("coef", [P, 2, KD, SEQ])
        tmp = sb("tmp", [P, 10, KD])
        tmp_i = sb("tmp_i", [P, KD], I32)
        scratch = sb("scratch", [P, 2, SEQ])
        par_loaded, tab = sem("par_loaded"), sem("tab")

        with nc.Block() as block:
            @block.sync
            def _(sp):
                sp.dma_start(par[:], A["phasor"]).then_inc(par_loaded, 16)
                sp.dma_start(modb[:].rearrange("p b s d -> p (b s d)"),
                             env["mod_rows"][1].ap().rearrange("(o b) n -> o (b n)", o=1).to_broadcast([P, BATCH * 6 * D])
                             ).then_inc(env["mod_loaded"], 16)
                sp.wait_ge(env["mod_loaded"], 32)

            @block.vector
            def _(dve):
                n = counter()
                a, b, init_re, init_im, last_re, last_im = (par[:, i] for i in range(6))
                t = [tmp[:, i] for i in range(10)]
                dve.wait_ge(par_loaded, 16)

                def ts(out, in0, s1, s2, op0, op1=None):
                    dve.tensor_scalar(out, in0, s1, s2, op0, *([op1] if op1 is not None else [])).then_inc(tab, 1)
                    dve.wait_ge(tab, n())

                def tt(out, in0, in1, op):
                    dve.tensor_tensor(out, in0, in1, op).then_inc(tab, 1)
                    dve.wait_ge(tab, n())

                def stt(out, in0, s, in1, op0, op1):
                    dve.scalar_tensor_tensor(out=out, in0=in0, scalar=s, in1=in1, op0=op0, op1=op1).then_inc(tab, 1)
                    dve.wait_ge(tab, n())

                tt(t[0], a, a, ALU.mult)
                tt(t[1], b, b, ALU.mult)
                tt(t[0], t[0], t[1], ALU.add)
                ts(t[1], t[0], 87.3, None, ALU.is_le)
                ts(t[0], t[0], 87.3, None, ALU.min)
                ts(t[2], t[0], math.log2(math.e), ROUND, ALU.mult, ALU.add)
                ts(t[2], t[2], ROUND, None, ALU.subtract)
                ln2_hi = 0.693359375
                stt(t[0], t[2], -ln2_hi, t[0], ALU.mult, ALU.add)
                stt(t[0], t[2], -(math.log(2) - ln2_hi), t[0], ALU.mult, ALU.add)
                ts(t[0], t[0], -1.0, None, ALU.mult)
                ts(t[3], t[0], 1.0 / 8, 1.0, ALU.mult, ALU.add)
                for k in range(7, 0, -1):
                    stt(t[3], t[3], 1.0 / k, t[0], ALU.mult, ALU.mult)
                    ts(t[3], t[3], 1.0, None, ALU.add)
                ts(tmp_i[:, :], t[2], -float(1 << 23), 127.0 * (1 << 23), ALU.mult, ALU.add)
                tt(t[3], t[3], tmp_i[:, :].bitcast(F32), ALU.mult)
                tt(rho[:, :], t[3], t[1], ALU.mult)
                ts(t[0], a, -1.0, None, ALU.mult)
                ts(t[1], b, -1.0, None, ALU.mult)
                tt(t[0], t[0], a, ALU.max)
                tt(t[1], t[1], b, ALU.max)
                tt(t[0], t[0], t[1], ALU.max)
                ts(t[1], t[0], 1.2e-38, None, ALU.is_lt)
                tt(t[0], t[0], t[1], ALU.add)
                dve.reciprocal(t[0], t[0]).then_inc(tab, 1)
                dve.wait_ge(tab, n())
                tt(t[2], a, t[0], ALU.mult)
                tt(t[2], t[2], t[1], ALU.add)
                tt(t[3], b, t[0], ALU.mult)
                tt(t[4], t[2], t[2], ALU.mult)
                tt(t[5], t[3], t[3], ALU.mult)
                tt(t[4], t[4], t[5], ALU.add)
                inverse_sqrt(dve, t[4], t[5], t[6], t[7], tmp_i[:, :], tab, n)
                c, s = t[2], t[3]
                tt(c, c, t[6], ALU.mult)
                tt(s, s, t[6], ALU.mult)
                tt(t[0], c, last_re, ALU.mult)
                tt(t[1], s, last_im, ALU.mult)
                tt(first[:, 0], t[0], t[1], ALU.subtract)
                tt(t[0], s, last_re, ALU.mult)
                tt(t[1], c, last_im, ALU.mult)
                tt(first[:, 1], t[0], t[1], ALU.add)
                dve.memset(rot[:, 0, :, 0:1], 1.0).then_inc(tab, 1)
                dve.memset(rot[:, 1, :, 0:1], 0.0).then_inc(tab, 1)
                dve.wait_ge(tab, n(2))
                m = 1
                while m < SEQ:
                    for k in range(KD):
                        ck, sk = c[:, k:k + 1], s[:, k:k + 1]
                        for i, (own, other, sign) in enumerate(((0, 1, ALU.subtract), (1, 0, ALU.add))):
                            dve.tensor_scalar(scratch[:, i, 0:m], rot[:, other, k, 0:m], sk, None, ALU.mult).then_inc(tab, 1)
                        dve.wait_ge(tab, n(2))
                        for i, (own, other, sign) in enumerate(((0, 1, ALU.subtract), (1, 0, ALU.add))):
                            dve.scalar_tensor_tensor(out=rot[:, own, k, m:2 * m], in0=rot[:, own, k, 0:m], scalar=ck,
                                                     in1=scratch[:, i, 0:m], op0=ALU.mult, op1=sign).then_inc(tab, 1)
                        dve.wait_ge(tab, n(2))
                    tt(t[0], c, c, ALU.mult)
                    tt(t[1], s, s, ALU.mult)
                    stt(s, s, 2.0, c, ALU.mult, ALU.mult)
                    tt(c, t[0], t[1], ALU.subtract)
                    m *= 2
                for k in range(KD):
                    re, im = init_re[:, k:k + 1], init_im[:, k:k + 1]
                    for i, (q, r2) in enumerate(((im, 1), (re, 1))):
                        dve.tensor_scalar(scratch[:, i], rot[:, 1, k, :], q, None, ALU.mult).then_inc(tab, 1)
                    dve.wait_ge(tab, n(2))
                    for i, (q, sign) in enumerate(((re, ALU.add), (im, ALU.subtract))):
                        dve.scalar_tensor_tensor(out=coef[:, i, k, :], in0=rot[:, 0, k, :], scalar=q,
                                                 in1=scratch[:, i], op0=ALU.mult, op1=sign).then_inc(tab, 1)
                    dve.wait_ge(tab, n(2))

        xs = sb("xs", [P, 2, D])
        h = sb("h", [P, TPG, D])
        hT = sb("hT", [P, KD, SEQ])
        r = sb("r", [P, 2, 2, SEQ])
        yT = sb("yT", [P, KD, SEQ])
        gated = sb("gated", [P, 2, 2, D])
        tp = [bank(f"tp{i}") for i in range(4)]
        dd = [bank(f"dd{i}") for i in range(2)]
        h_ready, h_used, xs_ready, hT_done, re_ready, im_ready, scanned, turned_re, turned_im, y_ready, dd_ready, dd_done, x_done = (
            sem(k) for k in ("h_ready", "h_used", "xs_ready", "hT_done", "re_ready", "im_ready", "scanned", "turned_re",
                             "turned_im", "y_ready", "dd_ready", "dd_done", "x_done"))
        NGB = SEQ // G
        UB = TPB // 2
        block = st.enter_context(nc.Block())

        @block.gpsimd
        def _(pool):
            pool.sem_inc(x_done, 2)
            with pool.Fori(0, BATCH) as b:
                for k in range(KD):
                    pool.wait_ge(hT_done, b * KD * NGB + KD * NGB)
                    pool.tensor_tensor(r[:, k, 1, :], coef[:, 1, k, :], hT[:, k, :], ALU.mult).then_inc(im_ready, 1)
                for k in range(KD):
                    pool.wait_ge(scanned, (b * KD + k) * 2 + 2)
                    pool.tensor_tensor(r[:, k, 1, :], rot[:, 1, k, :], r[:, k, 1, :], ALU.mult).then_inc(turned_im, 1)
                for u in range(UB):
                    pool.wait_ge(dd_done, b * UB + u + 1 + 2)
                    xx = x[:, bass.ds(b * TPB + 2 * u, 2), :]
                    pool.tensor_tensor(xx, xx, gated[:, u % 2], ALU.add).then_inc(x_done, 1)

        @block.tensor
        def _(pe):
            pe.sem_inc(h_used, TPG)
            with pe.Fori(0, BATCH) as b:
                for g in range(NGB):
                    for t in range(TPG):
                        pe.wait_ge(h_ready, b * TPB + g * TPG + t + 1)
                        for k in range(KD):
                            i = pe.transpose(tp[2 * g + k][:, t * P:(t + 1) * P], h[:, t, k * P:(k + 1) * P], ident[:, :])
                        i.then_inc(h_used, 1)
                pe.wait_ge(y_ready, (b + 1) * KD)
                for u in range(UB):
                    pe.wait_ge(dd_done, b * UB + u + 1)
                    for t in range(2):
                        for k in range(KD):
                            c = (2 * u + t) * P
                            i = pe.transpose(dd[u % 2][:, t * D + k * P:t * D + (k + 1) * P], yT[:, k, c:c + P], ident[:, :])
                    i.then_inc(dd_ready, 1)

        @block.scalar
        def _(act):
            with act.Fori(0, BATCH) as b:
                for g in range(NGB):
                    act.wait_ge(h_used, b * TPB + (g + 1) * TPG + TPG)
                    for k in range(KD):
                        act.activation(hT[:, k, g * G:(g + 1) * G], tp[2 * g + k][:, :], ACT.Copy).then_inc(hT_done, 1)

        @block.vector
        def _(dve):
            dve.sem_inc(dd_done, 2)
            with dve.Fori(0, BATCH) as b:
                for t in range(TPB):
                    T = b * TPB + t
                    dve.wait_ge(h_used, T + 1)
                    modulate(dve, env, T, h[:, t % TPG], xs[:, t % 2], b, SHIFT_A, SCALE_A, xs_ready, T + 1
                             ).then_inc(h_ready, 1)
                dve.wait_ge(hT_done, (b + 1) * KD * NGB)
                for k in range(KD):
                    dve.tensor_tensor(r[:, k, 0, :], coef[:, 0, k, :], hT[:, k, :], ALU.mult).then_inc(re_ready, 1)
                for k in range(KD):
                    decay = rho[:, k:k + 1].to_broadcast([P, SEQ])
                    for i, ready in enumerate((re_ready, im_ready)):
                        dve.wait_ge(ready, b * KD + k + 1)
                        dve.tensor_tensor_scan(r[:, k, i, :], decay, r[:, k, i, :], first[:, i, k:k + 1], ALU.mult, ALU.add
                                               ).then_inc(scanned, 1)
                    dve.wait_ge(scanned, (b * KD + k) * 2 + 2)
                    dve.tensor_tensor(r[:, k, 0, :], rot[:, 0, k, :], r[:, k, 0, :], ALU.mult).then_inc(turned_re, 1)
                for k in range(KD):
                    dve.wait_ge(turned_re, b * KD + k + 1)
                    dve.wait_ge(turned_im, b * KD + k + 1)
                    dve.tensor_tensor(yT[:, k, :], r[:, k, 0, :], r[:, k, 1, :], ALU.subtract).then_inc(y_ready, 1)
                for u in range(UB):
                    dve.wait_ge(dd_ready, b * UB + u + 1)
                    dve.wait_ge(x_done, b * UB + u + 1)
                    dve.tensor_tensor(gated[:, u % 2], dd[u % 2][:, :].rearrange("p (t d) -> p t d", d=D),
                                      modb[:, bass.ds(b, 1), GATE_A, :].to_broadcast([P, 2, D]), ALU.mult
                                      ).then_inc(dd_done, 1)


def dense_and_router(nc, A, env, layer):
    with ExitStack() as st:
        sb = lambda n, s, dt=F32: st.enter_context(nc.sbuf_tensor(f"dn{layer}_" + n, s, dt))
        sem = lambda n: st.enter_context(nc.semaphore(f"dn{layer}_" + n))
        bank = lambda n: st.enter_context(nc.psum_tensor(f"dn{layer}_" + n, [P, 512], F32))
        x, ident, modb, hall, logits = (env[k] for k in ("x", "ident", "modb", "hall", "logits"))
        shared = layer == 0
        FK = FF0 // P
        rw = sb("rw", [P, KD, E])
        if shared:
            wg, wu, wd = sb("wg", [P, KD, FF0]), sb("wu", [P, KD, FF0]), sb("wd", [P, FK, D])
        xs = sb("xs", [P, 2, D])
        h = sb("h", [P, TPG, D])
        hT = sb("hT", [P, KD, G])
        silu = sb("silu", [P, 2, G])
        aT = sb("aT", [P, FK, G])
        gated = sb("gated", [P, 2, 2, D])
        if not shared:
            gh = sb("gh", [P, 2, D])
            gh_ready = sem("gh_ready")
        tp = [bank(f"tp{i}") for i in range(KD)]
        gp = [bank(f"gp{i}") for i in range(2)]
        upp = [bank(f"up{i}") for i in range(2)]
        dd = [bank(f"dd{i}") for i in range(2)]
        w_loaded, h_ready, h_used, h_kept, xs_ready, hT_done = (
            sem("w_loaded"), sem("h_ready"), sem("h_used"), sem("h_kept"), sem("xs_ready"), sem("hT_done"))
        gu_ready, silu_ready, a_done, dd_ready, dd_done, x_done = (
            sem("gu_ready"), sem("silu_ready"), sem("a_done"), sem("dd_ready"), sem("dd_done"), sem("x_done"))
        block = st.enter_context(nc.Block())
        NGB = SEQ // G
        DDG = 1 + 2 * shared

        def sweep(engine, body):
            with engine.Fori(0, BATCH - 1) as b:
                body(b, False)
            body(BATCH - 1, True)

        @block.sync
        def _(sp):
            sp.dma_start(rw[:], A[f"rw{layer}T"].rearrange("(k p) n -> p k n", p=P)).then_inc(w_loaded, 16)
            if shared:
                for t, k in ((wg, "sgT"), (wu, "suT"), (wd, "sdT")):
                    sp.dma_start(t[:], A[k].rearrange("(k p) n -> p k n", p=P)).then_inc(w_loaded, 16)

        @block.gpsimd
        def _(pool):
            pool.sem_inc(h_kept, TPG)
            pool.sem_inc(x_done, 2)

            def keep(gi):
                for t in range(TPG):
                    T = gi * TPG + t
                    pool.wait_ge(h_ready, T + 1)
                    pool.tensor_copy(row(hall, T), h[:, t]).then_inc(h_kept, 1)
                    if not shared:
                        pool.wait_ge(gh_ready, T + 1)
                        pool.tensor_tensor(row(x, T), row(x, T), gh[:, t % 2], ALU.add).then_inc(x_done, 1)

            def add_shared(gi):
                for u in range(2):
                    pool.wait_ge(dd_done, gi * DDG + 1 + u + 1 + 2)
                    xx = x[:, bass.ds(gi * TPG + 2 * u, 2), :]
                    pool.tensor_tensor(xx, xx, gated[:, u], ALU.add).then_inc(x_done, 1)
            keep(0)

            def body(b, last):
                for g in range(NGB):
                    gi = b * NGB + g
                    if not (last and g == NGB - 1):
                        keep(gi + 1)
                    if shared:
                        add_shared(gi)
            sweep(pool, body)

        @block.tensor
        def _(pe):
            pe.sem_inc(h_used, TPG)
            pe.wait_ge(w_loaded, 16 * (1 + 3 * shared))

            def transposes(gi):
                pe.wait_ge(hT_done, gi * KD + KD)
                for t in range(TPG):
                    pe.wait_ge(h_ready, gi * TPG + t + 1)
                    for j in range(KD):
                        i = pe.transpose(tp[j][:, t * P:(t + 1) * P], h[:, t, j * P:(j + 1) * P], ident[:, :])
                    i.then_inc(h_used, 1)
            transposes(0)

            def body(b, last):
                df = counter()

                def dd_bank():
                    i = df()
                    pe.wait_ge(dd_done, b * NGB * DDG + i)
                    return dd[(i - 1) % 2]
                for g in range(NGB):
                    gi = b * NGB + g
                    pe.wait_ge(hT_done, gi * KD + 2 * KD)
                    bk = dd_bank()
                    for t in range(TPG):
                        for k in range(KD):
                            i = pe.matmul(bk[:, t * E:(t + 1) * E], hT[:, k, t * P:(t + 1) * P], rw[:, k, :],
                                          start=k == 0, stop=k == KD - 1)
                    i.then_inc(dd_ready, 1)
                    if shared:
                        for f in range(FK):
                            pe.wait_ge(a_done, gi * FK + f + 1)
                            for wt, bkk in ((wg, gp), (wu, upp)):
                                for k in range(KD):
                                    i = pe.matmul(bkk[f % 2][:, :], wt[:, k, f * P:(f + 1) * P], hT[:, k, :],
                                                  start=k == 0, stop=k == KD - 1)
                            i.then_inc(gu_ready, 1)
                    if not (last and g == NGB - 1):
                        transposes(gi + 1)
                    if shared:
                        pe.wait_ge(a_done, (gi + 1) * FK + 2)
                        for u in range(2):
                            bk = dd_bank()
                            for t in range(2):
                                for k in range(FK):
                                    c = (2 * u + t) * P
                                    i = pe.matmul(bk[:, t * D:(t + 1) * D], aT[:, k, c:c + P], wd[:, k, :],
                                                  start=k == 0, stop=k == FK - 1)
                            i.then_inc(dd_ready, 1)
            sweep(pe, body)

        @block.scalar
        def _(act):
            act.sem_inc(hT_done, KD)

            def copy_hT(gi):
                act.wait_ge(h_used, (gi + 1) * TPG + TPG)
                for j in range(KD):
                    act.activation(hT[:, j, :], tp[j][:, :], ACT.Copy).then_inc(hT_done, 1)
            copy_hT(0)

            def body(b, last):
                for g in range(NGB):
                    gi = b * NGB + g
                    if shared:
                        for f in range(FK):
                            act.wait_ge(gu_ready, gi * FK + f + 1)
                            act.activation(silu[:, f % 2], gp[f % 2][:, :], ACT.Silu).then_inc(silu_ready, 1)
                    if not (last and g == NGB - 1):
                        copy_hT(gi + 1)
            sweep(act, body)

        @block.vector
        def _(dve):
            dve.sem_inc(a_done, 2)
            dve.sem_inc(dd_done, 2)
            if not shared:
                dve.sem_inc(a_done, 1)

            def make_h(gi, batch):
                for t in range(TPG):
                    T = gi * TPG + t
                    dve.wait_ge(h_used, T + 1)
                    dve.wait_ge(h_kept, T + 1)
                    modulate(dve, env, T, h[:, t], xs[:, t % 2], batch, SHIFT_B, SCALE_B, xs_ready, T + 1
                             ).then_inc(h_ready, 1)
                    if not shared:
                        dve.wait_ge(h_ready, T + 1)
                        dve.wait_ge(x_done, T + 1)
                        dve.tensor_tensor(gh[:, t % 2], h[:, t],
                                          modb[:, bass.ds(batch, 1), GATE_B, :].rearrange("p o n -> p (o n)"),
                                          ALU.mult).then_inc(gh_ready, 1)
            make_h(0, 0)

            def body(b, last):
                df = counter()
                for g in range(NGB):
                    gi = b * NGB + g
                    if not (last and g == NGB - 1):
                        make_h(gi + 1, b + (g + 1) // NGB)
                    n = df()
                    dve.wait_ge(dd_ready, b * NGB * DDG + n)
                    dve.tensor_copy(logits[:, bass.ds(gi * TPG, TPG), :],
                                    dd[(n - 1) % 2][:, 0:TPG * E].rearrange("p (t e) -> p t e", e=E)).then_inc(dd_done, 1)
                    if not shared:
                        continue
                    for f in range(FK):
                        dve.wait_ge(silu_ready, gi * FK + f + 1)
                        dve.tensor_tensor(aT[:, f, :], upp[f % 2][:, :], silu[:, f % 2], ALU.mult).then_inc(a_done, 1)
                    for u in range(2):
                        n = df()
                        dve.wait_ge(dd_ready, b * NGB * DDG + n)
                        dve.wait_ge(x_done, gi * 2 + u + 1)
                        dve.tensor_tensor(gated[:, u], dd[(n - 1) % 2][:, :].rearrange("p (t d) -> p t d", d=D),
                                          modb[:, bass.ds(b, 1), GATE_B, :].to_broadcast([P, 2, D]), ALU.mult
                                          ).then_inc(dd_done, 1)
            sweep(dve, body)


def routing(nc, A, env, layer):
    with ExitStack() as st:
        sb = lambda n, s, dt=F32: st.enter_context(nc.sbuf_tensor(f"rt{layer}_" + n, s, dt))
        sem = lambda n: st.enter_context(nc.semaphore(f"rt{layer}_" + n))
        before, ones, hall, logits = (env[k] for k in ("before", "ones", "hall", "logits"))
        weight, put, get, experts = (env[k] for k in ("weight", "put", "get", "experts"))
        bias = sb("bias", [P, E])
        prob, work, m1, m2, both, rank = (sb(k, [P, NT, E]) for k in ("prob", "work", "m1", "m2", "both", "rank"))
        best = sb("best", [P, 2, NT])
        pick = sb("pick", [P, NT])
        order = sb("order", [P, E])
        run = sb("run", [P, NT, E])
        need = sb("need", [P, E])
        upto = sb("upto", [P, E])
        base = sb("base", [P, E])
        slot = sb("slot", [P, NT])
        slot2 = sb("slot2", [P, NT])
        block_id = sb("block_id", [P, NB0 + 1])
        fits = sb("fits", [P, NB0 + 1, E])
        ps = [st.enter_context(nc.psum_tensor(f"rt{layer}_ps{i}", [P, 512], F32)) for i in range(2)]
        step, bias_loaded, exp_in, exp_done, both_ready, ranks_ready, const_ready, routed, sent = (
            sem("step"), sem("bias_loaded"), sem("exp_in"), sem("exp_done"), sem("both_ready"), sem("ranks_ready"),
            sem("const_ready"), sem("routed"), sem("sent"))
        block = st.enter_context(nc.Block())

        def over_e(ap):
            return ap.unsqueeze(2).to_broadcast([P, NT, E])

        def over_t(ap):
            return ap.unsqueeze(1).to_broadcast([P, NT, E])

        @block.sync
        def _(sp):
            if layer == 0:
                sp.dma_start(bias[:, :], A["L0_ffn_routing_bias"].rearrange("(o e) -> o e", o=1).to_broadcast([P, E])
                             ).then_inc(bias_loaded, 16)

        @block.gpsimd
        def _(pool):
            pool.iota(order[:, :], pattern=[[-1, E]], base=E, channel_multiplier=0,
                      allow_small_or_imprecise_dtypes=True).then_inc(const_ready, 1)
            pool.iota(block_id[:, :], pattern=[[1, NB0 + 1]], base=0, channel_multiplier=0,
                      allow_small_or_imprecise_dtypes=True).then_inc(const_ready, 1)
            pool.wait_ge(env["zeroed"], 16 * env["zero_dmas"])
            pool.wait_ge(routed, 1)
            slots = env[f"slots{layer}"].ap()
            for t in range(NT):
                for c in range(2):
                    pool.indirect_dma_start(slots, bass.IndirectOffsetOnAxis(ap=put[:, c, t:t + 1], axis=0),
                                            hall[:, t, :], None, bounds_check=slots.shape[0] - 1,
                                            oob_is_err=False).then_inc(sent, 16)
            pool.wait_ge(sent, 16 * 2 * NT)

        @block.scalar
        def _(act):
            act.wait_ge(exp_in, 1)
            act.activation(prob[:], work[:], ACT.Exp, scale=-1.0 if layer == 0 else 1.0).then_inc(exp_done, 1)

        @block.tensor
        def _(pe):
            pe.wait_ge(both_ready, 1)
            m = both[:].rearrange("p t e -> p (t e)")
            pe.matmul(ps[0][:, 0:NT * E], before[:, :], m, start=True, stop=True).then_inc(ranks_ready, 1)
            pe.matmul(ps[1][:, 0:NT * E], ones[:, :], m, start=True, stop=True).then_inc(ranks_ready, 1)

        @block.vector
        def _(dve):
            n = counter()
            if layer == 0:
                dve.wait_ge(bias_loaded, 16)
                dve.tensor_tensor(work[:], logits[:], over_t(bias[:, :]), ALU.add).then_inc(exp_in, 1)
                dve.wait_ge(exp_done, 1)
                dve.tensor_scalar(work[:], prob[:], 1.0, None, ALU.add).then_inc(step, 1)
                dve.wait_ge(step, n())
                dve.reciprocal(prob[:], work[:]).then_inc(step, 1)
                dve.wait_ge(step, n())
            else:
                dve.tensor_reduce(pick[:, :], logits[:], AXX, ALU.max).then_inc(step, 1)
                dve.wait_ge(step, n())
                dve.tensor_tensor(work[:], logits[:], over_e(pick[:, :]), ALU.subtract).then_inc(exp_in, 1)
                dve.wait_ge(exp_done, 1)
                dve.tensor_reduce(pick[:, :], prob[:], AXX, ALU.add).then_inc(step, 1)
                dve.wait_ge(step, n())
                dve.reciprocal(slot[:, :], pick[:, :]).then_inc(step, 1)
                dve.wait_ge(step, n())
                dve.tensor_tensor(prob[:], prob[:], over_e(slot[:, :]), ALU.mult).then_inc(step, 1)
                dve.wait_ge(step, n())
            dve.wait_ge(const_ready, 2)
            for c, m in enumerate((m1, m2)):
                dve.tensor_reduce(best[:, c], prob[:], AXX, ALU.max).then_inc(step, 1)
                dve.wait_ge(step, n())
                dve.tensor_tensor(work[:], prob[:], over_e(best[:, c]), ALU.is_equal).then_inc(step, 1)
                dve.wait_ge(step, n())
                dve.tensor_tensor(work[:], work[:], over_t(order[:, :]), ALU.mult).then_inc(step, 1)
                dve.wait_ge(step, n())
                dve.tensor_reduce(pick[:, :], work[:], AXX, ALU.max).then_inc(step, 1)
                dve.wait_ge(step, n())
                dve.tensor_tensor(m[:], work[:], over_e(pick[:, :]), ALU.is_equal).then_inc(step, 1)
                dve.wait_ge(step, n())
                if c == 0:
                    dve.scalar_tensor_tensor(out=prob[:].rearrange("p t e -> p (t e)"),
                                             in0=m[:].rearrange("p t e -> p (t e)"), scalar=-4.0,
                                             in1=prob[:].rearrange("p t e -> p (t e)"),
                                             op0=ALU.mult, op1=ALU.add).then_inc(step, 1)
                    dve.wait_ge(step, n())
            dve.tensor_tensor(both[:], m1[:], m2[:], ALU.add).then_inc(both_ready, 1)
            dve.tensor_tensor(pick[:, :], best[:, 0], best[:, 1], ALU.add).then_inc(step, 1)
            dve.wait_ge(step, n())
            dve.reciprocal(slot[:, :], pick[:, :]).then_inc(step, 1)
            dve.wait_ge(step, n())
            for c in range(2):
                dve.tensor_tensor(weight[:, c], best[:, c], slot[:, :], ALU.mult).then_inc(step, 1)
            dve.wait_ge(step, n(2))
            dve.wait_ge(ranks_ready, 2)
            total = ps[1][:, 0:NT * E].rearrange("p (t e) -> p t e", e=E)
            for e in range(E):
                dve.tensor_tensor_scan(run[:, :, e], ones[:, 0:NT], total[:, :, e], 0.0, ALU.mult, ALU.add
                                       ).then_inc(step, 1)
            dve.wait_ge(step, n(E))
            dve.tensor_tensor(rank[:], run[:], total, ALU.subtract).then_inc(step, 1)
            dve.wait_ge(step, n())
            dve.tensor_tensor(rank[:], rank[:], ps[0][:, 0:NT * E].rearrange("p (t e) -> p t e", e=E), ALU.add
                              ).then_inc(step, 1)
            dve.wait_ge(step, n())
            if layer == 0:
                dve.tensor_scalar(need[:, :], run[:, NT - 1, :], 1.0 / BLK0,
                                  (BLK0 - 1) / BLK0 - 0.5 + 0.5 / BLK0, ALU.mult, ALU.add).then_inc(step, 1)
                dve.wait_ge(step, n())
                dve.tensor_scalar(need[:, :], need[:, :], ROUND, ROUND, ALU.add, ALU.subtract).then_inc(step, 1)
                dve.wait_ge(step, n())
                dve.tensor_tensor_scan(upto[:, :], ones[:, 0:E], need[:, :], 0.0, ALU.mult, ALU.add).then_inc(step, 1)
                dve.wait_ge(step, n())
                dve.tensor_tensor(base[:, :], upto[:, :], need[:, :], ALU.subtract).then_inc(step, 1)
                nb = NB0 + 1
                dve.tensor_tensor(fits[:], upto[:, :].unsqueeze(1).to_broadcast([P, nb, E]),
                                  block_id[:, :].unsqueeze(2).to_broadcast([P, nb, E]), ALU.is_le).then_inc(step, 1)
                dve.wait_ge(step, n(2))
                dve.tensor_scalar(base[:, :], base[:, :], float(BLK0), None, ALU.mult).then_inc(step, 1)
                dve.tensor_reduce(block_id[:, :], fits[:], AXX, ALU.add).then_inc(step, 1)
                dve.wait_ge(step, n(2))
                dve.tensor_scalar(experts[0:1, :], block_id[0:1, :], float(E - 1), None, ALU.min).then_inc(step, 1)
                n()
            else:
                dve.tensor_scalar(base[:, :], order[:, :], -float(SLOTS1), float(E * SLOTS1), ALU.mult, ALU.add
                                  ).then_inc(step, 1)
                dve.wait_ge(step, n())
            dve.tensor_tensor(work[:], rank[:], over_t(base[:, :]), ALU.add).then_inc(step, 1)
            dve.wait_ge(step, n())
            for c, m in enumerate((m1, m2)):
                dve.tensor_tensor(prob[:], m[:], work[:], ALU.mult).then_inc(step, 1)
                dve.wait_ge(step, n())
                dve.tensor_reduce(slot[:, :], prob[:], AXX, ALU.add).then_inc(step, 1)
                dve.wait_ge(step, n())
                if layer == 1:
                    dve.tensor_tensor(prob[:], m[:], rank[:], ALU.mult).then_inc(step, 1)
                    dve.wait_ge(step, n())
                    dve.tensor_reduce(pick[:, :], prob[:], AXX, ALU.add).then_inc(step, 1)
                    dve.wait_ge(step, n())
                    dve.tensor_scalar(pick[:, :], pick[:, :], float(CAP), None, ALU.is_lt).then_inc(step, 1)
                    dve.wait_ge(step, n())
                    dve.tensor_tensor(weight[:, c], weight[:, c], pick[:, :], ALU.mult).then_inc(step, 1)
                    dve.tensor_tensor(slot[:, :], slot[:, :], pick[:, :], ALU.mult).then_inc(step, 1)
                    dve.wait_ge(step, n(2))
                    dve.tensor_scalar(slot2[:, :], pick[:, :], -float(DROP), float(DROP), ALU.mult, ALU.add
                                      ).then_inc(step, 1)
                    dve.tensor_copy(get[:, c], slot[:, :]).then_inc(step, 1)
                    dve.wait_ge(step, n(2))
                    dve.tensor_tensor(put[:, c], slot[:, :], slot2[:, :], ALU.add).then_inc(step, 1)
                    dve.wait_ge(step, n())
                else:
                    dve.tensor_copy(get[:, c], slot[:, :]).then_inc(step, 1)
                    dve.tensor_copy(put[:, c], slot[:, :]).then_inc(step, 1)
                    dve.wait_ge(step, n(2))
            dve.sem_inc(routed, 1)


def expert_blocks(nc, A, env, layer):
    with ExitStack() as st:
        sb = lambda n, s, dt=F32: st.enter_context(nc.sbuf_tensor(f"ex{layer}_" + n, s, dt))
        sem = lambda n: st.enter_context(nc.semaphore(f"ex{layer}_" + n))
        bank = lambda n: st.enter_context(nc.psum_tensor(f"ex{layer}_" + n, [P, 512], F32))
        ident, experts = env["ident"], env["experts"]
        gated = layer == 0
        FF = FF0 if gated else FF1
        FK = FF // P
        R = P if gated else RT1
        BLK = TPG * R
        NBLK = NB0 if gated else E * NB1
        SAME = 1 if gated else NB1
        NSETS = NBLK // SAME
        AHEAD = 2 if gated else 1
        BODY = 2 * SAME
        LOOPS = (NBLK - AHEAD * SAME) // BODY
        WIN = (1 + gated) * KD * FF
        WOUT = FK * D
        NA = 2 if gated else 4
        SPLIT = 0 if gated else 1
        staging = [sb(f"staging{i}", [P, WIN + WOUT]) for i in range(AHEAD)]
        w_part = [sb(f"w{i}", [P, 2, WIN + WOUT], F32R) for i in range(2)]
        rows = sb("rows", [P, 2, TPG, D])
        hT = sb("hT", [P, 2, KD, BLK], F32R)
        silu = sb("silu", [P, 2, BLK])
        a = sb("a", [P, NA, BLK])
        aT = sb("aT", [P, 2, FK, BLK], F32R)
        ysb = sb("ysb", [P, 2, TPG, D])
        tp = [bank(f"tp{i}") for i in range(KD)]
        gp = [bank(f"gp{i}") for i in range(NA)]
        upp = [bank(f"up{i}") for i in range(NA)] if gated else None
        dd = [bank(f"dd{i}") for i in range(2)]
        w_loaded = [sem(f"w_loaded{i}") for i in range(AHEAD)]
        w_hi, w_ready = sem("w_hi"), sem("w_ready")
        rows_loaded = [sem(f"rows_loaded{i}") for i in range(2)]
        y_stored = [sem(f"y_stored{i}") for i in range(2)]
        rows_used, hT_hi, hT_done, gu_ready, silu_ready, a_ready, a_hi, a_done, dd_ready, dd_done = (
            sem(k) for k in ("rows_used", "hT_hi", "hT_done", "gu_ready", "silu_ready", "a_ready", "a_hi", "a_done",
                             "dd_ready", "dd_done"))
        block = st.enter_context(nc.Block())
        src = env[f"slots{layer}"].ap()
        dst = env[f"y{layer}"].ap()
        n_w = 3 if gated else 2
        FREE = 4 * SAME
        PIECES = (slice(0, WIN), slice(WIN, WIN + WOUT))
        PASSES = ((0, 0), (0, 1), (1, 0))

        def sweep(engine, body):
            with engine.Fori(0, LOOPS) as i:
                for s in range(BODY):
                    body(i * BODY + s, i, s)
            for s in range(NBLK - LOOPS * BODY):
                body(LOOPS * BODY + s, LOOPS + s // BODY, s % BODY)

        def last(i, s):
            return isinstance(i, int) and i * BODY + s == NBLK - 1

        def next_set(i, s, k=1):
            v = i * 2 + s // SAME + k
            return None if isinstance(v, int) and v >= NSETS else v

        @block.sync
        def _(sp):
            def load_weights(v, buf):
                sp.wait_ge(w_ready, v + 1)
                if gated:
                    e = sp.value_load(experts[0:1, bass.ds(v, 1)], min_val=0, max_val=E - 1)
                    names = (("L0_ffn_gate_w", 0, KD * FF), ("L0_ffn_up_w", KD * FF, WIN), ("L0_ffn_down_w", WIN, WIN + WOUT))
                else:
                    e = v
                    names = (("L1_ffn_w1", 0, WIN), ("L1_ffn_w2", WIN, WIN + WOUT))
                for name, lo, hi in names:
                    sp.dma_start(staging[buf][:, lo:hi].rearrange("p (k n) -> p k n", n=D if lo == WIN else FF),
                                 A[name][bass.ds(e, 1)].rearrange("o (k p) n -> p (o k) n", p=P)
                                 ).then_inc(w_loaded[buf], 16)

            def load_rows(n, s):
                sp.wait_ge(rows_used, n + 1)
                sp.dma_start(rows[0:R, s % 2], src[bass.ds(n * BLK, BLK), :].rearrange("(t p) d -> p t d", p=R)
                             ).then_inc(rows_loaded[s % 2], 16)
            load_weights(0, 0)
            load_rows(0, 0)
            if AHEAD == 2:
                load_weights(1, 1)

            def body(n, i, s):
                if not last(i, s):
                    load_rows(n + 1, s + 1)
                v = next_set(i, s, AHEAD)
                if s % SAME == 0 and v is not None:
                    load_weights(v, (s // SAME) % AHEAD)
                sp.wait_ge(dd_done, 2 * n + 2 + 2)
                sp.dma_start(dst[bass.ds(n * BLK, BLK), :].rearrange("(t p) d -> p t d", p=R), ysb[0:R, s % 2]
                             ).then_inc(y_stored[s % 2], 16)
            sweep(sp, body)
            sp.wait_ge(y_stored[0], 16 * (-(-NBLK // 2)) + 16)
            sp.wait_ge(y_stored[1], 16 * (NBLK // 2) + 16)

        @block.gpsimd
        def _(pool):
            pool.sem_inc(w_ready, AHEAD)

            def split(v, par):
                for q, c in enumerate(PIECES):
                    pool.wait_ge(w_hi, 2 * v + q + 1)
                    i = pool.tensor_tensor(w_part[par][:, 1, c], staging[par % AHEAD][:, c],
                                           w_part[par][:, 0, c].bitcast(F32), ALU.subtract)
                i.then_inc(w_ready, 1)
            split(0, 0)

            def body(n, i, s):
                v = next_set(i, s)
                if s % SAME == SPLIT and v is not None:
                    split(v, (s // SAME + 1) % 2)
            sweep(pool, body)

        @block.tensor
        def _(pe):
            pe.sem_inc(dd_ready, FREE)
            pe.sem_inc(rows_used, 2)

            def w_in(par, part, m, k, f):
                c = (m * KD + k) * FF + f * P
                return w_part[par][:, part, c:c + P]

            def w_out(par, part, k):
                return w_part[par][:, part, WIN + k * D:WIN + (k + 1) * D]

            def transposes(n, i, s):
                pe.wait_ge(hT_done, n * KD + KD)
                pe.wait_ge(rows_loaded[s % 2], 16 * (i * (BODY // 2) + s // 2 + 1))
                for t in range(TPG):
                    for j in range(KD):
                        m = pe.transpose(tp[j][:, t * R:(t + 1) * R], rows[0:R, s % 2, t, j * P:(j + 1) * P],
                                         ident[0:R, 0:R])
                m.then_inc(rows_used, 1)
            transposes(0, 0, 0)

            def body(n, i, s):
                par = s // SAME % 2
                if s % SAME == 0:
                    pe.wait_ge(w_ready, i * 2 + s // SAME + 1 + AHEAD)
                pe.wait_ge(hT_done, n * KD + 2 * KD)
                for f in range(FK):
                    pe.wait_ge(a_ready, n * FK + f + 1)
                    for m in range(1 + gated):
                        for k in range(KD):
                            for q, (pw, ph) in enumerate(PASSES):
                                mm = pe.matmul((gp, upp)[m][f % NA][:, 0:BLK], w_in(par, pw, m, k, f), hT[:, ph, k, :],
                                               start=k == 0 and q == 0, stop=k == KD - 1 and q == 2)
                    mm.then_inc(gu_ready, 1)
                if not last(i, s):
                    transposes(n + 1, *((i, s + 1) if s + 1 < BODY else (i + 1, 0)))
                for u in range(2):
                    pe.wait_ge(dd_done, 2 * n + u + 1)
                    for t in range(2):
                        for k in range(FK):
                            c = (2 * u + t) * R
                            if c == 0:
                                pe.wait_ge(a_done, n * FK + k + 1)
                            for q, (pa, pw) in enumerate(PASSES):
                                mm = pe.matmul(dd[u][0:R, t * D:(t + 1) * D], aT[:, pa, k, c:c + R], w_out(par, pw, k),
                                               start=k == 0 and q == 0, stop=k == FK - 1 and q == 2)
                    if u == 0:
                        mm.then_inc(dd_ready, 1)
                mm.then_inc(dd_ready, 1)
            sweep(pe, body)

        @block.scalar
        def _(act):
            if not gated:
                act.sem_inc(a_ready, NA)

            def copy_hT(n):
                act.wait_ge(rows_used, n + 1 + 2)
                for j in range(KD):
                    act.activation(hT[:, 0, j, :], tp[j][:, 0:BLK], ACT.Copy).then_inc(hT_hi, 1)

            def round_weights(q, v, buf, par, v_buf):
                act.wait_ge(w_loaded[buf], 16 * n_w * (v_buf + 1))
                act.wait_ge(dd_ready, 2 * SAME * (v - 1) + FREE)
                act.activation(w_part[par][:, 0, PIECES[q]], staging[buf][:, PIECES[q]], ACT.Copy).then_inc(w_hi, 1)
            for q in range(2):
                round_weights(q, 0, 0, 0, 0)
            copy_hT(0)

            def body(n, i, s):
                def round_a(f):
                    act.wait_ge(a_ready, n * FK + f + 1 + NA)
                    act.activation(aT[:, 0, f, :], a[:, f % NA], ACT.Copy).then_inc(a_hi, 1)
                v = next_set(i, s)
                for f in range(FK):
                    act.wait_ge(gu_ready, n * FK + f + 1)
                    if gated:
                        act.activation(silu[:, f % 2], gp[f % NA][:, 0:BLK], ACT.Silu).then_inc(silu_ready, 1)
                    else:
                        if f >= NA:
                            act.wait_ge(a_done, n * FK + f - NA + 1)
                        act.activation(a[:, f % NA], gp[f % NA][:, 0:BLK], ACT.Silu).then_inc(a_ready, 1)
                    if f > 0:
                        round_a(f - 1)
                    if s % SAME == SPLIT and f < 2 and v is not None:
                        t = s // SAME + 1
                        round_weights(f, v, t % AHEAD, t % 2, v if AHEAD == 1 else i + t // 2)
                round_a(FK - 1)
                if not last(i, s):
                    copy_hT(n + 1)
            sweep(act, body)

        @block.vector
        def _(dve):
            if gated:
                dve.sem_inc(a_ready, NA)
            dve.sem_inc(hT_done, KD)
            dve.sem_inc(dd_done, 2)
            for i in range(2):
                dve.sem_inc(y_stored[i], 16)

            def rest_of_hT(n):
                for j in range(KD):
                    dve.wait_ge(hT_hi, n * KD + j + 1)
                    dve.tensor_tensor(hT[:, 1, j, :], tp[j][:, 0:BLK], hT[:, 0, j, :].bitcast(F32), ALU.subtract
                                      ).then_inc(hT_done, 1)
            rest_of_hT(0)

            def body(n, i, s):
                def rest_of_a(f):
                    dve.wait_ge(a_hi, n * FK + f + 1)
                    dve.tensor_tensor(aT[:, 1, f, :], a[:, f % NA], aT[:, 0, f, :].bitcast(F32), ALU.subtract
                                      ).then_inc(a_done, 1)
                for f in range(FK):
                    if gated:
                        dve.wait_ge(silu_ready, n * FK + f + 1)
                        if f >= NA:
                            dve.wait_ge(a_done, n * FK + f - NA + 1)
                        dve.tensor_tensor(a[:, f % NA], upp[f % NA][:, 0:BLK], silu[:, f % 2], ALU.mult).then_inc(a_ready, 1)
                        if f > 0:
                            rest_of_a(f - 1)
                    else:
                        rest_of_a(f)
                if gated:
                    rest_of_a(FK - 1)
                if not last(i, s):
                    rest_of_hT(n + 1)
                dve.wait_ge(y_stored[s % 2], 16 * (i * (BODY // 2) + s // 2) + 16)
                for u in range(2):
                    dve.wait_ge(dd_ready, 2 * n + u + 1 + FREE)
                    dve.tensor_copy(ysb[0:R, s % 2, 2 * u:2 * u + 2, :],
                                    dd[u][0:R, :].rearrange("p (t d) -> p t d", d=D)).then_inc(dd_done, 1)
            sweep(dve, body)


def combine(nc, A, env, layer, out=None):
    with ExitStack() as st:
        sb = lambda n, s, dt=F32: st.enter_context(nc.sbuf_tensor(f"cb{layer}_" + n, s, dt))
        sem = lambda n: st.enter_context(nc.semaphore(f"cb{layer}_" + n))
        x, modb, weight, get = (env[k] for k in ("x", "modb", "weight", "get"))
        NBUF = 4
        y = sb("y", [P, NBUF, 2, D])
        s1 = sb("s1", [P, NBUF, D])
        fetched = [sem(f"fetched{i}") for i in range(NBUF)]
        y_used, step = sem("y_used"), sem("step")
        block = st.enter_context(nc.Block())

        @block.gpsimd
        def _(pool):
            for t in range(NT):
                if t >= NBUF:
                    pool.wait_ge(y_used, t - NBUF + 1)
                for c in range(2):
                    pool.indirect_dma_start(y[:, t % NBUF, c, :], None, env[f"y{layer}"].ap(),
                                            bass.IndirectOffsetOnAxis(ap=get[:, c, t:t + 1], axis=0)
                                            ).then_inc(fetched[t % NBUF], 16)

        @block.vector
        def _(dve):
            for t in range(NT):
                i = t % NBUF
                dve.wait_ge(fetched[i], 32 * (t // NBUF + 1))
                dve.tensor_scalar(s1[:, i], y[:, i, 0], weight[:, 0, t:t + 1], None, ALU.mult).then_inc(step, 1)
                dve.wait_ge(step, 3 * t + 1)
                dve.scalar_tensor_tensor(out=s1[:, i], in0=y[:, i, 1], scalar=weight[:, 1, t:t + 1], in1=s1[:, i],
                                         op0=ALU.mult, op1=ALU.add).then_inc(y_used, 1)
                dve.wait_ge(y_used, t + 1)
                dve.tensor_tensor(s1[:, i], s1[:, i], modb[:, t // TPB, GATE_B, :], ALU.mult).then_inc(step, 1)
                dve.wait_ge(step, 3 * t + 2)
                dve.tensor_tensor(x[:, t], x[:, t], s1[:, i], ALU.add).then_inc(step, 1)


def store_x(nc, env, out):
    with ExitStack() as st:
        stored = st.enter_context(nc.semaphore("stored"))
        block = st.enter_context(nc.Block())

        @block.sync
        def _(sp):
            sp.dma_start(out.rearrange("b (t p) d -> p (b t) d", p=P), env["x"][:]).then_inc(stored, 16)
            sp.wait_ge(stored, 16)
            sp.wait_ge(env["zeroed"], 16 * env["zero_dmas"])


_PLAIN = ["L0_attn_x", "L0_wmod", "L1_wmod", "L0_ffn_gate_w", "L0_ffn_up_w", "L0_ffn_down_w", "L0_ffn_routing_bias",
          "L1_ffn_w1", "L1_ffn_w2"]
_TRANSPOSED = {"ct0": "L0_c", "ct1": "L1_c", "wqT": "L0_attn_wq", "wkT": "L0_attn_wk", "wvT": "L0_attn_wv",
               "woT": "L0_attn_wo", "rfT": "L0_attn_rf", "sgT": "L0_ffn_shared_gate", "suT": "L0_ffn_shared_up",
               "sdT": "L0_ffn_shared_down", "rw0T": "L0_ffn_router_w", "rw1T": "L1_ffn_router_w"}
_COLUMNS = ["L1_attn_phazor_real", "L1_attn_phazor_imag", "L1_attn_phazor_init_real", "L1_attn_phazor_init_imag",
            "L1_attn_last_conv_real", "L1_attn_last_conv_imag"]


def layout(inputs):
    a = {k: np.ascontiguousarray(inputs[k]) for k in _PLAIN}
    a |= {k: np.ascontiguousarray(np.asarray(inputs[v]).T) for k, v in _TRANSPOSED.items()}
    a["phasor"] = np.ascontiguousarray(
        np.stack([np.asarray(inputs[k]) for k in _COLUMNS]).reshape(6, KD, P).transpose(2, 0, 1))
    return a


def kernel(**inputs):
    import concourse.bacc as _bacc
    from concourse.bass_utils import run_bass_kernel_spmd as _run

    nc = _bacc.Bacc("TRN2", target_bir_lowering=False, num_devices=1)
    arrays = layout(inputs)
    A = {k: nc.dram_tensor(k, v.shape, mybir.dt.from_np(v.dtype), kind="ExternalInput").ap() for k, v in arrays.items()}
    out = nc.dram_tensor("out", (BATCH, SEQ, D), F32, kind="ExternalOutput").ap()
    build_program(nc, A, out)
    return _run(nc, [arrays], core_ids=[0]).results[0]["out"]
```

```python
import math
from contextlib import ExitStack

import numpy as np

import concourse.bass as bass
from concourse import mybir

F32 = mybir.dt.float32
F32R = mybir.dt.float32r
I32 = mybir.dt.int32
U32 = mybir.dt.uint32
ACT = mybir.ActivationFunctionType
ALU = mybir.AluOpType
AXX = mybir.AxisListType.X

P = 128
BATCH, SEQ, D = 4, 1024, 256
TOK = BATCH * SEQ
NT = TOK // P
TPB = SEQ // P
KD = D // P
G = 512
TPG = G // P
NG = TOK // G
HEADS, DH, FEAT = 16, 16, 64
HPK = P // DH
PAIRS = HEADS // 2
VA = DH + 2
EPS = 1e-5
QN_MAX = 165.0
ROUND = 1.5 * 2.0 ** 23
E = 8
FF0, FF1 = 512, 1024
BLK0 = 512
NB0 = (2 * TOK + E * (BLK0 - 1)) // BLK0
STRIDE0 = TOK + BLK0
SPARE0 = NB0 - 2 * TOK // BLK0
ROUTE_STEPS = (37, 59)
CAP = int(1.25 * TOK * 2 / E) + 1
BLK1, RT1 = 432, 108
NB1 = -(-CAP // BLK1)
SLOTS1 = NB1 * BLK1
STATS_STEPS = 19
RING = 6
SET0_LOADED = (48, 48 + 32)
CHUNK = 48
CHUNKS = -(-SEQ // CHUNK)
PHASOR_STEPS = 62
POWER_STEPS = 140
CHUNK_STEPS = 4 * KD
ZERO = 512
DROP = 1 << 20
SHIFT_A, SCALE_A, GATE_A, SHIFT_B, SCALE_B, GATE_B = range(6)


def counter(n=0):

    def more(k=1):
        nonlocal n
        n += k
        return n
    return more


def one(ap):
    return ap.rearrange("p o n -> p (o n)")


def row(ap, i):
    return one(ap[:, bass.ds(i, 1), :])


def build_program(nc, A, out):
    ctx = ExitStack()
    with ctx:
        def sb(name, shape, dt=F32, stack=ctx):
            return stack.enter_context(nc.sbuf_tensor(name, shape, dt))

        def sem(name):
            return ctx.enter_context(nc.semaphore(name))

        S = {}
        x = sb("x", [P, NT, D])
        ident = sb("ident", [P, P])
        before = sb("before", [P, P])
        ones = sb("ones", [P, P])
        half_pi = sb("half_pi", [P, 1])
        zero = sb("zero", [P, ZERO])
        modb = sb("modb", [P, BATCH, 6, D])
        stats = sb("stats", [P, NT, 6])
        mean = sb("mean", [P, NT])
        rstd = sb("rstd", [P, NT])
        ntmp = sb("ntmp", [P, 3, NT])
        seed = sb("seed", [P, NT], I32)
        par = sb("par", [P, 6, KD])
        rho = sb("rho", [P, KD])
        mod_col = sb("mod_col", [P, 6, KD, BATCH])
        first = sb("first", [P, 2, KD])
        step_c = sb("step_c", [P, 2, KD])
        tmp = sb("tmp", [P, 8, KD])
        tmp_i = sb("tmp_i", [P, KD], I32)
        mod_rows = [nc.dram_tensor(f"mod_rows{l}", (BATCH, 6 * D), F32) for l in range(2)]
        slots0 = nc.dram_tensor("slots0", (E * STRIDE0 + SPARE0 * BLK0, D), F32)
        slots1 = nc.dram_tensor("slots1", (E * SLOTS1, D), F32)
        y0 = nc.dram_tensor("y0", (NB0 * BLK0, D), F32)
        y1 = nc.dram_tensor("y1", (E * SLOTS1, D), F32)
        zeroed = sem("zeroed")
        par_loaded, tab = sem("par_loaded"), sem("tab")
        set0_loaded, set0_hi = sem("set0_loaded"), sem("set0_hi")
        stats_done, rstd_step = sem("stats_done"), sem("rstd_step")
        mod_loaded = sem("mod_loaded")
        env = dict(locals())
        setup(nc, A, env)
        attention(nc, A, env)
        layer_stats(nc, env, 1, [BATCH - 1])
        experts_of(nc, A, env, 0)
        layer_stats(nc, env, 3, [BATCH - 1])
        experts_of(nc, A, env, 1, out)


def experts_of(nc, A, env, layer, out=None):
    with ExitStack() as st:
        sb = lambda n, s, dt=F32: st.enter_context(nc.sbuf_tensor(f"{n}{layer}", s, dt))
        own = dict(env)
        own["weight"] = sb("weight", [P, 2, NT])
        own["put"] = sb("put", [P, 2, NT], U32)
        own["get"] = sb("get", [P, 2, NT], U32)
        if layer == 0:
            own["rot0"] = sb("rot0", [P, 2, KD, CHUNK])
            own["scratch"] = sb("scratch", [P, KD, 2, CHUNK])
            own["counts"] = sb("counts", [1, E], I32)
            own["experts"] = sb("experts", [1, NB0], I32)
            own["first_slot"] = sb("first_slot", [1, NB0], I32)
        width = 3 * KD * FF0 if layer == 0 else 2 * KD * FF1
        own["staging"] = [sb(f"staging{i}_", [P, width]) for i in range(2 - layer)]
        own["w_part"] = [sb(f"w_part{i}_", [P, 2, width], F32R) for i in (1, 2)[:1 + layer]]
        if layer == 1:
            own["ring"] = sb("ring", [P, RING, D])
            own["part"] = sb("part", [P, 2, D])
            own["fetched"] = [st.enter_context(nc.semaphore(f"fetched{i}")) for i in range(RING)]
            own["part_ready"], own["part_used"] = (st.enter_context(nc.semaphore(k)) for k in ("part_ready", "part_used"))
        dense_and_router(nc, A, own, layer)
        if layer == 0:
            own["rot"] = sb("rot", [P, 2, KD, CHUNKS * CHUNK])
        if layer == 0:
            own["w_part"] = [sb("w_part0_", [P, 2, width], F32R), own["w_part"][0]]
        expert_blocks(nc, A, own, layer)
        if layer == 0:
            own["coef"] = sb("coef", [P, 2, KD, SEQ])
            combine(nc, A, own)
            layer_stats(nc, own, 2, [])
            recurrence(nc, A, own)
        else:
            last_results(nc, own, out)


def setup(nc, A, env):
    with ExitStack() as st:
        sb = lambda n, s, dt=F32: st.enter_context(nc.sbuf_tensor(n, s, dt))
        sem = lambda n: st.enter_context(nc.semaphore(n))
        x, ident, before, ones, half_pi = (env[k] for k in ("x", "ident", "before", "ones", "half_pi"))
        ct = sb("ct", [P, 2, KD, BATCH])
        wmod = sb("wmod", [P, 2, KD, 6 * D])
        mods = sb("mods", [BATCH, 2, 6, D])
        sgn = sb("sgn", [BATCH, 2, D])
        zero = env["zero"]
        env["zero_dmas"] = 0
        ps = st.enter_context(nc.psum_tensor("mod_ps", [BATCH, 2, 3, 512], F32))
        loaded, silu_done, mod_ps_ready, copied = sem("loaded"), sem("silu_done"), sem("mod_ps_ready"), sem("copied")
        mod_step, mods_ready, rows_stored, const_step, x_loaded = (
            sem("mod_step"), sem("mods_ready"), sem("rows_stored"), sem("const_step"), sem("x_loaded"))
        turned = st.enter_context(nc.psum_tensor("mod_turned", [P, 512], F32))
        turned_ready = sem("turned_ready")
        block = st.enter_context(nc.Block())

        @block.sync
        def _(sp):
            sp.dma_start(env["par"][:], A["phasor"]).then_inc(env["par_loaded"], 16)
            for l in range(2):
                sp.dma_start(ct[:, l], A[f"ct{l}"].rearrange("(k p) b -> p k b", p=P)).then_inc(loaded, 16)
                sp.dma_start(wmod[:, l], A[f"L{l}_wmod"].rearrange("(k p) n -> p k n", p=P)).then_inc(loaded, 16)
            xin = A["L0_attn_x"].rearrange("b (t p) d -> p (b t) d", p=P)
            for q in range(4):
                sp.dma_start(x[:, 8 * q:8 * q + 8, :], xin[:, 8 * q:8 * q + 8, :]).then_inc(x_loaded, 16)
            sp.wait_ge(mods_ready, 1)
            for l in range(2):
                sp.dma_start(env["mod_rows"][l].ap(), mods[:, l].rearrange("b s d -> b (s d)")).then_inc(rows_stored, 16)
            sp.wait_ge(rows_stored, 32)
            sp.dma_start(env["modb"][:].rearrange("p b s d -> p (b s d)"),
                         env["mod_rows"][0].ap().rearrange("(o b) n -> o (b n)", o=1).to_broadcast([P, BATCH * 6 * D])
                         ).then_inc(env["mod_loaded"], 16)
            sp.wait_ge(x_loaded, 64)
            sp.wait_ge(env["mod_loaded"], 16)

        @block.gpsimd
        def _(pool):
            pool.memset(ident[:, :], 0.0).then_inc(const_step, 1)
            pool.memset(ones[:, :], 1.0).then_inc(const_step, 1)
            pool.wait_ge(const_step, 2)
            pool.affine_select(out=ident[:, :], in_=ident[:, :], compare_op=ALU.not_equal, fill=1.0,
                               base=0, pattern=[[-1, P]], channel_multiplier=1).then_inc(const_step, 1)
            pool.affine_select(out=before[:, :], in_=ones[:, :], compare_op=ALU.is_gt, fill=0.0,
                               base=0, pattern=[[1, P]], channel_multiplier=-1).then_inc(const_step, 1)
            pool.memset(half_pi[:, :], math.pi / 2).then_inc(const_step, 1)
            pool.wait_ge(const_step, 5)

        @block.scalar
        def _(act):
            act.wait_ge(loaded, 64)
            act.activation(ct[:], ct[:], ACT.Silu).then_inc(silu_done, 1)
            act.wait_ge(turned_ready, 1)
            act.activation(env["mod_col"][:].rearrange("p s k b -> p (s k b)"), turned[:, 0:6 * KD * BATCH], ACT.Copy)

        @block.tensor
        def _(pe):
            pe.wait_ge(silu_done, 1)
            for l in range(2):
                for n in range(3):
                    if l == 1:
                        pe.wait_ge(copied, n + 1)
                    for k in range(KD):
                        mm = pe.matmul(ps[:, 0, n], ct[:, l, k, :], wmod[:, l, k, 512 * n:512 * n + 512],
                                       start=k == 0, stop=k == KD - 1)
                    mm.then_inc(mod_ps_ready, 1)
            pe.wait_ge(const_step, 5)
            pe.wait_ge(mods_ready, 1)
            for i in range(6):
                for k in range(KD):
                    c = (i * KD + k) * BATCH
                    mm = pe.transpose(turned[:, c:c + BATCH], mods[:, 1, i, k * P:(k + 1) * P], ident[0:BATCH, 0:BATCH])
            mm.then_inc(turned_ready, 1)

        @block.vector
        def _(dve):
            dve.memset(zero[:, :], 0.0)
            phasor(dve, env)
            for l in range(2):
                for n in range(3):
                    dve.wait_ge(mod_ps_ready, 3 * l + n + 1)
                    dve.tensor_copy(mods[:, l, 2 * n:2 * n + 2, :],
                                    ps[:, 0, n].rearrange("b (s d) -> b s d", s=2)).then_inc(copied, 1)
            dve.wait_ge(copied, 6)
            n = counter()
            for l in range(2):
                for scale in (SCALE_A, SCALE_B):
                    dve.tensor_scalar(mods[:, l, scale], mods[:, l, scale], 1.0, None, ALU.add).then_inc(mod_step, 1)
                    n()
                for gate in (GATE_A, GATE_B):
                    g = mods[:, l, gate]
                    dve.tensor_scalar(sgn[:, 0], g, 0.0, 2.0, ALU.is_ge, ALU.mult).then_inc(mod_step, 1)
                    dve.wait_ge(mod_step, n())
                    dve.scalar_tensor_tensor(out=sgn[:, 1], in0=sgn[:, 0], scalar=-1.0, in1=g,
                                             op0=ALU.add, op1=ALU.mult).then_inc(mod_step, 1)
                    dve.wait_ge(mod_step, n())
                    dve.tensor_scalar(sgn[:, 1], sgn[:, 1], 0.25, None, ALU.max).then_inc(mod_step, 1)
                    dve.wait_ge(mod_step, n())
                    dve.scalar_tensor_tensor(out=g, in0=sgn[:, 0], scalar=-1.0, in1=sgn[:, 1],
                                             op0=ALU.add, op1=ALU.mult).then_inc(mod_step, 1)
                    dve.wait_ge(mod_step, n())
            dve.tensor_copy(sgn[:, 0, 0:1], mods[:, 0, 0, 0:1]).then_inc(mods_ready, 1)
            dve.wait_ge(x_loaded, 64)
            for b in range(BATCH):
                batch_stats(dve, env, b)
            mean_and_rstd(dve, env, 0)


def batch_stats(dve, env, b):
    for t in range(TPB):
        dve.bn_stats(row(env["stats"], b * TPB + t), row(env["x"], b * TPB + t)).then_inc(env["stats_done"], 1)


def mean_and_rstd(dve, env, at):
    stats, mean, rstd, ntmp, seed, rstd_step = (env[k] for k in ("stats", "mean", "rstd", "ntmp", "seed", "rstd_step"))
    dve.wait_ge(env["stats_done"], (at + 1) * NT)
    var, half, y, y2 = ntmp[:, 0], ntmp[:, 1], rstd[:, :], ntmp[:, 2]
    mean_e, m2_e, mean_o, m2_o = (stats[:, :, i] for i in (1, 2, 4, 5))
    n = counter(at * STATS_STEPS)
    dve.tensor_tensor(half, mean_e, mean_o, ALU.subtract).then_inc(rstd_step, 1)
    dve.tensor_tensor(var, m2_e, m2_o, ALU.add).then_inc(rstd_step, 1)
    dve.tensor_tensor(y2, mean_e, mean_o, ALU.add).then_inc(rstd_step, 1)
    dve.wait_ge(rstd_step, n(3))
    dve.tensor_tensor(half, half, half, ALU.mult).then_inc(rstd_step, 1)
    dve.tensor_scalar(mean[:, :], y2, 0.5, None, ALU.mult).then_inc(rstd_step, 1)
    dve.tensor_scalar(var, var, 1.0 / D, EPS, ALU.mult, ALU.add).then_inc(rstd_step, 1)
    dve.wait_ge(rstd_step, n(3))
    dve.scalar_tensor_tensor(out=var, in0=half, scalar=0.25, in1=var, op0=ALU.mult, op1=ALU.add).then_inc(rstd_step, 1)
    dve.wait_ge(rstd_step, n())
    inverse_sqrt(dve, var, half, y, y2, seed[:, :], rstd_step, n)
    assert n(0) == (at + 1) * STATS_STEPS


def layer_stats(nc, env, at, batches):
    with ExitStack() as st:
        block = st.enter_context(nc.Block())

        @block.sync
        def _(sp):
            if at == 2:
                sp.dma_start(env["modb"][:].rearrange("p b s d -> p (b s d)"),
                             env["mod_rows"][1].ap().rearrange("(o b) n -> o (b n)", o=1).to_broadcast([P, BATCH * 6 * D])
                             ).then_inc(env["mod_loaded"], 16)
                sp.wait_ge(env["mod_loaded"], 32)

        @block.vector
        def _(dve):
            for b in batches:
                batch_stats(dve, env, b)
            mean_and_rstd(dve, env, at)


def inverse_sqrt(dve, v, half, y, y2, seed, step, n):
    dve.tensor_scalar(seed, v.bitcast(I32), 1, None, ALU.logical_shift_right).then_inc(step, 1)
    dve.tensor_scalar(half, v, -0.5, None, ALU.mult).then_inc(step, 1)
    dve.wait_ge(step, n(2))
    dve.tensor_scalar(y.bitcast(I32), seed, -1.0, float(0x5F3759DF), ALU.mult, ALU.add).then_inc(step, 1)
    dve.wait_ge(step, n())
    for _ in range(3):
        dve.tensor_tensor(y2, y, y, ALU.mult).then_inc(step, 1)
        dve.wait_ge(step, n())
        dve.tensor_tensor(y2, y2, half, ALU.mult).then_inc(step, 1)
        dve.wait_ge(step, n())
        dve.scalar_tensor_tensor(out=y, in0=y2, scalar=1.5, in1=y, op0=ALU.add, op1=ALU.mult).then_inc(step, 1)
        dve.wait_ge(step, n())


def modulate(dve, env, T, dst, xs, batch, shift, scale, xs_ready, h_ready):
    x, mean, rstd, modb = env["x"], env["mean"], env["rstd"], env["modb"]

    def mod(i):
        return modb[:, bass.ds(batch, 1), i, :].rearrange("p o n -> p (o n)")
    for i in range(2):
        dve.wait_ge(h_ready, T + i + 1)
        dve.scalar_tensor_tensor(out=xs[:, i], in0=row(x, T + i), scalar=mean[:, bass.ds(T + i, 1)], in1=mod(scale),
                                 op0=ALU.subtract, op1=ALU.mult).then_inc(xs_ready, 1)
    for i in range(2):
        dve.wait_ge(xs_ready, T + i + 1)
        dve.scalar_tensor_tensor(out=dst[i], in0=xs[:, i], scalar=rstd[:, bass.ds(T + i, 1)], in1=mod(shift),
                                 op0=ALU.mult, op1=ALU.add).then_inc(h_ready, 1)


def attention(nc, A, env):
    with ExitStack() as st:
        sb = lambda n, s, dt=F32: st.enter_context(nc.sbuf_tensor("at_" + n, s, dt))
        sem = lambda n: st.enter_context(nc.semaphore("at_" + n))
        bank = lambda n: st.enter_context(nc.psum_tensor("at_" + n, [P, 512], F32))
        x, ident, modb, half_pi = (env[k] for k in ("x", "ident", "modb", "half_pi"))
        NGB = SEQ // G
        HP = PAIRS // KD
        w = {k: sb(k, [P, KD, D]) for k in ("wqT", "wkT", "wvT", "woT")}
        rf = sb("rf", [P, HPK * FEAT])
        headsel = sb("headsel", [P, HPK])
        headblk = sb("headblk", [P, HPK, DH])
        log_k = sb("log_k", [P, 1])
        log_q = sb("log_q", [P, 1])
        xs = sb("xs", [P, 2, D])
        h = sb("h", [P, TPG, D])
        hT = sb("hT", [P, KD, SEQ])
        qkT = sb("qkT", [P, 2, KD, SEQ])
        sq = sb("sq", [P, KD, SEQ])
        ks = sb("ks", [P, TPB, 2, HEADS])
        floor = sb("floor", [P, KD, SEQ])
        va = sb("va", [P, TPB, HEADS, DH])
        turn = sb("turn", [P, 2, 512])
        frac = sb("frac", [P, 2, 512])
        fabs = sb("fabs", [P, 2, 512])
        kf = sb("kf", [P, 2, 2, HEADS * FEAT])
        sums = sb("sums", [P, 2, 512])
        raw = sums
        kvT = sb("kvT", [P, KD, 2, HP, 2, DH])
        kzT = sb("kzT", [P, KD, 2, HP, 2, DH])
        qf = sb("qf", [P, 2, HP, 2, G])
        den = sb("den", [P, 2, G])
        oT = sb("oT", [P, KD, G])
        att = sb("att", [P, 2, 2, D])
        mm = [bank(f"mm{i}") for i in range(2)]
        dd = [bank(f"dd{i}") for i in range(2)]
        up = [bank(f"u{i}") for i in range(2)]
        acc = [bank(f"acc{i}") for i in range(2)]
        w_loaded, rf_zero, rf_ready, const_step, const_ready = (
            sem("w_loaded"), sem("rf_zero"), sem("rf_ready"), sem("const_step"), sem("const_ready"))
        h_ready, h_used, xs_ready = sem("h_ready"), sem("h_used"), sem("xs_ready")
        mm_ready, mm_done, dd_ready, dd_done = sem("mm_ready"), sem("mm_done"), sem("dd_ready"), sem("dd_done")
        u_ready, turn_ready, frac_ready, fabs_ready, feat_ready, kf_used, qf_used = (
            sem("u_ready"), sem("turn_ready"), sem("frac_ready"), sem("fabs_ready"),
            sem("feat_ready"), sem("kf_used"), sem("qf_used"))
        norms_ready, ks_ready, sums_ready, z_ready, den_done, inv_ready, raw_ready, oT_ready, x_done = (
            sem(k) for k in ("norms_ready", "ks_ready", "sums_ready", "z_ready", "den_done", "inv_ready", "raw_ready",
                             "oT_ready", "x_done"))
        qn_ready, floor_ready = sem("qn_ready"), sem("floor_ready")
        block = st.enter_context(nc.Block())
        MM_HT, MM_QK, MM_S = KD * NGB, 2 * KD * NGB, 2
        MM_BATCH = MM_HT + MM_QK + MM_S
        MM_RB = MM_BATCH - MM_HT
        DD_V, DD_N, DD_O = TPB // 2, KD * NGB, TPB // 2
        DD_BATCH = DD_V + DD_N + DD_O
        U_K = 2 * TPB
        UNITS = KD * NGB
        H_UNITS = (0, 3)
        U_BATCH = U_K + HP * UNITS

        @block.sync
        def _(sp):
            for k in w:
                sp.dma_start(w[k][:], A[k].rearrange("(k p) n -> p k n", p=P)).then_inc(w_loaded, 16)
            sp.wait_ge(rf_zero, 1)
            for i in range(HPK):
                sp.dma_start(rf[i * DH:(i + 1) * DH, i * FEAT:(i + 1) * FEAT], A["rfT"]).then_inc(w_loaded, 16)
            for name, rows, total in (("slots0", SPARE0 * BLK0, E * STRIDE0 + SPARE0 * BLK0), ("slots1", E * SLOTS1, E * SLOTS1)):
                per = rows * D // P
                flat = env[name].ap()[total - rows:total, :].rearrange("(p n) d -> p (n d)", p=P)
                for at in range(0, per, ZERO):
                    n = min(ZERO, per - at)
                    sp.dma_start(flat[:, at:at + n], env["zero"][:, 0:n]).then_inc(env["zeroed"], 16)
                    env["zero_dmas"] += 1

        @block.gpsimd
        def _(pool):
            pool.memset(rf[:, :], 0.0).then_inc(rf_zero, 1)
            pool.memset(headsel[:, :], 1.0).then_inc(const_step, 1)
            pool.memset(headblk[:], 1.0).then_inc(const_step, 1)
            pool.wait_ge(const_step, 2)
            for n, (m, extra) in enumerate(((headsel, []), (headblk, [[0, DH]]))):
                pool.affine_select(out=m[:], in_=m[:], compare_op=ALU.is_ge, fill=0.0, base=0,
                                   pattern=[[-DH, HPK]] + extra, channel_multiplier=1).then_inc(const_step, 1)
                pool.wait_ge(const_step, 3 + n)
                pool.affine_select(out=m[:], in_=m[:], compare_op=ALU.is_ge, fill=0.0, base=DH - 1,
                                   pattern=[[DH, HPK]] + extra, channel_multiplier=-1).then_inc(const_ready, 1)
            for m, v in ((kvT[:], 0.0), (kzT[:], 0.0), (ks[:], 0.0), (log_k[:, :], -0.5 * math.log(FEAT)),
                         (log_q[:, :], math.log(1e-6) + 0.5 * math.log(FEAT))):
                pool.memset(m, v).then_inc(const_ready, 1)
            pool.sem_inc(x_done, 2)
            pool.sem_inc(oT_ready, 2)

            def add(b, g):
                for u in range(g * TPG // 2, (g + 1) * TPG // 2):
                    pool.wait_ge(dd_done, b * DD_BATCH + DD_V + DD_N + u + 1 + 2)
                    xx = x[:, bass.ds(b * TPB + 2 * u, 2), :]
                    pool.tensor_tensor(xx, xx, att[:, u % 2], ALU.add).then_inc(x_done, 1)

            def batch(b, first):
                if not first:
                    add(b - 1, NGB - 1)
                for n in range(UNITS):
                    N = b * UNITS + n
                    pool.wait_ge(inv_ready, N + 1)
                    pool.wait_ge(raw_ready, N + 1 + 1)
                    if n >= KD:
                        pool.wait_ge(dd_ready, b * DD_BATCH + DD_V + DD_N + (n // KD) * (TPG // 2))
                    pool.tensor_tensor(oT[:, n % KD, :], raw[:, n % 2], den[:, n % 2], ALU.mult).then_inc(oT_ready, 1)
                    if n > 0 and n % KD == 0:
                        add(b, n // KD - 1)
            batch(0, True)
            with pool.Fori(1, BATCH) as b:
                batch(b, False)
            add(BATCH - 1, NGB - 1)

        @block.tensor
        def _(pe):
            pe.sem_inc(h_used, TPG)
            pe.sem_inc(kf_used, 2)
            pe.sem_inc(qf_used, 2)
            pe.wait_ge(rf_ready, 1)
            pe.wait_ge(w_loaded, 16 * (4 + HPK))
            pe.wait_ge(const_ready, 7)

            def write_out(g, b, dd_bank):
                pe.wait_ge(oT_ready, b * UNITS + (g + 1) * KD + 2)
                for t2 in range(TPG // 2):
                    bk = dd_bank()
                    for t in (2 * t2, 2 * t2 + 1):
                        for k in range(KD):
                            i = pe.matmul(bk[:, (t % 2) * D:(t % 2 + 1) * D], oT[:, k, t * P:(t + 1) * P],
                                          w["woT"][:, k, :], start=k == 0, stop=k == KD - 1)
                    i.then_inc(dd_ready, 1)

            def write_last(b):
                df = counter(DD_BATCH - TPG // 2)

                def dd_bank():
                    i = df()
                    pe.wait_ge(dd_done, b * DD_BATCH + i)
                    return dd[(i - 1) % 2]
                write_out(NGB - 1, b, dd_bank)

            def turn_h(b, g):
                for j in range(KD):
                    pe.wait_ge(mm_done, b * MM_BATCH + g * KD + j + 1)
                for t in range(TPG):
                    pe.wait_ge(h_ready, b * TPB + g * TPG + t + 1 + 2)
                    for j in range(KD):
                        i = pe.transpose(mm[j][:, t * P:(t + 1) * P], h[:, t, j * P:(j + 1) * P], ident[:, :])
                    i.then_inc(h_used, 1)

            def batch(b, first, last):
                mf, df = counter(MM_HT), counter()

                def mm_bank():
                    i = mf()
                    pe.wait_ge(mm_done, b * MM_BATCH + i)
                    return mm[(i - 1) % 2]

                def dd_bank():
                    i = df()
                    pe.wait_ge(dd_done, b * DD_BATCH + i)
                    return dd[(i - 1) % 2]

                def project(u):
                    pe.wait_ge(frac_ready, b * U_BATCH + u + 1)
                    if u < U_K:
                        t, j = u // 2, u % 2
                        pe.matmul(up[u % 2][:, :], qkT[:, 1, j, t * P:(t + 1) * P], rf[:, :],
                                  start=True, stop=True).then_inc(u_ready, 1)
                    else:
                        unit, c = (u - U_K) // HP, (u - U_K) % HP
                        g, j = unit // KD, unit % KD
                        pe.matmul(up[u % 2][:, :], rf[:, c * P:(c + 1) * P], qkT[:, 0, j, g * G:(g + 1) * G],
                                  start=True, stop=True).then_inc(u_ready, 1)

                def heads(name):
                    for g in range(NGB):
                        for j in range(KD):
                            bk = mm_bank()
                            if name == "wkT":
                                pe.wait_ge(mm_done, b * MM_BATCH + (g + 1) * KD + 2)
                            for k in range(KD):
                                i = pe.matmul(bk[:, :], w[name][:, k, j * P:(j + 1) * P], hT[:, k, g * G:(g + 1) * G],
                                              start=k == 0, stop=k == KD - 1)
                            i.then_inc(mm_ready, 1)

                def values(t2):
                    bk = dd_bank()
                    for t in (2 * t2, 2 * t2 + 1):
                        for k in range(KD):
                            i = pe.matmul(bk[:, (t % 2) * D:(t % 2 + 1) * D], hT[:, k, t * P:(t + 1) * P],
                                          w["wvT"][:, k, :], start=k == 0, stop=k == KD - 1)
                    i.then_inc(dd_ready, 1)
                heads("wkT")
                if not first:
                    write_last(b - 1)
                values(0)
                values(1)
                pe.wait_ge(mm_done, b * MM_BATCH + MM_HT + MM_QK // 2 + 2)
                pe.wait_ge(raw_ready, b * UNITS + 1)
                for t in range(TPB):
                    for j in range(KD):
                        c = (t * KD + j) * HPK
                        i = pe.matmul(acc[0][:, c:c + HPK], sq[:, j, t * P:(t + 1) * P], headsel[:, :],
                                      start=True, stop=True)
                i.then_inc(norms_ready, 1)
                heads("wqT")
                for t2 in range(2, DD_V):
                    values(t2)
                for g in range(NGB):
                    for j in range(KD):
                        pe.wait_ge(mm_done, b * MM_BATCH + MM_HT + MM_QK // 2 + KD * g + j + 1 + 2)
                        bk = dd_bank()
                        pe.matmul(bk[:, :], headblk[:].rearrange("p h v -> p (h v)"), sq[:, j, g * G:(g + 1) * G],
                                  start=True, stop=True).then_inc(dd_ready, 1)

                project(0)
                project(1)
                for t in range(TPB):
                    if t + 1 < TPB:
                        project(2 * t + 2)
                        project(2 * t + 3)
                    else:
                        for c in range(HP):
                            project(U_K + c)
                    if t == 0:
                        pe.wait_ge(dd_done, b * DD_BATCH + DD_V + 2)
                        pe.wait_ge(ks_ready, b + 1)
                    pe.wait_ge(feat_ready, b * U_BATCH + 2 * t + 2 + 2)
                    for j in range(KD):
                        for c in range(HP):
                            p = j * HP + c
                            pe.matmul(acc[0][32 * c:32 * c + 32, j * 256:(j + 1) * 256],
                                      va[:, t, 2 * p:2 * p + 2, :].rearrange("p h v -> p (h v)"),
                                      kf[:, t % 2, :, p * P:(p + 1) * P],
                                      start=t == 0 and j == 0, stop=t == TPB - 1, skip_group_check=True)
                    for c in range(4):
                        i = pe.matmul(acc[1][32 * c:32 * c + 32, :], ks[:, t].rearrange("p m h -> p (m h)"),
                                      kf[:, t % 2, c // 2, (c % 2) * 512:(c % 2 + 1) * 512],
                                      start=t == 0, stop=t == TPB - 1, skip_group_check=True)
                    i.then_inc(kf_used, 1)
                for c in range(HP):
                    project(U_K + HP + c)
                pe.wait_ge(sums_ready, (b + 1) * 2)
                bk = mm_bank()
                for j in range(KD):
                    for cs in range(2):
                        i = pe.transpose(bk[:, (2 * j + cs) * P:(2 * j + cs + 1) * P],
                                         sums[:, 0, (2 * j + cs) * P:(2 * j + cs + 1) * P], ident[:, :])
                i.then_inc(mm_ready, 1)
                bk = mm_bank()
                for c in range(HP):
                    i = pe.transpose(bk[:, c * P:(c + 1) * P], sums[:, 1, c * P:(c + 1) * P], ident[:, :])
                i.then_inc(mm_ready, 1)

                for n in range(UNITS):
                    if 0 < n < UNITS - 1:
                        for c in range(HP):
                            project(U_K + (n + 1) * HP + c)
                    if n == 0:
                        pe.wait_ge(mm_done, b * MM_BATCH + MM_BATCH + 2)
                    if n in H_UNITS and not last:
                        turn_h(b + 1, n // 2)
                    pe.wait_ge(feat_ready, b * U_BATCH + U_K + (n + 1) * HP + 2)
                    j = n % KD
                    for a, m, left, done in ((1, kzT, den_done, z_ready), (0, kvT, raw_ready, qf_used)):
                        pe.wait_ge(left, b * UNITS + n + 1)
                        for cs in range(2):
                            for c in range(HP):
                                i = pe.matmul(acc[a][32 * c:32 * c + 32, :], m[:, j, cs, c].rearrange("p h v -> p (h v)"),
                                              qf[:, n % 2, c, cs, :], start=cs == 0, stop=cs == 1)
                        i.then_inc(done, 1)
                    if n > KD and n % KD == 1:
                        write_out(n // KD - 1, b, dd_bank)
            for g in range(NGB):
                turn_h(0, g)
            batch(0, True, False)
            with pe.Fori(1, BATCH - 1) as b:
                batch(b, False, False)
            batch(BATCH - 1, False, True)
            write_last(BATCH - 1)

        @block.scalar
        def _(act):
            act.wait_ge(w_loaded, 16 * (4 + HPK))
            act.activation(rf[:, :], rf[:, :], ACT.Copy, scale=1.0 / (2 * math.pi)).then_inc(rf_ready, 1)
            act.sem_inc(mm_done, 2)
            act.sem_inc(feat_ready, 2)
            act.sem_inc(raw_ready, 1)
            act.wait_ge(const_ready, 7)

            def copy_hT(b, g):
                act.wait_ge(h_used, b * TPB + (g + 1) * TPG + TPG)
                for j in range(KD):
                    act.activation(hT[:, j, g * G:(g + 1) * G], mm[j][:, :], ACT.Copy).then_inc(mm_done, 1)

            def batch(b, last):
                rf_ = counter()

                def mm_filled():
                    n = rf_()
                    act.wait_ge(mm_ready, b * MM_RB + n)
                    return mm[(n - 1) % 2]

                for m in (1, 0):
                    for g in range(NGB):
                        for j in range(KD):
                            bk = mm_filled()
                            act.activation(qkT[:, m, j, g * G:(g + 1) * G], bk[:, :], ACT.Copy)
                            act.activation(sq[:, j, g * G:(g + 1) * G], bk[:, :], ACT.Square).then_inc(mm_done, 1)
                    if m == 1:
                        act.wait_ge(norms_ready, b + 1)
                        act.activation(ks[:, :, 0, :], acc[0][:, 0:TPB * HEADS].rearrange("p (t h) -> p t h", h=HEADS),
                                       ACT.Exp, scale=-0.5, bias=log_k[:, 0:1]).then_inc(ks_ready, 1)
                act.wait_ge(qn_ready, (b + 1) * DD_N)
                act.activation(floor[:], floor[:], ACT.Exp, scale=0.5, bias=log_q[:, 0:1]).then_inc(floor_ready, 1)

                def features(u, cos, sin):
                    n = b * U_BATCH + u
                    i = u % 2
                    act.wait_ge(frac_ready, n + 1 + 2)
                    act.activation(fabs[:, i], frac[:, i], ACT.Abs).then_inc(fabs_ready, 1)
                    act.activation(sin, frac[:, i], ACT.Sin, scale=2 * math.pi)
                    act.wait_ge(fabs_ready, n + 1)
                    act.activation(cos, fabs[:, i], ACT.Sin, scale=-2 * math.pi,
                                   bias=half_pi[:, 0:1]).then_inc(feat_ready, 1)
                for t in range(TPB):
                    act.wait_ge(kf_used, b * TPB + t + 1)
                    for j in range(KD):
                        features(2 * t + j, *(kf[:, t % 2, cs, j * 512:(j + 1) * 512] for cs in range(2)))

                def copy_raw(n):
                    act.wait_ge(qf_used, b * UNITS + n + 1 + 2)
                    act.wait_ge(oT_ready, b * UNITS + n - 1 + 2)
                    act.activation(raw[:, n % 2], acc[0][:, :], ACT.Copy).then_inc(raw_ready, 1)
                for n in range(UNITS):
                    act.wait_ge(qf_used, b * UNITS + n + 1)
                    for c in range(HP):
                        if n == 0 and c == HP // 2:
                            act.wait_ge(kf_used, (b + 1) * TPB + 2)
                            for a in range(2):
                                act.activation(sums[:, a], acc[a][:, :], ACT.Copy).then_inc(sums_ready, 1)
                        features(U_K + n * HP + c, *(qf[:, n % 2, c, cs, :] for cs in range(2)))
                    if n > 0:
                        copy_raw(n - 1)
                        if n in H_UNITS and not last:
                            copy_hT(b + 1, n // 2)
                        continue
                    bk = mm_filled()
                    for hh in range(2):
                        q = slice(hh * FEAT, (hh + 1) * FEAT)
                        i = act.activation(kvT[q, :, :, :, hh, :].rearrange("p j s c v -> p (j s c) v"),
                                           bk[q, :].rearrange("p (n h v) -> p n h v", h=2, v=DH)[:, :, hh, :], ACT.Copy)
                    i.then_inc(mm_done, 1)
                    bk = mm_filled()
                    for j in range(KD):
                        for cs in range(2):
                            for hh in range(2):
                                q = slice(hh * FEAT, (hh + 1) * FEAT)
                                at = (2 * cs + j) * 32 + j * HPK + hh
                                i = act.activation(kzT[q, j, cs, :, hh, :],
                                                   bk[q, at:at + (P + 2) * (HP - 1) + 1:P + 2].unsqueeze(2)
                                                   .to_broadcast([FEAT, HP, DH]), ACT.Copy)
                    i.then_inc(mm_done, 1)
                    if not last:
                        copy_hT(b + 1, 0)
                copy_raw(UNITS - 1)

            for g in range(NGB):
                copy_hT(0, g)
            with act.Fori(0, BATCH - 1) as b:
                batch(b, False)
            batch(BATCH - 1, True)

        @block.vector
        def _(dve):
            dve.sem_inc(dd_done, 2)
            dve.sem_inc(frac_ready, 2)
            dve.sem_inc(h_ready, 2)
            dve.sem_inc(den_done, 1)

            def make_h(b, tiles):
                for t in tiles[::2]:
                    T = b * TPB + t
                    dve.wait_ge(h_used, T + 2)
                    modulate(dve, env, T, [h[:, (t + i) % TPG] for i in range(2)], xs, b, SHIFT_A, SCALE_A, xs_ready, h_ready)
            make_h(0, range(TPB))

            def gate_out(g, b):
                for t2 in range(TPG // 2):
                    u = g * TPG // 2 + t2
                    dve.wait_ge(dd_ready, b * DD_BATCH + DD_V + DD_N + u + 1)
                    dve.wait_ge(x_done, b * DD_O + u + 1)
                    dve.tensor_tensor(att[:, u % 2], dd[u % 2][:, :].rearrange("p (t d) -> p t d", d=D),
                                      modb[:, bass.ds(b, 1), GATE_A, :].to_broadcast([P, 2, D]), ALU.mult
                                      ).then_inc(dd_done, 1)

            def batch(b, first, last):
                if not first:
                    gate_out(NGB - 1, b - 1)
                dve.wait_ge(ks_ready, b + 1)
                for t2 in range(DD_V):
                    dve.wait_ge(dd_ready, b * DD_BATCH + t2 + 1)
                    dve.tensor_tensor(va[:, 2 * t2:2 * t2 + 2],
                                      dd[t2 % 2][:, :].rearrange("p (t h v) -> p t h v", t=2, v=DH),
                                      ks[:, 2 * t2:2 * t2 + 2, 0, :].unsqueeze(3).to_broadcast([P, 2, HEADS, DH]),
                                      ALU.mult).then_inc(dd_done, 1)
                for g in range(NGB):
                    for j in range(KD):
                        u = DD_V + KD * g + j
                        dve.wait_ge(dd_ready, b * DD_BATCH + u + 1)
                        i = dve.tensor_scalar(floor[:, j, g * G:(g + 1) * G], dd[u % 2][:, :], QN_MAX, None, ALU.min)
                        i.then_inc(dd_done, 1)
                        dve.wait_ge(dd_done, b * DD_BATCH + u + 1 + 2)
                        dve.sem_inc(qn_ready, 1)

                def reduce_turns(us):
                    for u in us:
                        n = b * U_BATCH + u
                        dve.wait_ge(u_ready, n + 1)
                        dve.tensor_scalar(turn[:, u % 2], up[u % 2][:, :], ROUND, ROUND, ALU.add, ALU.subtract
                                          ).then_inc(turn_ready, 1)
                        dve.wait_ge(turn_ready, n + 1)
                        dve.wait_ge(feat_ready, n + 1)
                        dve.tensor_tensor(frac[:, u % 2], up[u % 2][:, :], turn[:, u % 2], ALU.subtract
                                          ).then_inc(frac_ready, 1)

                def unit_turns(n):
                    reduce_turns(range(U_K + n * HP, U_K + (n + 1) * HP))

                def denominator(n):
                    g, j = n // KD, n % KD
                    dve.wait_ge(z_ready, b * UNITS + n + 1)
                    dve.wait_ge(floor_ready, b + 1)
                    dve.wait_ge(oT_ready, b * UNITS + n - 1 + 2)
                    dve.tensor_tensor(den[:, n % 2], acc[1][:, :], floor[:, j, g * G:(g + 1) * G], ALU.max
                                      ).then_inc(den_done, 1)

                def divide(n):
                    N = b * UNITS + n
                    dve.wait_ge(den_done, N + 1 + 1)
                    dve.reciprocal(den[:, n % 2], den[:, n % 2]).then_inc(inv_ready, 1)

                reduce_turns(range(U_K // 2))
                if not first:
                    dve.wait_ge(x_done, b * DD_O + 2)
                    batch_stats(dve, env, b - 1)
                if not last:
                    make_h(b + 1, range(2))
                reduce_turns(range(U_K // 2, U_K * 3 // 4))
                if not last:
                    make_h(b + 1, range(2, TPG))
                reduce_turns(range(U_K * 3 // 4, U_K))
                unit_turns(0)
                for n in range(UNITS):
                    if n + 1 < UNITS:
                        unit_turns(n + 1)
                    if n > 0:
                        divide(n - 1)
                    denominator(n)
                    if n > KD and n % KD == 1:
                        gate_out(n // KD - 1, b)
                    if n < 2 and not last:
                        make_h(b + 1, range(TPG + 2 * n, TPG + 2 * n + 2))
                divide(UNITS - 1)

            batch(0, True, False)
            with dve.Fori(1, BATCH - 1) as b:
                batch(b, False, False)
            batch(BATCH - 1, False, True)
            gate_out(NGB - 1, BATCH - 1)


def phasor(dve, env):
    par, rho, first, tmp, tmp_i, tab = (env[k] for k in ("par", "rho", "first", "tmp", "tmp_i", "tab"))
    n = counter()
    a, b, _, _, last_re, last_im = (par[:, i] for i in range(6))
    t = [tmp[:, i] for i in range(8)]
    dve.wait_ge(env["par_loaded"], 16)

    def ts(out, in0, s1, s2, op0, op1=None):
        dve.tensor_scalar(out, in0, s1, s2, op0, *([op1] if op1 is not None else [])).then_inc(tab, 1)
        dve.wait_ge(tab, n())

    def tt(out, in0, in1, op):
        dve.tensor_tensor(out, in0, in1, op).then_inc(tab, 1)
        dve.wait_ge(tab, n())

    def stt(out, in0, s, in1, op0, op1):
        dve.scalar_tensor_tensor(out=out, in0=in0, scalar=s, in1=in1, op0=op0, op1=op1).then_inc(tab, 1)
        dve.wait_ge(tab, n())

    tt(t[0], a, a, ALU.mult)
    tt(t[1], b, b, ALU.mult)
    tt(t[0], t[0], t[1], ALU.add)
    ts(t[1], t[0], 87.3, None, ALU.is_le)
    ts(t[0], t[0], 87.3, None, ALU.min)
    ts(t[2], t[0], math.log2(math.e), ROUND, ALU.mult, ALU.add)
    ts(t[2], t[2], ROUND, None, ALU.subtract)
    ln2_hi = 0.693359375
    stt(t[0], t[2], -ln2_hi, t[0], ALU.mult, ALU.add)
    stt(t[0], t[2], -(math.log(2) - ln2_hi), t[0], ALU.mult, ALU.add)
    ts(t[0], t[0], -1.0, None, ALU.mult)
    ts(t[3], t[0], 1.0 / 8, 1.0, ALU.mult, ALU.add)
    for k in range(7, 0, -1):
        stt(t[3], t[3], 1.0 / k, t[0], ALU.mult, ALU.mult)
        ts(t[3], t[3], 1.0, None, ALU.add)
    ts(tmp_i[:, :], t[2], -float(1 << 23), 127.0 * (1 << 23), ALU.mult, ALU.add)
    tt(t[3], t[3], tmp_i[:, :].bitcast(F32), ALU.mult)
    tt(rho[:, :], t[3], t[1], ALU.mult)
    ts(t[0], a, -1.0, None, ALU.mult)
    ts(t[1], b, -1.0, None, ALU.mult)
    tt(t[0], t[0], a, ALU.max)
    tt(t[1], t[1], b, ALU.max)
    tt(t[0], t[0], t[1], ALU.max)
    ts(t[1], t[0], 1.2e-38, None, ALU.is_lt)
    tt(t[0], t[0], t[1], ALU.add)
    dve.reciprocal(t[0], t[0]).then_inc(tab, 1)
    dve.wait_ge(tab, n())
    tt(t[2], a, t[0], ALU.mult)
    tt(t[2], t[2], t[1], ALU.add)
    tt(t[3], b, t[0], ALU.mult)
    tt(t[4], t[2], t[2], ALU.mult)
    tt(t[5], t[3], t[3], ALU.mult)
    tt(t[4], t[4], t[5], ALU.add)
    inverse_sqrt(dve, t[4], t[5], t[6], t[7], tmp_i[:, :], tab, n)
    c, s = t[2], t[3]
    tt(c, c, t[6], ALU.mult)
    tt(s, s, t[6], ALU.mult)
    tt(t[0], c, last_re, ALU.mult)
    tt(t[1], s, last_im, ALU.mult)
    tt(first[:, 0], t[0], t[1], ALU.subtract)
    tt(t[0], s, last_re, ALU.mult)
    tt(t[1], c, last_im, ALU.mult)
    tt(first[:, 1], t[0], t[1], ALU.add)
    assert n(0) == PHASOR_STEPS, n(0)


def first_powers(dve, env):
    rot0, step_c, tmp, scratch, tab = (env[k] for k in ("rot0", "step_c", "tmp", "scratch", "tab"))
    n = counter(PHASOR_STEPS)
    t = [tmp[:, i] for i in range(8)]
    c, s = t[2], t[3]

    def tt(out, in0, in1, op):
        dve.tensor_tensor(out, in0, in1, op).then_inc(tab, 1)
        dve.wait_ge(tab, n())
    dve.memset(rot0[:, 0, :, 0:1], 1.0).then_inc(tab, 1)
    dve.memset(rot0[:, 1, :, 0:1], 0.0).then_inc(tab, 1)
    dve.wait_ge(tab, n(2))
    m = 1
    while m < CHUNK:
        w = min(m, CHUNK - m)
        rotate(dve, lambda i, k: rot0[:, i, k, 0:w], lambda i, k: rot0[:, i, k, m:m + w], c, s, scratch, w, tab, n)
        if w < m:
            tt(t[0], c, step_c[:, 0], ALU.mult)
            tt(t[1], s, step_c[:, 1], ALU.mult)
            tt(t[4], c, step_c[:, 1], ALU.mult)
            tt(t[5], s, step_c[:, 0], ALU.mult)
            tt(step_c[:, 0], t[0], t[1], ALU.subtract)
            tt(step_c[:, 1], t[4], t[5], ALU.add)
            break
        if m == CHUNK % 32:
            dve.tensor_copy(step_c[:, 0], c).then_inc(tab, 1)
            dve.tensor_copy(step_c[:, 1], s).then_inc(tab, 1)
            dve.wait_ge(tab, n(2))
        tt(t[0], c, c, ALU.mult)
        tt(t[1], s, s, ALU.mult)
        dve.scalar_tensor_tensor(out=s, in0=s, scalar=2.0, in1=c, op0=ALU.mult, op1=ALU.mult).then_inc(tab, 1)
        dve.wait_ge(tab, n())
        tt(c, t[0], t[1], ALU.subtract)
        m *= 2
    assert n(0) == POWER_STEPS, n(0)


def rotate(dve, src, dst, c, s, scratch, w, tab, n):
    for k in range(KD):
        for i in range(2):
            dve.tensor_scalar(scratch[:, k, i, 0:w], src(1 - i, k), s[:, k:k + 1], None, ALU.mult).then_inc(tab, 1)
    for k in range(KD):
        dve.wait_ge(tab, n(2))
        for i, sign in enumerate((ALU.subtract, ALU.add)):
            dve.scalar_tensor_tensor(out=dst(i, k), in0=src(i, k), scalar=c[:, k:k + 1], in1=scratch[:, k, i, 0:w],
                                     op0=ALU.mult, op1=sign).then_inc(tab, 1)
    dve.wait_ge(tab, n(2 * KD))


def table_chunk(dve, env, at, steps):
    rot, step_c, scratch, tab = (env[k] for k in ("rot", "step_c", "scratch", "tab"))
    n = counter()
    dve.wait_ge(tab, steps)
    rotate(dve, lambda i, k: rot[:, i, k, bass.ds(at, CHUNK)], lambda i, k: rot[:, i, k, bass.ds(at + CHUNK, CHUNK)],
           step_c[:, 0], step_c[:, 1], scratch, CHUNK, tab, lambda k: steps + n(k))


def coefficients(dve, env, scratch, k, step, n):
    par, rot, coef = (env[q] for q in ("par", "rot", "coef"))
    init_re, init_im = par[:, 2, k:k + 1], par[:, 3, k:k + 1]
    for i, q in enumerate((init_im, init_re)):
        dve.tensor_scalar(scratch[:, i], rot[:, 1, k, 0:SEQ], q, None, ALU.mult).then_inc(step, 1)
    dve.wait_ge(step, n(2))
    for i, (q, sign) in enumerate(((init_re, ALU.add), (init_im, ALU.subtract))):
        dve.scalar_tensor_tensor(out=coef[:, i, k, :], in0=rot[:, 0, k, 0:SEQ], scalar=q, in1=scratch[:, i],
                                 op0=ALU.mult, op1=sign).then_inc(step, 1)
    dve.wait_ge(step, n(2))


def recurrence(nc, A, env):
    with ExitStack() as st:
        sb = lambda n, s, dt=F32: st.enter_context(nc.sbuf_tensor("rc_" + n, s, dt))
        sem = lambda n: st.enter_context(nc.semaphore("rc_" + n))
        bank = lambda n: st.enter_context(nc.psum_tensor("rc_" + n, [P, 512], F32))
        x, ident, modb = (env[k] for k in ("x", "ident", "modb"))
        rho, first, rot, coef = (env[k] for k in ("rho", "first", "rot", "coef"))
        mean, rstd, mod_col = (env[k] for k in ("mean", "rstd", "mod_col"))
        h = sb("h", [P, TPG, D])
        shift_n = sb("shift_n", [P, NT])
        scale_c = sb("scale_c", [P, KD, BATCH])
        shift_c = sb("shift_c", [P, KD, BATCH])
        first_c = sb("first_c", [P, 2, KD, BATCH])
        hT, yT = (env["staging"][i][:, 0:KD * SEQ].rearrange("p (k t) -> p k t", k=KD) for i in range(2))
        r = sb("r", [P, 2, 2, SEQ])
        tp = [bank(f"tp{i}") for i in range(4)]
        dd = [bank(f"dd{i}") for i in range(2)]
        h_ready, h_used, cols_ready, hT_done, re_ready, im_ready, scanned, turned_re, turned_im, y_ready, dd_ready, x_done = (
            sem(k) for k in ("h_ready", "h_used", "cols_ready", "hT_done", "re_ready", "im_ready", "scanned", "turned_re",
                             "turned_im", "y_ready", "dd_ready", "x_done"))
        NGB = SEQ // G
        UB = TPB // 2
        block = st.enter_context(nc.Block())

        @block.gpsimd
        def _(pool):
            with pool.Fori(0, BATCH) as b:
                pool.wait_ge(y_ready, b * KD + 1)
                for k in range(KD):
                    pool.wait_ge(hT_done, (b + 1) * KD * NGB + 2 * KD)
                    pool.tensor_tensor(r[:, k, 1, :], coef[:, 1, k, :], hT[:, k, :], ALU.mult).then_inc(im_ready, 1)
                for k in range(KD):
                    pool.wait_ge(scanned, (b * KD + k) * 2 + 2)
                    pool.tensor_tensor(r[:, k, 1, :], rot[:, 1, k, 0:SEQ], r[:, k, 1, :], ALU.mult).then_inc(turned_im, 1)

        @block.tensor
        def _(pe):
            pe.sem_inc(h_used, TPG)

            def turn_h(b):
                for g in range(NGB):
                    for t in range(TPG):
                        pe.wait_ge(h_ready, b * TPB + g * TPG + t + 1)
                        if t == 0:
                            pe.wait_ge(hT_done, (b * NGB + g) * KD + KD)
                        for k in range(KD):
                            i = pe.transpose(tp[2 * g + k][:, t * P:(t + 1) * P], h[:, t, k * P:(k + 1) * P], ident[:, :])
                        i.then_inc(h_used, 1)

            def turn_y(b):
                pe.wait_ge(y_ready, (b + 1) * KD + 1)
                for u in range(UB):
                    pe.wait_ge(x_done, b * UB + u + 1)
                    for t in range(2):
                        for k in range(KD):
                            c = (2 * u + t) * P
                            i = pe.transpose(dd[u % 2][:, t * D + k * P:t * D + (k + 1) * P], yT[:, k, c:c + P], ident[:, :])
                    i.then_inc(dd_ready, 1)
            turn_h(0)
            with pe.Fori(0, BATCH - 1) as b:
                turn_h(b + 1)
                turn_y(b)
            turn_y(BATCH - 1)

        @block.scalar
        def _(act):
            act.sem_inc(hT_done, 2 * KD)
            act.wait_ge(cols_ready, 7)

            def normalise(b, g):
                for t in range(TPG):
                    T = b * TPB + g * TPG + t
                    act.wait_ge(h_used, T + 1)
                    act.activation(h[:, t], row(x, T), ACT.Identity, scale=rstd[:, bass.ds(T, 1)],
                                   bias=shift_n[:, bass.ds(T, 1)]).then_inc(h_ready, 1)

            def copy_hT(b, g):
                act.wait_ge(h_used, b * TPB + (g + 1) * TPG + TPG)
                for k in range(KD):
                    act.activation(hT[:, k, g * G:(g + 1) * G], tp[2 * g + k][:, :], ACT.Identity,
                                   scale=scale_c[:, k, bass.ds(b, 1)], bias=shift_c[:, k, bass.ds(b, 1)]).then_inc(hT_done, 1)

            def batch(b, last):
                act.wait_ge(re_ready, b * KD + 1)
                act.wait_ge(im_ready, b * KD + 1)
                copy_hT(b, 0)
                normalise(b, 1)
                copy_hT(b, 1)
                if not last:
                    normalise(b + 1, 0)
            normalise(0, 0)
            for b in range(BATCH):
                batch(b, b == BATCH - 1)

        @block.vector
        def _(dve):
            dve.tensor_tensor(shift_n[:, :], mean[:, :], rstd[:, :], ALU.mult).then_inc(cols_ready, 1)
            gate = mod_col[:, GATE_A]
            dve.tensor_tensor(scale_c[:], mod_col[:, SCALE_A], gate, ALU.mult).then_inc(cols_ready, 1)
            dve.tensor_tensor(shift_c[:], mod_col[:, SHIFT_A], gate, ALU.mult).then_inc(cols_ready, 1)
            for i in range(2):
                dve.tensor_tensor(first_c[:, i], first[:, i].unsqueeze(2).to_broadcast([P, KD, BATCH]), gate, ALU.mult
                                  ).then_inc(cols_ready, 1)
            dve.wait_ge(cols_ready, 5)
            dve.tensor_scalar(shift_n[:, :], shift_n[:, :], -1.0, None, ALU.mult).then_inc(cols_ready, 1)
            dve.wait_ge(cols_ready, 6)
            dve.sem_inc(re_ready, 1)
            dve.sem_inc(im_ready, 1)
            dve.sem_inc(cols_ready, 1)
            dve.sem_inc(x_done, 2)
            dve.sem_inc(y_ready, 1)

            def batch(b, opening):
                dve.wait_ge(y_ready, b * KD + 1)
                dve.wait_ge(hT_done, (b + 1) * KD * NGB + 2 * KD)
                for k in range(KD):
                    dve.tensor_tensor(r[:, k, 0, :], coef[:, 0, k, :], hT[:, k, :], ALU.mult).then_inc(re_ready, 1)
                for k in range(KD):
                    decay = rho[:, k:k + 1].to_broadcast([P, SEQ])
                    for i, ready in enumerate((re_ready, im_ready)):
                        dve.wait_ge(ready, b * KD + k + 1 + 1)
                        dve.tensor_tensor_scan(r[:, k, i, :], decay, r[:, k, i, :], first_c[:, i, k, bass.ds(b, 1)],
                                               ALU.mult, ALU.add).then_inc(scanned, 1)
                    dve.wait_ge(scanned, (b * KD + k) * 2 + 2)
                    dve.tensor_tensor(r[:, k, 0, :], rot[:, 0, k, 0:SEQ], r[:, k, 0, :], ALU.mult).then_inc(turned_re, 1)
                if not opening:
                    dve.wait_ge(x_done, b * UB + 2)
                    batch_stats(dve, env, b - 1)
                for k in range(KD):
                    dve.wait_ge(turned_re, b * KD + k + 1)
                    dve.wait_ge(turned_im, b * KD + k + 1)
                    dve.tensor_tensor(yT[:, k, :], r[:, k, 0, :], r[:, k, 1, :], ALU.subtract).then_inc(y_ready, 1)
                for u in range(UB):
                    dve.wait_ge(dd_ready, b * UB + u + 1)
                    xx = x[:, bass.ds(b * TPB + 2 * u, 2), :]
                    dve.tensor_tensor(xx, xx, dd[u % 2][:, :].rearrange("p (t d) -> p t d", d=D), ALU.add).then_inc(x_done, 1)
            batch(0, True)
            with dve.Fori(1, BATCH) as b:
                batch(b, False)


def dense_and_router(nc, A, env, layer):
    with ExitStack() as st:
        sb = lambda n, s, dt=F32: st.enter_context(nc.sbuf_tensor(f"dn{layer}_" + n, s, dt))
        sem = lambda n: st.enter_context(nc.semaphore(f"dn{layer}_" + n))
        bank = lambda n: st.enter_context(nc.psum_tensor(f"dn{layer}_" + n, [P, 512], F32))
        x, ident, modb, before, ones = (env[k] for k in ("x", "ident", "modb", "before", "ones"))
        weight, put, get = (env[k] for k in ("weight", "put", "get"))
        shared = layer == 0
        STRIDE = STRIDE0 if shared else SLOTS1
        FK = FF0 // P
        WIN, WOUT = 2 * KD * FF0, FK * D
        hall = sb("hall", [P, NT, D])
        rw = sb("rw", [P, KD, E])
        xs = sb("xs", [P, 2, D])
        h = sb("h", [P, TPG, D])
        hT = sb("hT", [P, KD, G])
        if shared:
            raw, w_part = env["staging"][1], env["w_part"][0]
            hs = sb("hs", [P, 2, KD, G], F32R)
            silu = sb("silu", [P, 2, G])
            a = sb("a", [P, 2, G])
            aT = sb("aT", [P, 2, FK, G], F32R)
            gated = sb("gated", [P, 2, 2, D])
            choice = sb("choice", [P, 2, NT])
            sent_to = sb("sent_to", [P, 2, NT])
        else:
            gh = sb("gh", [P, 2, D])
            gh_ready = sem("gh_ready")
        bias = sb("bias", [P, E])
        logits, prob, others, work, m1, m2, both, rank, run = (
            sb(k, [P, TPB, E]) for k in ("logits", "prob", "others", "work", "m1", "m2", "both", "rank", "run"))
        best = sb("best", [P, 2, TPB])
        pick, slot, slot2 = (sb(k, [P, TPB]) for k in ("pick", "slot", "slot2"))
        order = sb("order", [P, E])
        base = sb("base", [P, E])
        count = sb("count", [P, E])
        tp = [bank(f"tp{i}") for i in range(KD)]
        gp = [bank(f"gp{i}") for i in range(2)]
        upp = [bank(f"up{i}") for i in range(2)]
        dd = [bank(f"dd{i}") for i in range(2)]
        w_loaded, h_ready, h_used, h_kept, xs_ready, hT_done = (
            sem("w_loaded"), sem("h_ready"), sem("h_used"), sem("h_kept"), sem("xs_ready"), sem("hT_done"))
        dd_ready, dd_done, x_done = sem("dd_ready"), sem("dd_done"), sem("x_done")
        step, exp_in, exp_done, both_ready, const_ready, routed, sent, logits_ready = (
            sem(k) for k in ("step", "exp_in", "exp_done", "both_ready", "const_ready", "routed", "sent", "logits_ready"))
        if shared:
            w_hi, w_ready, hs_hi, hs_done, gu_ready, silu_ready, a_ready, a_hi, a_done, tabled, padded = (
                sem(k) for k in ("w_hi", "w_ready", "hs_hi", "hs_done", "gu_ready", "silu_ready", "a_ready", "a_hi",
                                 "a_done", "tabled", "padded"))
        block = st.enter_context(nc.Block())
        NGB = SEQ // G
        DDB = NGB * (1 + 2 * shared) + 2
        PASSES = ((0, 0), (0, 1), (1, 0))

        def fills_before(b):
            return 0 if isinstance(b, int) and b == 0 else b * DDB - 2

        def sweep(engine, body):
            body(0, True, False)
            with engine.Fori(1, BATCH - 1) as b:
                body(b, False, False)
            body(BATCH - 1, False, True)

        @block.sync
        def _(sp):
            if shared:
                for k, lo, hi, n in (("sgT", 0, WIN // 2, FF0), ("suT", WIN // 2, WIN, FF0), ("sdT", WIN, WIN + WOUT, D)):
                    sp.dma_start(raw[:, lo:hi].rearrange("p (k n) -> p k n", n=n), A[k].rearrange("(k p) n -> p k n", p=P)
                                 ).then_inc(w_loaded, 16)
                sp.dma_start(bias[:, :], A["L0_ffn_routing_bias"].rearrange("(o e) -> o e", o=1).to_broadcast([P, E])
                             ).then_inc(w_loaded, 16)
            sp.dma_start(rw[:], A[f"rw{layer}T"].rearrange("(k p) n -> p k n", p=P)).then_inc(w_loaded, 16)
            if shared:
                sp.wait_ge(tabled, 1)
                for e in range(E):
                    c = sp.value_load(env["counts"][0:1, e:e + 1], min_val=0, max_val=TOK)
                    for part in range(2):
                        sp.dma_start(env["slots0"].ap()[bass.ds(c + (e * STRIDE + part * BLK0 // 2), BLK0 // 2), :]
                                     .rearrange("(p r) d -> p (r d)", p=P), env["zero"][:, 0:BLK0 // 2 * D // P]
                                     ).then_inc(padded, 16)
                sp.wait_ge(tabled, 2)
                load_set(sp, A, env, 0, 0, 0, env["set0_loaded"])
                sp.wait_ge(padded, 16 * 2 * E)
            else:
                load_set(sp, A, env, 1, 0, 0, env["set0_loaded"])

        @block.gpsimd
        def _(pool):
            pool.iota(order[:, :], pattern=[[-1, E]], base=E, channel_multiplier=0,
                      allow_small_or_imprecise_dtypes=True).then_inc(const_ready, 1)
            pool.iota(base[:, :], pattern=[[STRIDE, E]], base=0, channel_multiplier=0,
                      allow_small_or_imprecise_dtypes=True).then_inc(const_ready, 1)
            pool.memset(count[:, :], 0.0).then_inc(const_ready, 1)
            if shared:
                pool.wait_ge(w_hi, 1)
                pool.tensor_tensor(w_part[:, 1], raw[:, :], w_part[:, 0].bitcast(F32), ALU.subtract).then_inc(w_ready, 1)
            if shared:
                pool.sem_inc(x_done, 2)
            pool.wait_ge(env["zeroed"], 16 * env["zero_dmas"])
            slots = env[f"slots{layer}"].ap()

            def send(b):
                pool.wait_ge(routed, b + 1)
                pool.wait_ge(h_kept, (b + 1) * TPB + TPG)
                for t in range(b * TPB, (b + 1) * TPB):
                    for c in range(2):
                        pool.indirect_dma_start(slots, bass.IndirectOffsetOnAxis(ap=put[:, c, t:t + 1], axis=0),
                                                hall[:, t, :], None, bounds_check=slots.shape[0] - 1,
                                                oob_is_err=False).then_inc(sent, 16)

            def add(b, g):
                gi = b * NGB + g
                for u in range(2):
                    pool.wait_ge(dd_done, fills_before(b) + 2 + (3 * g + 1 + u + 1) + (2 if b > 0 and g == NGB - 1 else 0))
                    xx = x[:, gi * TPG + 2 * u:gi * TPG + 2 * u + 2, :]
                    pool.tensor_tensor(xx, xx, gated[:, u], ALU.add).then_inc(x_done, 1)
            for b in range(BATCH):
                if shared:
                    add(b, 0)
                if b > 0:
                    send(b - 1)
                if shared:
                    add(b, 1)
            send(BATCH - 1)
            pool.wait_ge(sent, 16 * 2 * NT)

        @block.tensor
        def _(pe):
            pe.sem_inc(h_used, TPG)
            pe.wait_ge(w_loaded, 16 * (1 + 4 * shared))

            def transposes(gi):
                pe.wait_ge(hs_done if shared else hT_done, gi * KD + KD)
                for t in range(TPG):
                    pe.wait_ge(h_ready, gi * TPG + t + 1 + 2)
                    for j in range(KD):
                        i = pe.transpose(tp[j][:, t * P:(t + 1) * P], h[:, t, j * P:(j + 1) * P], ident[:, :])
                    i.then_inc(h_used, 1)
            transposes(0)

            def ranks(b, bank_of):
                for q, m in enumerate((before, ones)):
                    bk = bank_of()
                    if q == 0:
                        pe.wait_ge(both_ready, b + 1)
                    pe.matmul(bk[:, 0:TPB * E], m[:, :], both[:].rearrange("p t e -> p (t e)"), start=True, stop=True
                              ).then_inc(dd_ready, 1)

            def bank_from(b):
                df = counter()

                def dd_bank():
                    i = df()
                    pe.wait_ge(dd_done, fills_before(b) + i)
                    return dd[(i - 1) % 2]
                return dd_bank

            def body(b, first, last):
                dd_bank = bank_from(b)
                for g in range(NGB):
                    gi = b * NGB + g
                    pe.wait_ge(hT_done, gi * KD + 2 * KD)
                    bk = dd_bank()
                    for t in range(TPG):
                        for k in range(KD):
                            i = pe.matmul(bk[:, t * E:(t + 1) * E], hT[:, k, t * P:(t + 1) * P], rw[:, k, :],
                                          start=k == 0, stop=k == KD - 1)
                    i.then_inc(dd_ready, 1)
                    if shared:
                        if first and g == 0:
                            pe.wait_ge(w_ready, 1)
                        pe.wait_ge(hs_done, gi * KD + 2 * KD)
                        for f in range(FK):
                            pe.wait_ge(a_ready, gi * FK + f + 1)
                            for m, bkk in enumerate((gp, upp)):
                                for k in range(KD):
                                    c = (m * KD + k) * FF0 + f * P
                                    for q, (pw, ph) in enumerate(PASSES):
                                        i = pe.matmul(bkk[f % 2][:, :], w_part[:, pw, c:c + P], hs[:, ph, k, :],
                                                      start=k == 0 and q == 0, stop=k == KD - 1 and q == 2)
                            i.then_inc(gu_ready, 1)
                            if g == NGB - 1 and f == 0 and not first:
                                ranks(b - 1, dd_bank)
                    if not (last and g == NGB - 1):
                        transposes(gi + 1)
                    if not shared and g == NGB - 1 and not first:
                        ranks(b - 1, dd_bank)
                    if shared:
                        for u in range(2):
                            bk = dd_bank()
                            for t in range(2):
                                for k in range(FK):
                                    c = (2 * u + t) * P
                                    if c == 0:
                                        pe.wait_ge(a_done, gi * FK + k + 1)
                                    for q, (pa, pw) in enumerate(PASSES):
                                        i = pe.matmul(bk[:, t * D:(t + 1) * D], aT[:, pa, k, c:c + P],
                                                      w_part[:, pw, WIN + k * D:WIN + (k + 1) * D],
                                                      start=k == 0 and q == 0, stop=k == FK - 1 and q == 2)
                            i.then_inc(dd_ready, 1)
            sweep(pe, body)
            ranks(BATCH - 1, bank_from(BATCH))

        @block.scalar
        def _(act):
            act.sem_inc(h_kept, TPG)
            act.sem_inc(hT_done, KD)
            if shared:
                act.wait_ge(w_loaded, 16 * 5)
                act.activation(w_part[:, 0], raw[:, :], ACT.Copy).then_inc(w_hi, 1)

            def keep(gi):
                for t in range(TPG):
                    T = gi * TPG + t
                    act.wait_ge(h_ready, T + 1 + 2)
                    act.activation(row(hall, T), h[:, t], ACT.Copy).then_inc(h_kept, 1)

            def copy_hT(gi):
                act.wait_ge(h_used, (gi + 1) * TPG + TPG)
                for j in range(KD):
                    act.activation(hT[:, j, :], tp[j][:, :], ACT.Copy).then_inc(hT_done, 1)
                if shared:
                    for j in range(KD):
                        act.activation(hs[:, 0, j, :], tp[j][:, :], ACT.Copy).then_inc(hs_hi, 1)
            keep(0)
            copy_hT(0)

            def exponentials(b):
                act.wait_ge(exp_in, b + 1)
                act.activation(prob[:], work[:], ACT.Exp, scale=-1.0 if shared else 1.0).then_inc(exp_done, 1)

            def body(b, first, last):
                for g in range(NGB):
                    gi = b * NGB + g
                    if not shared and g == 0 and not first:
                        exponentials(b - 1)
                    if shared:
                        def round_a(f):
                            act.wait_ge(a_ready, gi * FK + f + 1 + 2)
                            act.activation(aT[:, 0, f, :], a[:, f % 2], ACT.Copy).then_inc(a_hi, 1)
                        for f in range(FK):
                            act.wait_ge(gu_ready, gi * FK + f + 1)
                            act.activation(silu[:, f % 2], gp[f % 2][:, :], ACT.Silu).then_inc(silu_ready, 1)
                            if f > 0:
                                round_a(f - 1)
                            if g == 0 and f == 0 and not first:
                                exponentials(b - 1)
                        round_a(FK - 1)
                    if not (last and g == NGB - 1):
                        keep(gi + 1)
                        copy_hT(gi + 1)
            sweep(act, body)
            exponentials(BATCH - 1)
            if not shared:
                round_set0(act, env, layer)

        @block.vector
        def _(dve):
            if shared:
                dve.sem_inc(a_ready, 2)
                dve.sem_inc(hs_done, KD)
            else:
                dve.sem_inc(x_done, 2)
            dve.sem_inc(dd_done, 2)
            dve.sem_inc(h_ready, 2)
            dve.sem_inc(step, 1)

            def over_e(ap):
                return ap.unsqueeze(2).to_broadcast([P, TPB, E])

            def over_t(ap):
                return ap.unsqueeze(1).to_broadcast([P, TPB, E])

            def route(b):
                n = counter()
                tiles = slice(b * TPB, (b + 1) * TPB) if isinstance(b, int) else bass.ds(b * TPB, TPB)
                flat = lambda ap: ap.rearrange("p t e -> p (t e)")

                def done(k=1):
                    dve.wait_ge(step, b * ROUTE_STEPS[layer] + n(k) + 1)

                def probabilities():
                    dve.wait_ge(logits_ready, NGB * (b + 1))
                    dve.wait_ge(step, b * ROUTE_STEPS[layer] + 1)
                    if shared:
                        dve.tensor_tensor(work[:], logits[:], over_t(bias[:, :]), ALU.add).then_inc(exp_in, 1)
                    else:
                        dve.tensor_reduce(pick[:, :], logits[:], AXX, ALU.max).then_inc(step, 1)
                        done()
                        dve.tensor_tensor(work[:], logits[:], over_e(pick[:, :]), ALU.subtract).then_inc(exp_in, 1)

                def normalise():
                    dve.wait_ge(exp_done, b + 1)
                    if shared:
                        dve.tensor_scalar(work[:], prob[:], 1.0, None, ALU.add).then_inc(step, 1)
                        done()
                        dve.reciprocal(prob[:], work[:]).then_inc(step, 1)
                        done()
                    else:
                        dve.tensor_reduce(pick[:, :], prob[:], AXX, ALU.add).then_inc(step, 1)
                        done()
                        dve.reciprocal(slot[:, :], pick[:, :]).then_inc(step, 1)
                        done()
                        dve.tensor_tensor(prob[:], prob[:], over_e(slot[:, :]), ALU.mult).then_inc(step, 1)
                        done()

                def largest(c, m, prob):
                    dve.tensor_reduce(best[:, c], prob[:], AXX, ALU.max).then_inc(step, 1)
                    done()
                    dve.tensor_tensor(work[:], prob[:], over_e(best[:, c]), ALU.is_equal).then_inc(step, 1)
                    done()
                    dve.tensor_tensor(work[:], work[:], over_t(order[:, :]), ALU.mult).then_inc(step, 1)
                    done()
                    found = choice[:, c, tiles] if shared else pick[:, :]
                    dve.tensor_reduce(found, work[:], AXX, ALU.max).then_inc(step, 1)
                    done()
                    dve.tensor_tensor(m[:], work[:], over_e(found), ALU.is_equal).then_inc(step, 1)
                    done()

                def second():
                    dve.scalar_tensor_tensor(out=flat(others[:]), in0=flat(m1[:]), scalar=-4.0, in1=flat(prob[:]),
                                             op0=ALU.mult, op1=ALU.add).then_inc(step, 1)
                    done()
                    largest(1, m2, others)
                    dve.tensor_tensor(both[:], m1[:], m2[:], ALU.add).then_inc(both_ready, 1)

                def by_number():
                    dve.wait_ge(both_ready, b + 1)
                    dve.tensor_tensor(work[:], both[:], over_t(order[:, :]), ALU.mult).then_inc(step, 1)
                    done()
                    dve.tensor_reduce(pick[:, :], work[:], AXX, ALU.max).then_inc(step, 1)
                    done()
                    dve.tensor_tensor(m1[:], work[:], over_e(pick[:, :]), ALU.is_equal).then_inc(step, 1)
                    done()
                    dve.tensor_tensor(m2[:], both[:], m1[:], ALU.subtract).then_inc(step, 1)
                    dve.tensor_tensor(work[:], m1[:], prob[:], ALU.mult).then_inc(step, 1)
                    done(2)
                    dve.tensor_tensor(others[:], m2[:], prob[:], ALU.mult).then_inc(step, 1)
                    dve.tensor_reduce(best[:, 0], work[:], AXX, ALU.add).then_inc(step, 1)
                    done(2)
                    dve.tensor_reduce(best[:, 1], others[:], AXX, ALU.add).then_inc(step, 1)
                    done()

                def shares():
                    if not shared:
                        by_number()
                    dve.tensor_tensor(pick[:, :], best[:, 0], best[:, 1], ALU.add).then_inc(step, 1)
                    done()
                    dve.reciprocal(slot[:, :], pick[:, :]).then_inc(step, 1)
                    done()
                    for c in range(2):
                        dve.tensor_tensor(weight[:, c, tiles], best[:, c], slot[:, :], ALU.mult).then_inc(step, 1)
                    done(2)

                def ranks():
                    F = fills_before(b + 1) + (0 if isinstance(b, int) and b == BATCH - 1 else NGB + 2 * shared)
                    lo, hi = dd
                    dve.wait_ge(dd_ready, F + 2)
                    total = hi[:, 0:TPB * E].rearrange("p (t e) -> p t e", e=E)
                    for e in range(E):
                        dve.tensor_tensor_scan(run[:, :, e], ones[:, 0:TPB], total[:, :, e], count[:, e:e + 1], ALU.mult,
                                               ALU.add).then_inc(step, 1)
                    done(E)
                    dve.tensor_tensor(rank[:], run[:], total, ALU.subtract).then_inc(step, 1)
                    dve.tensor_copy(count[:, :], run[:, TPB - 1, :]).then_inc(step, 1)
                    done(2)
                    dve.tensor_tensor(rank[:], rank[:], lo[:, 0:TPB * E].rearrange("p (t e) -> p t e", e=E), ALU.add
                                      ).then_inc(step, 1)
                    done()
                    dve.sem_inc(dd_done, 2)
                    dve.tensor_tensor(work[:], rank[:], over_t(base[:, :]), ALU.add).then_inc(step, 1)
                    done()

                def slots_of(c, m):
                    dve.tensor_tensor(prob[:], m[:], work[:], ALU.mult).then_inc(step, 1)
                    done()
                    dve.tensor_reduce(slot[:, :], prob[:], AXX, ALU.add).then_inc(step, 1)
                    done()
                    if shared:
                        dve.tensor_copy(sent_to[:, c, tiles], slot[:, :]).then_inc(step, 1)
                        dve.tensor_copy(put[:, c, tiles], slot[:, :]).then_inc(step, 1)
                        done(2)
                        return
                    dve.tensor_tensor(prob[:], m[:], rank[:], ALU.mult).then_inc(step, 1)
                    done()
                    dve.tensor_reduce(pick[:, :], prob[:], AXX, ALU.add).then_inc(step, 1)
                    done()
                    dve.tensor_scalar(pick[:, :], pick[:, :], float(CAP), None, ALU.is_lt).then_inc(step, 1)
                    done()
                    dve.tensor_tensor(weight[:, c, tiles], weight[:, c, tiles], pick[:, :], ALU.mult).then_inc(step, 1)
                    dve.tensor_tensor(slot[:, :], slot[:, :], pick[:, :], ALU.mult).then_inc(step, 1)
                    done(2)
                    dve.tensor_scalar(slot2[:, :], pick[:, :], -float(DROP), float(DROP), ALU.mult, ALU.add
                                      ).then_inc(step, 1)
                    dve.tensor_copy(get[:, c, tiles], slot[:, :]).then_inc(step, 1)
                    done(2)
                    dve.tensor_tensor(put[:, c, tiles], slot[:, :], slot2[:, :], ALU.add).then_inc(step, 1)
                    done()

                def finish():
                    slots_of(1, m2)
                    assert n(0) == ROUTE_STEPS[layer], n(0)
                    dve.sem_inc(routed, 1)
                return (probabilities, normalise, lambda: largest(0, m1, prob), second, shares, ranks,
                        lambda: slots_of(0, m1), finish)

            def rest_of_hT(gi):
                for j in range(KD):
                    dve.wait_ge(hs_hi, gi * KD + j + 1)
                    dve.tensor_tensor(hs[:, 1, j, :], tp[j][:, :], hs[:, 0, j, :].bitcast(F32), ALU.subtract
                                      ).then_inc(hs_done, 1)

            def make_h(gi, batch):
                for t in range(0, TPG, 2):
                    T = gi * TPG + t
                    dve.wait_ge(h_used, T + 2)
                    dve.wait_ge(h_kept, T + 2)
                    modulate(dve, env, T, [h[:, t + i] for i in range(2)], xs, batch, SHIFT_B, SCALE_B, xs_ready, h_ready)
                    if not shared:
                        for i in range(2):
                            dve.wait_ge(h_ready, T + i + 1 + 2)
                            dve.wait_ge(x_done, T + i + 1)
                            dve.tensor_tensor(gh[:, i], h[:, t + i],
                                              modb[:, bass.ds(batch, 1), GATE_B, :].rearrange("p o n -> p (o n)"),
                                              ALU.mult).then_inc(gh_ready, 1)
                        for i in range(2):
                            dve.wait_ge(gh_ready, T + i + 1)
                            dve.tensor_tensor(row(x, T + i), row(x, T + i), gh[:, i], ALU.add).then_inc(x_done, 1)
            make_h(0, 0)
            if shared:
                rest_of_hT(0)
            dve.wait_ge(const_ready, 3)
            if shared:
                dve.wait_ge(w_loaded, 16 * 5)

            def body(b, first, last):
                df = counter()
                pieces = None if first else route(b - 1)
                for g in range(NGB):
                    gi = b * NGB + g
                    if not (last and g == NGB - 1):
                        make_h(gi + 1, b + (g + 1) // NGB)
                    if g == 0 and pieces:
                        pieces[0]()
                        dve.wait_ge(exp_in, b)
                    k = df()
                    dve.wait_ge(dd_ready, fills_before(b) + k)
                    dve.tensor_copy(logits[:, g * TPG:(g + 1) * TPG, :],
                                    dd[(k - 1) % 2][:, 0:TPG * E].rearrange("p (t e) -> p t e", e=E)).then_inc(dd_done, 1)
                    dve.wait_ge(dd_done, fills_before(b) + k + 2)
                    dve.sem_inc(logits_ready, 1)
                    if not shared:
                        if pieces:
                            for piece in (pieces[1:5], pieces[5:])[g]:
                                piece()
                            if g == NGB - 1:
                                df(2)
                        continue

                    def rest_of_a(f):
                        dve.wait_ge(a_hi, gi * FK + f + 1)
                        dve.tensor_tensor(aT[:, 1, f, :], a[:, f % 2], aT[:, 0, f, :].bitcast(F32), ALU.subtract
                                          ).then_inc(a_done, 1)
                    for f in range(FK):
                        dve.wait_ge(silu_ready, gi * FK + f + 1)
                        if f >= 2:
                            dve.wait_ge(a_done, gi * FK + f - 1)
                        dve.tensor_tensor(a[:, f % 2], upp[f % 2][:, :], silu[:, f % 2], ALU.mult).then_inc(a_ready, 1)
                        if f > 0:
                            rest_of_a(f - 1)
                        if pieces and f > 0:
                            for piece in ((pieces[1:3], pieces[3:4], pieces[4:5]), (pieces[5:6], pieces[6:7], pieces[7:8])
                                          )[g][f - 1]:
                                piece()
                    if g == NGB - 1 and pieces:
                        df(2)
                    rest_of_a(FK - 1)
                    if not (last and g == NGB - 1):
                        rest_of_hT(gi + 1)
                    for u in range(2):
                        k = df()
                        dve.wait_ge(dd_ready, fills_before(b) + k)
                        dve.wait_ge(x_done, gi * 2 + u + 1)
                        dve.tensor_tensor(gated[:, u], dd[(k - 1) % 2][:, :].rearrange("p (t d) -> p t d", d=D),
                                          modb[:, bass.ds(b, 1), GATE_B, :].to_broadcast([P, 2, D]), ALU.mult
                                          ).then_inc(dd_done, 1)
            sweep(dve, body)
            for piece in route(BATCH - 1):
                piece()
            if shared:
                block_table(nc, dve, sb, env, order, base, count, ones, choice, sent_to, step,
                            BATCH * ROUTE_STEPS[0] + 1, tabled)
                dve.sem_inc(tabled, 1)
                first_powers(dve, env)
            else:
                rest_of_set0(dve, env, layer)


def block_table(nc, dve, sb, env, order, base, count, ones, choice, sent_to, step, start, tabled):
    need, upto, begin, term = (sb(k, [P, E]) for k in ("need", "upto", "begin", "term"))
    block_id, number, first = (sb(k, [P, NB0]) for k in ("block_id", "number", "first"))
    mine = sb("mine", [P, 2 * NT, E])
    past, within = sb("past", [P, NB0, E]), sb("within", [P, NB0, E])
    n = counter(start)

    def done(k=1):
        dve.wait_ge(step, n(k))

    def over_n(ap):
        return ap.unsqueeze(1).to_broadcast([P, NB0, E])
    dve.tensor_copy(env["counts"][0:1, :], count[0:1, :]).then_inc(step, 1)
    dve.tensor_scalar(need[:, :], count[:, :], 1.0 / BLK0, (BLK0 - 1) / BLK0 - 0.5 + 0.5 / BLK0, ALU.mult, ALU.add
                      ).then_inc(step, 1)
    dve.tensor_tensor_scan(block_id[:, :], ones[:, 0:NB0], ones[:, 0:NB0], -1.0, ALU.mult, ALU.add).then_inc(step, 1)
    done(3)
    dve.sem_inc(tabled, 1)
    dve.tensor_scalar(need[:, :], need[:, :], ROUND, ROUND, ALU.add, ALU.subtract).then_inc(step, 1)
    done()
    dve.tensor_tensor_scan(upto[:, :], ones[:, 0:E], need[:, :], 0.0, ALU.mult, ALU.add).then_inc(step, 1)
    done()
    dve.tensor_tensor(begin[:, :], upto[:, :], need[:, :], ALU.subtract).then_inc(step, 1)
    by_n = block_id[:, :].unsqueeze(2).to_broadcast([P, NB0, E])
    dve.tensor_tensor(past[:], over_n(upto[:, :]), by_n, ALU.is_le).then_inc(step, 1)
    done(2)
    dve.tensor_tensor(within[:], over_n(begin[:, :]), by_n, ALU.is_le).then_inc(step, 1)
    dve.tensor_reduce(number[:, :], past[:], AXX, ALU.add).then_inc(step, 1)
    dve.scalar_tensor_tensor(out=term[:, :], in0=begin[:, :], scalar=-float(BLK0), in1=base[:, :], op0=ALU.mult,
                             op1=ALU.add).then_inc(step, 1)
    done(3)
    dve.tensor_tensor(within[:], within[:], past[:], ALU.subtract).then_inc(step, 1)
    dve.tensor_scalar(env["experts"][0:1, :], number[0:1, :], float(E - 1), None, ALU.min).then_inc(step, 1)
    dve.tensor_scalar(need[:, 0:1], upto[:, E - 1:E], -float(BLK0), float(E * STRIDE0), ALU.mult, ALU.add).then_inc(step, 1)
    done(3)
    dve.tensor_tensor(within[:], within[:], over_n(term[:, :]), ALU.mult).then_inc(step, 1)
    done()
    dve.tensor_reduce(first[:, :], within[:], AXX, ALU.add).then_inc(step, 1)
    dve.tensor_scalar(number[:, :], past[:, :, E - 1], need[:, 0:1], None, ALU.mult).then_inc(step, 1)
    done(2)
    dve.tensor_tensor(first[:, :], first[:, :], number[:, :], ALU.add).then_inc(step, 1)
    done()
    dve.scalar_tensor_tensor(out=env["first_slot"][0:1, :], in0=block_id[0:1, :], scalar=float(BLK0), in1=first[0:1, :],
                             op0=ALU.mult, op1=ALU.add).then_inc(step, 1)
    dve.scalar_tensor_tensor(out=term[:, :], in0=begin[:, :], scalar=float(BLK0), in1=base[:, :], op0=ALU.mult,
                             op1=ALU.subtract).then_inc(step, 1)
    pairs = choice[:].rearrange("p c t -> p (c t)")
    dve.tensor_tensor(mine[:], pairs.unsqueeze(2).to_broadcast([P, 2 * NT, E]),
                      order[:, :].unsqueeze(1).to_broadcast([P, 2 * NT, E]), ALU.is_equal).then_inc(step, 1)
    done(3)
    dve.tensor_tensor(mine[:], mine[:], term[:, :].unsqueeze(1).to_broadcast([P, 2 * NT, E]), ALU.mult).then_inc(step, 1)
    done()
    dve.tensor_reduce(pairs, mine[:], AXX, ALU.add).then_inc(step, 1)
    done()
    dve.tensor_tensor(env["get"][:], sent_to[:], choice[:], ALU.add).then_inc(step, 1)
    done()


def load_set(sp, A, env, layer, v, buf, loaded, wait=lambda: None):
    if layer == 0:
        e = sp.value_load(env["experts"][0:1, bass.ds(v, 1)], min_val=0, max_val=E - 1)
        parts = (("L0_ffn_gate_w", KD, FF0), ("L0_ffn_up_w", KD, FF0), ("L0_ffn_down_w", FF0 // P, D))
    else:
        e = v
        parts = (("L1_ffn_w1", KD, FF1), ("L1_ffn_w2", FF1 // P, D))
    wait()
    at = 0
    for name, k, n in parts:
        sp.dma_start(env["staging"][buf][:, at:at + k * n].rearrange("p (k n) -> p k n", n=n),
                     A[name][bass.ds(e, 1)].rearrange("o (k p) n -> p (o k) n", p=P)).then_inc(loaded, 16)
        at += k * n


def round_set0(act, env, layer):
    act.wait_ge(env["set0_loaded"], SET0_LOADED[layer])
    act.activation(env["w_part"][0][:, 0], env["staging"][0][:, :], ACT.Copy).then_inc(env["set0_hi"], 1)


def rest_of_set0(dve, env, layer):
    dve.wait_ge(env["set0_hi"], layer + 1)
    return dve.tensor_tensor(env["w_part"][0][:, 1], env["staging"][0][:, :], env["w_part"][0][:, 0].bitcast(F32),
                             ALU.subtract)


def expert_blocks(nc, A, env, layer):
    with ExitStack() as st:
        sb = lambda n, s, dt=F32: st.enter_context(nc.sbuf_tensor(f"ex{layer}_" + n, s, dt))
        sem = lambda n: st.enter_context(nc.semaphore(f"ex{layer}_" + n))
        bank = lambda n: st.enter_context(nc.psum_tensor(f"ex{layer}_" + n, [P, 512], F32))
        ident = env["ident"]
        gated = layer == 0
        FF = FF0 if gated else FF1
        FK = FF // P
        R = P if gated else RT1
        BLK = TPG * R
        NBLK = NB0 if gated else E * NB1
        SAME = 1 if gated else NB1
        NSETS = NBLK // SAME
        AHEAD = 2 if gated else 1
        BODY = 2 * SAME
        LOOPS = (NBLK - AHEAD * SAME) // BODY
        WIN = (1 + gated) * KD * FF
        WOUT = FK * D
        NA = 2 if gated else 4
        SPLIT = 0 if gated else 1
        staging, w_part = env["staging"], env["w_part"]
        rows = sb("rows", [P, 2, TPG, D])
        hT = sb("hT", [P, 2, KD, BLK], F32R)
        silu = sb("silu", [P, 2, BLK]) if gated else None
        a = sb("a", [P, NA, BLK])
        aT = sb("aT", [P, 2, FK, BLK], F32R)
        ysb = sb("ysb", [P, 2, TPG, D])
        tp = [bank(f"tp{i}") for i in range(KD)]
        gp = [bank(f"gp{i}") for i in range(NA)]
        upp = [bank(f"up{i}") for i in range(NA)] if gated else None
        dd = [bank(f"dd{i}") for i in range(2)]
        w_loaded = [sem(f"w_loaded{i}") for i in range(AHEAD)]
        w_hi, w_ready = sem("w_hi"), sem("w_ready")
        rows_loaded = [sem(f"rows_loaded{i}") for i in range(2)]
        y_stored = [sem(f"y_stored{i}") for i in range(2)]
        silu_ready = sem("silu_ready") if gated else None
        rows_used, hT_hi, hT_done, gu_ready, a_ready, a_hi, a_done, dd_ready, dd_done = (
            sem(k) for k in ("rows_used", "hT_hi", "hT_done", "gu_ready", "a_ready", "a_hi", "a_done",
                             "dd_ready", "dd_done"))
        block = st.enter_context(nc.Block())
        src = env[f"slots{layer}"].ap()
        dst = env[f"y{layer}"].ap()
        n_w = 3 if gated else 2
        FREE = 4 * SAME
        PIECES = (slice(0, WIN), slice(WIN, WIN + WOUT))
        PASSES = ((0, 0), (0, 1), (1, 0))

        def sweep(engine, body):
            with engine.Fori(0, LOOPS) as i:
                for s in range(BODY):
                    body(i * BODY + s, i, s)
            for s in range(NBLK - LOOPS * BODY):
                body(LOOPS * BODY + s, LOOPS + s // BODY, s % BODY)

        def last(i, s):
            return isinstance(i, int) and i * BODY + s == NBLK - 1

        def next_set(i, s, k=1):
            v = i * 2 + s // SAME + k
            return None if isinstance(v, int) and v >= NSETS else v

        @block.sync
        def _(sp):
            def load_weights(v, buf):
                load_set(sp, A, env, layer, v, buf, w_loaded[buf], lambda: sp.wait_ge(w_ready, v + 1))

            def slots_of(n):
                if not gated:
                    return bass.ds(n * BLK, BLK)
                return bass.ds(sp.value_load(env["first_slot"][0:1, bass.ds(n, 1)], min_val=0,
                                             max_val=E * STRIDE0 + (SPARE0 - 1) * BLK0), BLK)

            def load_rows(n, s):
                slots = slots_of(n)
                sp.wait_ge(rows_used, n + 1)
                sp.dma_start(rows[0:R, s % 2], src[slots, :].rearrange("(t p) d -> p t d", p=R)
                             ).then_inc(rows_loaded[s % 2], 16)
            sp.sem_inc(w_loaded[0], 16 * n_w)
            load_rows(0, 0)
            if AHEAD == 2:
                load_weights(1, 1)

            def body(n, i, s):
                if not last(i, s):
                    load_rows(n + 1, s + 1)
                v = next_set(i, s, AHEAD)
                if s % SAME == 0 and v is not None:
                    load_weights(v, (s // SAME) % AHEAD)
                sp.wait_ge(dd_done, 2 * n + 2 + 2)
                sp.dma_start(dst[bass.ds(n * BLK, BLK), :].rearrange("(t p) d -> p t d", p=R), ysb[0:R, s % 2]
                             ).then_inc(y_stored[s % 2], 16)
            sweep(sp, body)
            sp.wait_ge(y_stored[0], 16 * (-(-NBLK // 2)) + 16)
            sp.wait_ge(y_stored[1], 16 * (NBLK // 2) + 16)

        @block.gpsimd
        def _(pool):
            pool.sem_inc(w_ready, AHEAD + (not gated))

            def split(v, par):
                for q, c in enumerate(PIECES):
                    pool.wait_ge(w_hi, 2 * v + q + 1)
                    i = pool.tensor_tensor(w_part[par][:, 1, c], staging[par % AHEAD][:, c],
                                           w_part[par][:, 0, c].bitcast(F32), ALU.subtract)
                i.then_inc(w_ready, 1)

            def body(n, i, s):
                v = next_set(i, s)
                if s % SAME == SPLIT and v is not None:
                    split(v, (s // SAME + 1) % 2)
            sweep(pool, body)
            if not gated:
                for q in range(2):
                    pool.wait_ge(y_stored[q], 16 * ((NBLK - NB1 + 1 - q) // 2) + 16)
                fetch(pool, env, 0)

        @block.tensor
        def _(pe):
            pe.sem_inc(dd_ready, FREE)
            pe.sem_inc(rows_used, 2)

            def w_in(par, part, m, k, f):
                c = (m * KD + k) * FF + f * P
                return w_part[par][:, part, c:c + P]

            def w_out(par, part, k):
                return w_part[par][:, part, WIN + k * D:WIN + (k + 1) * D]

            def transposes(n, i, s):
                pe.wait_ge(hT_done, n * KD + KD)
                pe.wait_ge(rows_loaded[s % 2], 16 * (i * (BODY // 2) + s // 2 + 1))
                for t in range(TPG):
                    for j in range(KD):
                        m = pe.transpose(tp[j][:, t * R:(t + 1) * R], rows[0:R, s % 2, t, j * P:(j + 1) * P],
                                         ident[0:R, 0:R])
                m.then_inc(rows_used, 1)
            transposes(0, 0, 0)

            def body(n, i, s):
                par = s // SAME % 2
                if s % SAME == 0:
                    pe.wait_ge(w_ready, i * 2 + s // SAME + 1 + AHEAD)
                pe.wait_ge(hT_done, n * KD + 2 * KD)
                for f in range(FK):
                    pe.wait_ge(a_ready, n * FK + f + 1)
                    for m in range(1 + gated):
                        for k in range(KD):
                            for q, (pw, ph) in enumerate(PASSES):
                                mm = pe.matmul((gp, upp)[m][f % NA][:, 0:BLK], w_in(par, pw, m, k, f), hT[:, ph, k, :],
                                               start=k == 0 and q == 0, stop=k == KD - 1 and q == 2)
                    mm.then_inc(gu_ready, 1)
                if not last(i, s):
                    transposes(n + 1, *((i, s + 1) if s + 1 < BODY else (i + 1, 0)))
                for u in range(2):
                    pe.wait_ge(dd_done, 2 * n + u + 1)
                    for t in range(2):
                        for k in range(FK):
                            c = (2 * u + t) * R
                            if c == 0:
                                pe.wait_ge(a_done, n * FK + k + 1)
                            for q, (pa, pw) in enumerate(PASSES):
                                mm = pe.matmul(dd[u][0:R, t * D:(t + 1) * D], aT[:, pa, k, c:c + R], w_out(par, pw, k),
                                               start=k == 0 and q == 0, stop=k == FK - 1 and q == 2)
                    if u == 0:
                        mm.then_inc(dd_ready, 1)
                mm.then_inc(dd_ready, 1)
            sweep(pe, body)

        @block.scalar
        def _(act):
            if not gated:
                act.sem_inc(a_ready, NA)

            def copy_hT(n):
                act.wait_ge(rows_used, n + 1 + 2)
                for j in range(KD):
                    act.activation(hT[:, 0, j, :], tp[j][:, 0:BLK], ACT.Copy).then_inc(hT_hi, 1)

            def round_weights(q, v, buf, par, v_buf):
                act.wait_ge(w_loaded[buf], 16 * n_w * (v_buf + 1))
                act.wait_ge(dd_ready, 2 * SAME * (v - 1) + FREE)
                act.activation(w_part[par][:, 0, PIECES[q]], staging[buf][:, PIECES[q]], ACT.Copy).then_inc(w_hi, 1)
            act.sem_inc(w_hi, 2)
            if gated:
                round_set0(act, env, layer)
            copy_hT(0)

            def body(n, i, s):
                def round_a(f):
                    act.wait_ge(a_ready, n * FK + f + 1 + NA)
                    act.activation(aT[:, 0, f, :], a[:, f % NA], ACT.Copy).then_inc(a_hi, 1)
                v = next_set(i, s)
                for f in range(FK):
                    act.wait_ge(gu_ready, n * FK + f + 1)
                    if gated:
                        act.activation(silu[:, f % 2], gp[f % NA][:, 0:BLK], ACT.Silu).then_inc(silu_ready, 1)
                    else:
                        if f >= NA:
                            act.wait_ge(a_done, n * FK + f - NA + 1)
                        act.activation(a[:, f % NA], gp[f % NA][:, 0:BLK], ACT.Silu).then_inc(a_ready, 1)
                    if f > 0:
                        round_a(f - 1)
                    if s % SAME == SPLIT and f < 2 and v is not None:
                        t = s // SAME + 1
                        round_weights(f, v, t % AHEAD, t % 2, v if AHEAD == 1 else i + t // 2)
                round_a(FK - 1)
                if not last(i, s):
                    copy_hT(n + 1)
            sweep(act, body)

        @block.vector
        def _(dve):
            if gated:
                dve.sem_inc(a_ready, NA)
            else:
                dve.sem_inc(env["part_used"], 2)
            dve.sem_inc(hT_done, KD)
            dve.sem_inc(dd_done, 2)
            for i in range(2):
                dve.sem_inc(y_stored[i], 16)

            def rest_of_hT(n):
                for j in range(KD):
                    dve.wait_ge(hT_hi, n * KD + j + 1)
                    dve.tensor_tensor(hT[:, 1, j, :], tp[j][:, 0:BLK], hT[:, 0, j, :].bitcast(F32), ALU.subtract
                                      ).then_inc(hT_done, 1)
            if gated:
                rest_of_set0(dve, env, layer).then_inc(w_ready, 1)
            rest_of_hT(0)
            if gated:
                dve.tensor_copy(env["rot"][:, :, :, 0:CHUNK], env["rot0"][:]).then_inc(env["tab"], 1)
            added = iter(range(NT))

            def take(k):
                return [next(added) for _ in range(k)]

            def body(n, i, s):
                early = i * BODY + s - (NBLK - NB1) if not gated and isinstance(i, int) else -1

                def rest_of_a(f):
                    dve.wait_ge(a_hi, n * FK + f + 1)
                    dve.tensor_tensor(aT[:, 1, f, :], a[:, f % NA], aT[:, 0, f, :].bitcast(F32), ALU.subtract
                                      ).then_inc(a_done, 1)
                for f in range(FK):
                    if gated:
                        dve.wait_ge(silu_ready, n * FK + f + 1)
                        if f >= NA:
                            dve.wait_ge(a_done, n * FK + f - NA + 1)
                        dve.tensor_tensor(a[:, f % NA], upp[f % NA][:, 0:BLK], silu[:, f % 2], ALU.mult).then_inc(a_ready, 1)
                        if f > 0:
                            rest_of_a(f - 1)
                    else:
                        rest_of_a(f)
                        if early > 0 and f in (2, 5):
                            add_results(dve, env, take(2), 0)
                if gated:
                    rest_of_a(FK - 1)
                if not last(i, s):
                    rest_of_hT(n + 1)
                if gated and not (isinstance(n, int) and n >= CHUNKS - 1):
                    table_chunk(dve, env, n * CHUNK, n * CHUNK_STEPS + POWER_STEPS + 1)
                if early >= 0:
                    add_results(dve, env, take(8), 0)
                dve.wait_ge(y_stored[s % 2], 16 * (i * (BODY // 2) + s // 2) + 16)
                for u in range(2):
                    dve.wait_ge(dd_ready, 2 * n + u + 1 + FREE)
                    dve.tensor_copy(ysb[0:R, s % 2, 2 * u:2 * u + 2, :],
                                    dd[u][0:R, :].rearrange("p (t d) -> p t d", d=D)).then_inc(dd_done, 1)
            sweep(dve, body)


def fetch(pool, env, c):
    y = env["y1"].ap()[0:(E - 1 + c) * SLOTS1, :]
    for t in range(NT):
        k = c * NT + t
        if k >= RING:
            pool.wait_ge(env["part_ready"], k - RING + 1)
        pool.indirect_dma_start(env["ring"][:, k % RING, :], None, y,
                                bass.IndirectOffsetOnAxis(ap=env["get"][:, c, t:t + 1], axis=0)
                                ).then_inc(env["fetched"][k % RING], 16)


def add_results(dve, env, tiles, c):
    x, modb, weight, ring, part, fetched, part_ready, part_used = (
        env[k] for k in ("x", "modb", "weight", "ring", "part", "fetched", "part_ready", "part_used"))
    for t in tiles[::2]:
        for i in (t, t + 1):
            k = c * NT + i
            dve.wait_ge(fetched[k % RING], 16 * (k // RING + 1))
            dve.wait_ge(part_used, k + 1)
            dve.scalar_tensor_tensor(out=part[:, k % 2], in0=ring[:, k % RING], scalar=weight[:, c, i:i + 1],
                                     in1=modb[:, i // TPB, GATE_B, :], op0=ALU.mult, op1=ALU.mult).then_inc(part_ready, 1)
        for i in (t, t + 1):
            k = c * NT + i
            dve.wait_ge(part_ready, k + 1)
            dve.tensor_tensor(x[:, i], x[:, i], part[:, k % 2], ALU.add).then_inc(part_used, 1)


def combine(nc, A, env):
    with ExitStack() as st:
        sb = lambda n, s, dt=F32: st.enter_context(nc.sbuf_tensor("cb0_" + n, s, dt))
        sem = lambda n: st.enter_context(nc.semaphore("cb0_" + n))
        x, modb, weight, get = (env[k] for k in ("x", "modb", "weight", "get"))
        NBUF = 4
        y = sb("y", [P, NBUF, 2, D])
        s1 = sb("s1", [P, NBUF, D])
        fetched = [sem(f"fetched{i}") for i in range(NBUF)]
        scratch = sb("scratch", [P, 2, SEQ])
        y_used, step, coef_step = sem("y_used"), sem("step"), sem("coef_step")
        n = counter()
        block = st.enter_context(nc.Block())

        @block.gpsimd
        def _(pool):
            for t in range(NT):
                if t >= NBUF:
                    pool.wait_ge(y_used, t - NBUF + 1)
                for c in range(2):
                    pool.indirect_dma_start(y[:, t % NBUF, c, :], None, env["y0"].ap(),
                                            bass.IndirectOffsetOnAxis(ap=get[:, c, t:t + 1], axis=0)
                                            ).then_inc(fetched[t % NBUF], 16)

        @block.vector
        def _(dve):
            for t in range(0, NT, 2):
                pair = [(i, i % NBUF) for i in (t, t + 1)]
                for i, q in pair:
                    dve.wait_ge(fetched[q], 32 * (i // NBUF + 1))
                    dve.tensor_scalar(s1[:, q], y[:, q, 0], weight[:, 0, i:i + 1], None, ALU.mult).then_inc(step, 1)
                for i, q in pair:
                    dve.wait_ge(step, 3 * t + i - t + 1)
                    dve.scalar_tensor_tensor(out=s1[:, q], in0=y[:, q, 1], scalar=weight[:, 1, i:i + 1], in1=s1[:, q],
                                             op0=ALU.mult, op1=ALU.add).then_inc(y_used, 1)
                for i, q in pair:
                    dve.wait_ge(y_used, i + 1)
                    dve.tensor_tensor(s1[:, q], s1[:, q], modb[:, i // TPB, GATE_B, :], ALU.mult).then_inc(step, 1)
                for i, q in pair:
                    dve.wait_ge(step, 3 * t + i - t + 3)
                    dve.tensor_tensor(x[:, i], x[:, i], s1[:, q], ALU.add).then_inc(step, 1)
                for i, q in pair:
                    dve.wait_ge(step, 3 * t + i - t + 5)
                    dve.bn_stats(env["stats"][:, i], x[:, i]).then_inc(env["stats_done"], 1)
                if t in (4, 12):
                    coefficients(dve, env, scratch, t // 8, coef_step, n)


def last_results(nc, env, out):
    with ExitStack() as st:
        stored = st.enter_context(nc.semaphore("stored"))
        block = st.enter_context(nc.Block())

        @block.gpsimd
        def _(pool):
            fetch(pool, env, 1)

        @block.vector
        def _(dve):
            add_results(dve, env, range(NT), 1)

        @block.sync
        def _(sp):
            tiles = out.rearrange("b (t p) d -> p (b t) d", p=P)
            for t in range(0, NT, 4):
                sp.wait_ge(env["part_used"], NT + t + 4 + 2)
                sp.dma_start(tiles[:, t:t + 4, :], env["x"][:, t:t + 4, :]).then_inc(stored, 16)
            sp.wait_ge(stored, 16 * NT // 4)
            sp.wait_ge(env["zeroed"], 16 * env["zero_dmas"])


_PLAIN = ["L0_attn_x", "L0_wmod", "L1_wmod", "L0_ffn_gate_w", "L0_ffn_up_w", "L0_ffn_down_w", "L0_ffn_routing_bias",
          "L1_ffn_w1", "L1_ffn_w2"]
_TRANSPOSED = {"ct0": "L0_c", "ct1": "L1_c", "wqT": "L0_attn_wq", "wkT": "L0_attn_wk", "wvT": "L0_attn_wv",
               "woT": "L0_attn_wo", "rfT": "L0_attn_rf", "sgT": "L0_ffn_shared_gate", "suT": "L0_ffn_shared_up",
               "sdT": "L0_ffn_shared_down", "rw0T": "L0_ffn_router_w", "rw1T": "L1_ffn_router_w"}
_COLUMNS = ["L1_attn_phazor_real", "L1_attn_phazor_imag", "L1_attn_phazor_init_real", "L1_attn_phazor_init_imag",
            "L1_attn_last_conv_real", "L1_attn_last_conv_imag"]


def layout(inputs):
    a = {k: np.ascontiguousarray(inputs[k]) for k in _PLAIN}
    a |= {k: np.ascontiguousarray(np.asarray(inputs[v]).T) for k, v in _TRANSPOSED.items()}
    a["phasor"] = np.ascontiguousarray(
        np.stack([np.asarray(inputs[k]) for k in _COLUMNS]).reshape(6, KD, P).transpose(2, 0, 1))
    return a


def kernel(**inputs):
    import concourse.bacc as _bacc
    from concourse.bass_utils import run_bass_kernel_spmd as _run

    nc = _bacc.Bacc("TRN2", target_bir_lowering=False, num_devices=1)
    arrays = layout(inputs)
    A = {k: nc.dram_tensor(k, v.shape, mybir.dt.from_np(v.dtype), kind="ExternalInput").ap() for k, v in arrays.items()}
    out = nc.dram_tensor("out", (BATCH, SEQ, D), F32, kind="ExternalOutput").ap()
    build_program(nc, A, out)
    return _run(nc, [arrays], core_ids=[0]).results[0]["out"]
```
